# Optimizing a Trainium2 kernel written in Bass

```python
import numpy as np
import jax
import jax.numpy as jnp

def _softmax(x, axis=-1):
    return jax.nn.softmax(x, axis=axis)

def _gelu(x):
    return jax.nn.gelu(x, approximate=True)

def _silu(x):
    return jax.nn.silu(x)

def _sigmoid(x):
    return jax.nn.sigmoid(x)

def _layernorm(x, axis=-1, eps=1e-05):
    m = jnp.mean(x, axis=axis, keepdims=True)
    v = jnp.var(x, axis=axis, keepdims=True)
    return (x - m) / jnp.sqrt(v + eps)

def _scatter_add(tgt, idx, src, axis=0):
    return tgt.at[idx].add(src)

def _segment_sum(src, seg, n):
    return jax.ops.segment_sum(src, seg, n)
kernel_name = 'mk_decoder_postln_d1_seqx_r8_ad8b84'

def setup_inputs(seed: int=0):
    np.random.seed(seed)
    _w = jnp.asarray

    def _rec_inputs():
        import jax
        import jax.numpy as jnp
        _rk = jax.random.key(seed)
        x = -0.000125 + 0.9999 * jax.random.normal(jax.random.fold_in(_rk, 1), (4, 256, 256), jnp.float32)
        _lenS = 256 - jax.random.randint(jax.random.fold_in(_rk, 7), (4,), 0, max(1, 256 // 4) + 1, jnp.int32)
        _lenS2 = 256 - jax.random.randint(jax.random.fold_in(_rk, 8), (4,), 0, max(1, 256 // 4) + 1, jnp.int32)
        itok_BxS_13_99985 = jax.random.randint(jax.random.fold_in(_rk, 11), (4, 256), 13, 99986, jnp.int32)
        _ctx_2048P = jax.random.normal(jax.random.fold_in(_rk, 12), (4, 16, 256), jnp.float32)
        _ctx_2048c = jax.random.dirichlet(jax.random.fold_in(_rk, 512), 0.3 * jnp.ones((16,), jnp.float32), (4, 256))
        _ctx_2048t = jnp.einsum('bsk,bkd->bsd', _ctx_2048c, _ctx_2048P)
        _ctx_2048t = _ctx_2048t * jax.lax.rsqrt(jnp.mean(jnp.square(_ctx_2048t)) + 1e-12) * 0.953939
        ctx_2048 = 6.82029e-06 + 0.0200006 * (_ctx_2048t + 0.3 * jax.random.normal(jax.random.fold_in(_rk, 612), (4, 256, 256), jnp.float32))
        return (x, itok_BxS_13_99985, ctx_2048)
    x, itok_BxS_13_99985, ctx_2048 = _rec_inputs()

    def _L0_attn_setup():
        import jax, jax.numpy as jnp
        import numpy as np
        EPS = 1e-06
        H, NOPE, ROPE, VD = (16, 128, 64, 128)
        QHD = NOPE + ROPE
        SCALE = QHD ** (-0.5)
        THETA = 10000.0

        def rmsnorm(x, w):
            x32 = x.astype(jnp.float32)
            var = jnp.mean(x32 * x32, axis=-1, keepdims=True)
            return (w * (x32 * jax.lax.rsqrt(var + EPS))).astype(x.dtype)

        def rope_cos_sin(seq_len):
            inv_freq = 1.0 / THETA ** (jnp.arange(0, ROPE, 2, dtype=jnp.float32) / ROPE)
            t = jnp.arange(seq_len, dtype=jnp.float32)
            freqs = jnp.outer(t, inv_freq)
            emb = jnp.concatenate([freqs, freqs], -1)
            return (jnp.cos(emb), jnp.sin(emb))

        def rotate_half(x):
            x1, x2 = (x[..., :x.shape[-1] // 2], x[..., x.shape[-1] // 2:])
            return jnp.concatenate([-x2, x1], axis=-1)
        key = jax.random.key(seed)
        ks = jax.random.split(key, 6)
        B, S, D = (2, 256, 256)
        return {'hidden_states': jax.random.normal(ks[0], (B, S, D), jnp.float32), 'q_a_w': jax.random.normal(ks[1], (192, D), jnp.float32) * 0.02, 'q_a_ln_w': jnp.ones((192,), jnp.float32), 'q_b_w': jax.random.normal(ks[2], (H * QHD, 192), jnp.float32) * 0.02, 'kv_a_w': jax.random.normal(ks[3], (64 + ROPE, D), jnp.float32) * 0.02, 'kv_a_ln_w': jnp.ones((64,), jnp.float32), 'kv_b_w': jax.random.normal(ks[4], (H * (NOPE + VD), 64), jnp.float32) * 0.02, 'o_w': jax.random.normal(ks[5], (D, H * VD), jnp.float32) * 0.02}
    _L0_attn_all = _L0_attn_setup()
    _L0_attn_in = {k: v for k, v in _L0_attn_all.items() if k in ('q_a_w', 'q_a_ln_w', 'q_b_w', 'kv_a_w', 'kv_a_ln_w', 'kv_b_w', 'o_w')}
    del _L0_attn_all

    def _L0_xattn_setup():
        import jax, jax.numpy as jnp
        import numpy as np
        B, S, D = (4, 512, 256)
        E = 4
        F = 1024 // E
        VOCAB = 12500
        key = jax.random.key(seed)
        k1, k2, k3, k4, k5 = jax.random.split(key, 5)
        hidden_states = jax.random.normal(k1, (B, S, D), dtype=jnp.float32)
        token_ids = jax.random.randint(k2, (B, S), 0, VOCAB, dtype=jnp.int64)
        Wg = jax.random.normal(k3, (E, F, D), dtype=jnp.float32) * 0.02
        Wu = jax.random.normal(k4, (E, F, D), dtype=jnp.float32) * 0.02
        Wd = jax.random.normal(k5, (E, D, F), dtype=jnp.float32) * 0.02
        return {'hidden_states': hidden_states, 'token_ids': token_ids, 'Wg': Wg, 'Wu': Wu, 'Wd': Wd}
    _L0_xattn_all = _L0_xattn_setup()
    _L0_xattn_in = {k: v for k, v in _L0_xattn_all.items() if k in ()}
    del _L0_xattn_all

    def _L0_ffn_setup():
        import jax, jax.numpy as jnp
        import numpy as np
        H = 256
        E = 16
        K = 4
        I = 176
        SH_I = 2 * I
        B, S = (1, 128)
        key = jax.random.key(seed)
        ks = jax.random.split(key, 9)
        sc_h = 1.0 / np.sqrt(H)
        sc_i = 1.0 / np.sqrt(I)
        return {'hidden_states': jax.random.normal(ks[0], (B, S, H), dtype=jnp.float32), 'w_gate': jax.random.normal(ks[1], (E, H), dtype=jnp.float32) * sc_h, 'wg': jax.random.normal(ks[2], (E, H, I), dtype=jnp.float32) * sc_h, 'wu': jax.random.normal(ks[3], (E, H, I), dtype=jnp.float32) * sc_h, 'wd': jax.random.normal(ks[4], (E, I, H), dtype=jnp.float32) * sc_i, 'sg': jax.random.normal(ks[5], (H, SH_I), dtype=jnp.float32) * sc_h, 'su': jax.random.normal(ks[6], (H, SH_I), dtype=jnp.float32) * sc_h, 'sd': jax.random.normal(ks[7], (SH_I, H), dtype=jnp.float32) * (1.0 / np.sqrt(SH_I))}
    _L0_ffn_all = _L0_ffn_setup()
    _L0_ffn_in = {k: v for k, v in _L0_ffn_all.items() if k in ('w_gate', 'wg', 'wu', 'wd', 'sg', 'su', 'sd')}
    del _L0_ffn_all
    return {'x': x, 'itok_BxS_13_99985': itok_BxS_13_99985, 'ctx_2048': ctx_2048, 'L0_attn_q_a_w': _L0_attn_in['q_a_w'], 'L0_attn_q_a_ln_w': _L0_attn_in['q_a_ln_w'], 'L0_attn_q_b_w': _L0_attn_in['q_b_w'], 'L0_attn_kv_a_w': _L0_attn_in['kv_a_w'], 'L0_attn_kv_a_ln_w': _L0_attn_in['kv_a_ln_w'], 'L0_attn_kv_b_w': _L0_attn_in['kv_b_w'], 'L0_attn_o_w': _L0_attn_in['o_w'], 'L0_ffn_w_gate': _L0_ffn_in['w_gate'], 'L0_ffn_wg': _L0_ffn_in['wg'], 'L0_ffn_wu': _L0_ffn_in['wu'], 'L0_ffn_wd': _L0_ffn_in['wd'], 'L0_ffn_sg': _L0_ffn_in['sg'], 'L0_ffn_su': _L0_ffn_in['su'], 'L0_ffn_sd': _L0_ffn_in['sd']}

def reference(x, itok_BxS_13_99985, ctx_2048, L0_attn_q_a_w, L0_attn_q_a_ln_w, L0_attn_q_b_w, L0_attn_kv_a_w, L0_attn_kv_a_ln_w, L0_attn_kv_b_w, L0_attn_o_w, L0_ffn_w_gate, L0_ffn_wg, L0_ffn_wu, L0_ffn_wd, L0_ffn_sg, L0_ffn_su, L0_ffn_sd):
    import jax
    import jax.numpy as jnp

    def _L0_attn_ref(hidden_states, q_a_w, q_a_ln_w, q_b_w, kv_a_w, kv_a_ln_w, kv_b_w, o_w):
        import jax, jax.numpy as jnp
        import numpy as np
        EPS = 1e-06
        H, NOPE, ROPE, VD = (16, 128, 64, 128)
        QHD = NOPE + ROPE
        SCALE = QHD ** (-0.5)
        THETA = 10000.0

        def rmsnorm(x, w):
            x32 = x.astype(jnp.float32)
            var = jnp.mean(x32 * x32, axis=-1, keepdims=True)
            return (w * (x32 * jax.lax.rsqrt(var + EPS))).astype(x.dtype)

        def rope_cos_sin(seq_len):
            inv_freq = 1.0 / THETA ** (jnp.arange(0, ROPE, 2, dtype=jnp.float32) / ROPE)
            t = jnp.arange(seq_len, dtype=jnp.float32)
            freqs = jnp.outer(t, inv_freq)
            emb = jnp.concatenate([freqs, freqs], -1)
            return (jnp.cos(emb), jnp.sin(emb))

        def rotate_half(x):
            x1, x2 = (x[..., :x.shape[-1] // 2], x[..., x.shape[-1] // 2:])
            return jnp.concatenate([-x2, x1], axis=-1)
        B, S, D = hidden_states.shape
        q_a = hidden_states @ q_a_w.T
        q = rmsnorm(q_a, q_a_ln_w) @ q_b_w.T
        q = q.reshape(B, S, H, QHD).transpose(0, 2, 1, 3)
        q_nope, q_pe = (q[..., :NOPE], q[..., NOPE:])
        ckv_full = hidden_states @ kv_a_w.T
        ckv, k_pe_raw = (ckv_full[..., :64], ckv_full[..., 64:])
        kv = rmsnorm(ckv, kv_a_ln_w) @ kv_b_w.T
        kv = kv.reshape(B, S, H, NOPE + VD).transpose(0, 2, 1, 3)
        k_nope, v = (kv[..., :NOPE], kv[..., NOPE:])
        k_pe = k_pe_raw.reshape(B, 1, S, ROPE)
        cos, sin = rope_cos_sin(S)
        cos, sin = (cos[None, None], sin[None, None])
        q_pe = q_pe * cos + rotate_half(q_pe) * sin
        k_pe = k_pe * cos + rotate_half(k_pe) * sin
        query = jnp.concatenate([q_nope, q_pe], -1)
        key_s = jnp.concatenate([k_nope, jnp.broadcast_to(k_pe, (B, H, S, ROPE))], -1)
        scores = jnp.einsum('bhqd,bhkd->bhqk', query, key_s) * SCALE
        causal = jnp.tril(jnp.ones((S, S), bool))
        scores = jnp.where(causal[None, None], scores, -jnp.inf)
        probs = jax.nn.softmax(scores.astype(jnp.float32), axis=-1).astype(query.dtype)
        attn = jnp.einsum('bhqk,bhkd->bhqd', probs, v)
        attn = attn.transpose(0, 2, 1, 3).reshape(B, S, H * VD)
        return attn @ o_w.T

    def _L0_xattn_ref(hidden_states, token_ids, Wg, Wu, Wd):
        import jax, jax.numpy as jnp
        import numpy as np
        B, S, D = (4, 512, 256)
        E = 4
        F = 1024 // E
        VOCAB = 12500
        tokens_per_expert = VOCAB // E
        tid = jnp.clip(token_ids, 0, VOCAB - 1)
        expert_ids = jnp.minimum(tid // tokens_per_expert, E - 1)
        out = jnp.zeros_like(hidden_states)
        for e in range(E):
            g = jax.nn.silu(jnp.einsum('bsd,fd->bsf', hidden_states, Wg[e]))
            u = jnp.einsum('bsd,fd->bsf', hidden_states, Wu[e])
            y = jnp.einsum('bsf,df->bsd', g * u, Wd[e])
            out = jnp.where((expert_ids == e)[..., None], y, out)
        return out

    def _L0_ffn_ref(hidden_states, w_gate, wg, wu, wd, sg, su, sd):
        import jax, jax.numpy as jnp
        import numpy as np
        H = 256
        E = 16
        K = 4
        I = 176
        SH_I = 2 * I
        B, S = (1, 128)
        b, s, h = hidden_states.shape
        x = hidden_states.reshape(-1, h)
        T = x.shape[0]
        logits = x @ w_gate.T
        probs = jax.nn.softmax(logits.astype(jnp.float32), axis=-1)
        top_w, top_i = jax.lax.top_k(probs, K)
        routing_weight = jnp.zeros((T, E), dtype=probs.dtype)
        routing_weight = routing_weight.at[jnp.arange(T)[:, None], top_i].add(top_w)
        g = jnp.einsum('th,ehi->tei', x, wg)
        u = jnp.einsum('th,ehi->tei', x, wu)
        act = jax.nn.silu(g) * u
        routed = jnp.einsum('te,tei,eih->th', routing_weight, act, wd)
        shared = jax.nn.silu(x @ sg) * (x @ su) @ sd
        out = (routed + shared).astype(hidden_states.dtype)
        return out.reshape(b, s, h)
    x = _layernorm(x + _L0_attn_ref(x, L0_attn_q_a_w, L0_attn_q_a_ln_w, L0_attn_q_b_w, L0_attn_kv_a_w, L0_attn_kv_a_ln_w, L0_attn_kv_b_w, L0_attn_o_w), axis=-1)
    x = _layernorm(x + _L0_xattn_ref(x, itok_BxS_13_99985, ctx_2048, ctx_2048, ctx_2048), axis=-1)
    x = _layernorm(x + _L0_ffn_ref(x, L0_ffn_w_gate, L0_ffn_wg, L0_ffn_wu, L0_ffn_wd, L0_ffn_sg, L0_ffn_su, L0_ffn_sd), axis=-1)
    return x

_drawn_inputs = setup_inputs


def setup_inputs(seed=0):
    import zlib

    import numpy as np

    out = dict(_drawn_inputs(seed))
    spreads = {'L0_attn_q_a_ln_w': (1.0, 0.6), 'L0_attn_kv_a_ln_w': (1.0, 0.6)}
    factors = {'L0_attn_q_a_w': 8.0, 'L0_attn_q_b_w': 8.0}
    for name, (base, spread) in spreads.items():
        noise = np.random.default_rng([zlib.crc32(name.encode()), seed]).standard_normal(out[name].shape)
        drawn = base * np.exp(spread * noise) if base else spread * noise
        out[name] = jnp.asarray(drawn.astype(out[name].dtype))
    for name, factor in factors.items():
        out[name] = (out[name] * factor).astype(out[name].dtype)
    return out
```

```python
from contextlib import ExitStack

import concourse.bass as bass
from concourse import mybir

ALU = mybir.AluOpType
ACT = mybir.ActivationFunctionType
AX = mybir.AxisListType.X
F32 = mybir.dt.float32
F16 = mybir.dt.float16
BF16 = mybir.dt.bfloat16
I32 = mybir.dt.int32
U32 = mybir.dt.uint32

P = 128
BATCH, SEQ, D = 4, 256, 256
TOKENS = BATCH * SEQ
TILES = TOKENS // P
TPB = SEQ // P
DC = D // P
HEADS, NOPE, ROPE, VD = 16, 128, 64, 128
QHD = NOPE + ROPE
SCALE = float(QHD) ** -0.5
QR, KR = 192, 64
QC = QR // 2
HD = KR + ROPE
QG = 4
GROUPS = HEADS // QG
CTX = 4
CTX_STEP = 12500 // CTX
EXPERTS, TOPK, INNER = 16, 4, 176
HALF = INNER // 2
SHARED = 2
GU = 2 * INNER
RMS_EPS, LN_EPS = 1e-6, 1e-5
MASKED = -1e30
SLOT_TILES = (TOKENS * TOPK + EXPERTS * (P - 1)) // P


def decoder_layer(nc, xT, x, ids, wqkvT, qlnw, kvlnw, qnope, qpeT, kvb, woT, cosT, sinT, ctxT,
                  wgateT, wgu, wd, out):
    x2_dram = nc.dram_tensor("x2_dram", (TOKENS, D), F32, kind="Internal").ap()
    table = nc.dram_tensor("table", (EXPERTS * TOKENS, 1), U32, kind="Internal").ap()
    y_dram = nc.dram_tensor("y_dram", (SLOT_TILES * P, D), F32, kind="Internal").ap()

    with ExitStack() as ctx:
        def sb(name, shape, dt=F32):
            return ctx.enter_context(nc.sbuf_tensor(name, shape, dt))

        def sem(name):
            return ctx.enter_context(nc.semaphore(name))

        bank = [ctx.enter_context(nc.psum_tensor(f"bank{i}", [P, 512], F32)) for i in range(8)]

        ident = sb("ident", [P, P])
        ident16 = sb("ident16", [P, P], BF16)
        causal = sb("causal", [P, P], BF16)
        earlier = sb("earlier", [P, P], BF16)
        ones = sb("ones", [P, P], BF16)
        iota16 = sb("iota16", [P, EXPERTS])
        region = sb("region", [P, EXPERTS])
        before = sb("before", [P, EXPERTS, EXPERTS])
        tile_starts = sb("tile_starts", [P, TILES])
        slot_iota = sb("slot_iota", [P, SLOT_TILES])
        token_id = sb("token_id", [P, TILES], U32)
        cos = sb("cos", [P, TPB, ROPE])
        sin = sb("sin", [P, TPB, ROPE])
        w_qkv = sb("w_qkv", [P, DC, QR + KR + ROPE])
        w_qn = sb("w_qn", [P, QR])
        w_kn = sb("w_kn", [P, KR])
        w_q = sb("w_q", [QC, 2, HEADS, HD])
        w_out = sb("w_out", [P, HEADS // 2, D])
        w_ctx = sb("w_ctx", [P, DC, CTX * D])
        w_gate = sb("w_gate", [P, DC, EXPERTS])
        w_gu = sb("w_gu", [P, DC, EXPERTS + SHARED, GU])
        area = sb("area", [P, (EXPERTS + SHARED) * 2 * D])
        w_down = area[0:HALF, :].rearrange("p (e c d) -> p e c d", e=EXPERTS + SHARED, c=2)
        raw_q = area[:, 0:HEADS * QR].rearrange("p (h r) -> p h r", h=HEADS)
        raw_kv = area[:, HEADS * QR:HEADS * (QR + 2 * KR)].rearrange("p (h t r) -> p h t r", h=HEADS, t=2)
        raw_o = area[:, HEADS * (QR + 2 * KR):HEADS * (QR + 2 * KR + D)].rearrange("p (h d) -> p h d", h=HEADS)
        x_t = sb("x_t", [P, DC, SEQ])
        rows = sb("rows", [P, TILES, D])
        act_junk = sb("act_junk", [P, TPB, QR + KR])
        ssq = sb("ssq", [P, 2 * TPB])
        ssq_eps = sb("ssq_eps", [P, 2 * TPB])
        minus_half = sb("minus_half", [P, 2 * TPB])
        rms = sb("rms", [P, 2 * TPB])
        qn = sb("qn", [P, TPB, QR])
        kv_row = sb("kv_row", [P, TPB, HD])
        k_cos = sb("k_cos", [P, TPB, ROPE])
        k_sin = sb("k_sin", [P, TPB, ROPE])
        v_hi = sb("v_hi", [P, TPB, KR + 2], F16)
        v_lo = sb("v_lo", [P, TPB, KR + 2], F16)
        qn_t = sb("qn_t", [QC, 2, SEQ])
        k_t = sb("k_t", [P, SEQ])
        q_row_mem = sb("q_row_mem", [P, TPB * HEADS * HD])
        q_t_mem = sb("q_t_mem", [P, HEADS * SEQ])
        o_row_mem = sb("o_row_mem", [P, TPB * HEADS * KR])
        probs_mem = sb("probs_mem", [P, 3 * 3 * P])

        def carve(mem, parts):
            at, views = 0, []
            for width, pattern, sizes in parts:
                views.append(mem[:, at:at + width].rearrange(pattern, **sizes))
                at += width
            return views

        q_row, = carve(q_row_mem, [(TPB * HEADS * HD, "p (j h d) -> p j h d", dict(j=TPB, h=HEADS))])
        q_t, = carve(q_t_mem, [(HEADS * SEQ, "p (h t) -> p h t", dict(h=HEADS))])
        o_row, = carve(o_row_mem, [(TPB * HEADS * KR, "p (j o) -> p j o", dict(j=TPB))])
        probs, = carve(probs_mem, [(9 * P, "p (r k) -> p r k", dict(r=3))])
        o_t, = carve(probs_mem, [(HEADS // 2 * P, "p (c t) -> p c t", dict(c=HEADS // 2))])
        pair = "p (r d) -> p r d", dict(r=2)
        picked, gated, a_row, s_act_t = carve(o_row_mem, [(2 * D, *pair)] * 3 + [
            (4 * P, "p (s c t) -> p s c t", dict(s=2, c=2))])
        s_act_t = s_act_t[0:HALF]
        XR, YR = 4, 3
        back, fin, s_gate, s_act, begun = carve(q_row_mem, [
            (2 * TOPK * D, "p (r k d) -> p r k d", dict(r=2, k=TOPK)), (2 * D, *pair),
            (2 * INNER, *pair), (2 * INNER, *pair),
            (SLOT_TILES * EXPERTS, "p (s e) -> p s e", dict(s=SLOT_TILES))])
        onehots, = carve(q_row_mem, [(TILES * TOPK * EXPERTS, "p (n e) -> p n e", dict(e=EXPERTS))])
        xs, e_xt, e_gate, e_act, e_act_t, ys, s_xt = carve(q_t_mem, [
            (XR * D, "p (r d) -> p r d", dict(r=XR)), (4 * P, "p (r c t) -> p r c t", dict(r=2, c=2)),
            (2 * INNER, *pair), (2 * INNER, *pair), (4 * P, "p (r c t) -> p r c t", dict(r=2, c=2)),
            (YR * D, "p (r d) -> p r d", dict(r=YR)), (DC * P, "p (c t) -> p c t", dict(c=DC))])
        e_act_t = e_act_t[0:HALF]
        q_cos = sb("q_cos", [P, 2, QG, ROPE])
        q_sin = sb("q_sin", [P, 2, QG, ROPE])
        neg_max = sb("neg_max", [P, 3, TPB])
        p_hi = sb("p_hi", [P, 2, 3 * P], F16)
        p_lo = sb("p_lo", [P, 2, 3 * P], F16)
        inv_sum = sb("inv_sum", [P, 2, 2 * TPB])
        res = sb("res", [P, TPB, D])
        turned = sb("turned", [P, TPB, DC, P])
        stats = sb("stats", [P, TPB, 6])
        moments = sb("moments", [P, TPB, 2])
        var_eps = sb("var_eps", [P, TPB, 1])
        rstd = sb("rstd", [P, TPB, 1])
        ids_i = sb("ids_i", [P, TILES], I32)
        ids_f = sb("ids_f", [P, TILES])
        above = sb("above", [P, TILES])
        picks = sb("picks", [P, TILES, CTX])
        logits = sb("logits", [P, TILES, EXPERTS])
        top = sb("top", [P, TILES, 8])
        top_i = sb("top_i", [P, TILES, 8], U32)
        top_f = sb("top_f", [P, TILES, TOPK])
        onehot = sb("onehot", [P, 2, TOPK, EXPERTS])
        chosen = sb("chosen", [P, TILES, EXPERTS], BF16)
        seen = sb("seen", [P, TILES + 1, EXPERTS], BF16)
        place = sb("place", [P, TILES, EXPERTS])
        placed = sb("placed", [P, 2, TOPK, EXPERTS])
        slot_f = sb("slot_f", [P, TILES, TOPK])
        slot = sb("slot", [P, TILES, TOPK], U32)
        count = sb("count", [P, EXPERTS])
        full = sb("full", [P, EXPERTS, TILES])
        tiles_of = sb("tiles_of", [P, EXPERTS])
        prior = sb("prior", [P, EXPERTS, EXPERTS])
        base = sb("base", [P, EXPERTS])
        t_expert = sb("t_expert", [P, SLOT_TILES])
        t_first = sb("t_first", [P, SLOT_TILES])
        t_within = sb("t_within", [P, SLOT_TILES])
        t_row = sb("t_row", [P, SLOT_TILES])
        tile_expert = sb("tile_expert", [P, SLOT_TILES], I32)
        shift = sb("shift", [P, EXPERTS])
        y_slot = sb("y_slot", [P, TILES, TOPK], U32)
        tile_block = sb("tile_block", [P, SLOT_TILES], I32)
        shifted = sb("shifted", [P, TILES, EXPERTS])
        soft_sum = sb("soft_sum", [P, TILES])
        soft_inv = sb("soft_inv", [P, TILES])
        soft_top = sb("soft_top", [P, TILES, TOPK])
        weight = sb("weight", [P, TILES, TOPK])

        zero_table = full[:, :, :].rearrange("p e n -> p (e n)").bitcast(U32)
        idx = sb("idx", [P, XR, 1], U32)

        in_xt = sem("in_xt")
        in_wqkv = sem("in_wqkv")
        in_norms = sem("in_norms")
        in_rope = sem("in_rope")
        in_rawq = sem("in_rawq")
        in_rawkv = sem("in_rawkv")
        in_wpe = sem("in_wpe")
        in_rawo = sem("in_rawo")
        in_x = sem("in_x")
        in_ids = sem("in_ids")
        in_wctx = sem("in_wctx")
        in_wgate = sem("in_wgate")
        in_wshared = sem("in_wshared")
        in_wgu = sem("in_wgu")
        in_wdown = sem("in_wdown")
        table_zeroed = sem("table_zeroed")
        const_made = sem("const_made")
        eye_made = sem("eye_made")
        norms_scaled = sem("norms_scaled")
        qkv_done = sem("qkv_done")
        ssq_done = sem("ssq_done")
        rms_eps_done = sem("rms_eps_done")
        rms_done = sem("rms_done")
        qn_done = sem("qn_done")
        kvc_done = sem("kvc_done")
        krope_done = sem("krope_done")
        kv_done = sem("kv_done")
        vhi_done = sem("vhi_done")
        vlo_done = sem("vlo_done")
        fturn_done = sem("fturn_done")
        fevac_done = sem("fevac_done")
        qproj_done = sem("qproj_done")
        qrope_done = sem("qrope_done")
        abs_done = sem("abs_done")
        qrow_done = sem("qrow_done")
        qturn_done = sem("qturn_done")
        qt_done = sem("qt_done")
        absorbed_q = sem("absorbed_q")
        absorbed_q_kept = sem("absorbed_q_kept")
        absorbed_o = sem("absorbed_o")
        absorbed_o_kept = sem("absorbed_o_kept")
        scores_done = sem("scores_done")
        max_done = sem("max_done")
        exp_done = sem("exp_done")
        pturn_done = sem("pturn_done")
        phi_done = sem("phi_done")
        plo_done = sem("plo_done")
        pv_done = sem("pv_done")
        inv_done = sem("inv_done")
        onorm_done = sem("onorm_done")
        oturn_done = sem("oturn_done")
        ot_done = sem("ot_done")
        oproj_done = sem("oproj_done")
        r1_done = sem("r1_done")
        r1_stat = sem("r1_stat")
        r1_mom = sem("r1_mom")
        r1_eps = sem("r1_eps")
        r1_rstd = sem("r1_rstd")
        x1_done = sem("x1_done")
        x1turn_done = sem("x1turn_done")
        x1t_done = sem("x1t_done")
        up_done = sem("up_done")
        pick_step = sem("pick_step")
        silu_done = sem("silu_done")
        a_done = sem("a_done")
        aturn_done = sem("aturn_done")
        at_done = sem("at_done")
        down_done = sem("down_done")
        sel_step = sem("sel_step")
        r2_stat = sem("r2_stat")
        r2_mom = sem("r2_mom")
        r2_eps = sem("r2_eps")
        r2_rstd = sem("r2_rstd")
        x2_done = sem("x2_done")
        x2turn_done = sem("x2turn_done")
        x2t_done = sem("x2t_done")
        gate_done = sem("gate_done")
        logits_done = sem("logits_done")
        masks_step = sem("masks_step")
        route_step = sem("route_step")
        chosen_done = sem("chosen_done")
        seen_done = sem("seen_done")
        rank_done = sem("rank_done")
        place_done = sem("place_done")
        placed_done = sem("placed_done")
        slot_done = sem("slot_done")
        scattered = sem("scattered")
        s_xturn_done = sem("s_xturn_done")
        s_xt_done = sem("s_xt_done")
        s_gu_done = sem("s_gu_done")
        s_silu_done = sem("s_silu_done")
        s_act_done = sem("s_act_done")
        s_turn_done = sem("s_turn_done")
        s_actt_done = sem("s_actt_done")
        s_down_done = sem("s_down_done")
        s_sum_done = sem("s_sum_done")
        count_done = sem("count_done")
        count_kept = sem("count_kept")
        plan_step = sem("plan_step")
        plan_done = sem("plan_done")
        y_slot_step = sem("y_slot_step")
        y_slot_done = sem("y_slot_done")
        soft_step = sem("soft_step")
        soft_shift = sem("soft_shift")
        soft_exp = sem("soft_exp")
        weight_done = sem("weight_done")
        e_turn_done = sem("e_turn_done")
        e_xt_done = sem("e_xt_done")
        e_gu_done = sem("e_gu_done")
        e_silu_done = sem("e_silu_done")
        e_act_done = sem("e_act_done")
        e_aturn_done = sem("e_aturn_done")
        e_actt_done = sem("e_actt_done")
        e_down_done = sem("e_down_done")
        e_y_done = sem("e_y_done")
        sum_step = sem("sum_step")
        r3_stat = sem("r3_stat")
        r3_mom = sem("r3_mom")
        r3_eps = sem("r3_eps")
        r3_rstd = sem("r3_rstd")
        fin_done = sem("fin_done")
        x2_stored = [sem(f"x2_stored{n}") for n in range(TILES)]
        idx_in = [sem(f"idx_in{r}") for r in range(XR)]
        xs_in = [sem(f"xs_in{r}") for r in range(XR)]
        y_stored = [sem(f"y_stored{r}") for r in range(YR)]
        back_in = [sem(f"back_in{r}") for r in range(2)]
        fin_stored = [sem(f"fin_stored{r}") for r in range(2)]

        def core_order(b):
            for h in range(HEADS + 3):
                if h < HEADS:
                    yield "scores", b, h
                if 2 <= h < HEADS + 2:
                    yield "turn", b, h - 2
                if h >= 3:
                    yield "values", b, h - 3

        def front_order(b):
            yield "qkv", b, 0
            yield "qkv", b, 1
            yield "norm", b, 0
            yield "norm", b, 1
            for j in range(TPB):
                for g in range(GROUPS + 1):
                    if g < GROUPS:
                        yield "qproj", b, (j, g)
                    if g >= 1:
                        yield "qturn", b, (j, g - 1)

        def back_order(b):
            for step in ("oproj", "x1", "up", "down", "x2", "route"):
                for j in range(TPB):
                    yield step, b, j

        def shared_order(b):
            for j in range(TPB):
                yield "shared", b, j

        def weave(long, short):
            long, short = list(long), list(short)
            done = 0
            for i, step in enumerate(long):
                yield step
                upto = (i + 1) * len(short) // len(long)
                yield from short[done:upto]
                done = upto

        def order():
            front = list(front_order(0))
            yield from front[:4]
            yield "absorb", 0, 0
            yield from front[4:]
            for b in range(BATCH):
                yield from core_order(b)
                if b + 1 < BATCH:
                    yield from weave(front_order(b + 1), back_order(b))
                else:
                    yield from back_order(b)
            yield "plan", 0, 0
            for b in range(SHARED_EARLY):
                yield from shared_order(b)
            yield from ((("e_x", 0, s) if k == 0 else ("e_y", 0, s - 1))
                        for s in range(SLOT_TILES + 1) for k in range(2)
                        if (k == 0 and s < SLOT_TILES) or (k == 1 and s >= 1))
            late = [step for b in range(SHARED_EARLY, BATCH) for step in shared_order(b)]
            yield from weave([("combine", 0, n) for n in range(len(late))], late)
            for n in range(len(late), TILES):
                yield "combine", 0, n

        SHARED_EARLY = 2
        ORDER = list(order())

        def run(steps):
            for name, b, i in ORDER:
                if name in steps:
                    steps[name](b, i)

        block = ctx.enter_context(nc.Block())

        @block.sync
        def _(sp):
            xt_v = xT.rearrange("(c p) t -> p c t", p=P)
            sp.dma_start(x_t[:, :, :], xt_v[:, :, 0:SEQ]).then_inc(in_xt, 16)
            sp.dma_start(w_qkv[:, :, :], wqkvT.rearrange("(c p) n -> p c n", p=P)).then_inc(in_wqkv, 16)
            sp.dma_start(w_qn[:, :], qlnw.partition_broadcast(P)).then_inc(in_norms, 16)
            sp.dma_start(w_kn[:, :], kvlnw.partition_broadcast(P)).then_inc(in_norms, 16)
            sp.dma_start(raw_kv, kvb.rearrange("(h t p) r -> p h t r", h=HEADS, t=2)).then_inc(in_rawkv, 16)
            sp.dma_start(raw_q, qnope.rearrange("h p r -> p h r")).then_inc(in_rawq, 16)
            sp.dma_start(cos[:, :, :], cosT.rearrange("(j p) r -> p j r", p=P)).then_inc(in_rope, 16)
            sp.dma_start(sin[:, :, :], sinT.rearrange("(j p) r -> p j r", p=P)).then_inc(in_rope, 16)
            qpe_v = qpeT.rearrange("(c p) h r -> p c h r", p=QC)
            for c in range(2):
                sp.dma_start(w_q[:, c, :, KR:HD], qpe_v[:, c]).then_inc(in_wpe, 16)
            sp.dma_start(raw_o, woT.rearrange("(h p) d -> p h d", p=P)).then_inc(in_rawo, 16)
            sp.dma_start(rows[:, :, :], x.rearrange("(n p) d -> p n d", p=P)).then_inc(in_x, 16)
            sp.dma_start(ids_i[:, :], ids).then_inc(in_ids, 16)
            sp.dma_start(w_ctx[:, :, :], ctxT.rearrange("(c p) n -> p c n", p=P)).then_inc(in_wctx, 16)
            sp.dma_start(w_gate[:, :, :], wgateT.rearrange("(c p) n -> p c n", p=P)).then_inc(in_wgate, 16)
            sp.wait_ge(const_made, 1)
            sp.dma_start(table.rearrange("(p n) o -> p (n o)", p=P), zero_table[:, :]).then_inc(table_zeroed, 16)
            sp.dma_start(w_gu[:, :, :, :], wgu.rearrange("(c p) e n -> p c e n", p=P)).then_inc(in_wgu, 16)
            sp.wait_ge(absorbed_o, 1)
            sp.dma_start(w_down, wd.rearrange("e (c p) d -> p e c d", p=HALF)).then_inc(in_wdown, 16)

            def next_x(b, h):
                if h == 0 and b + 1 < BATCH:
                    sp.wait_ge(qkv_done, TPB * (b + 1))
                    sp.dma_start(x_t[:, :, :], xt_v[:, :, (b + 1) * SEQ:(b + 2) * SEQ]).then_inc(in_xt, 16)

            def x2_store(b, j):
                n = TPB * b + j
                sp.wait_ge(x2_done, n + 1)
                sp.dma_start(x2_dram[n * P:(n + 1) * P, :], rows[:, n, :]).then_inc(x2_stored[n], 16)

            def plan(b, i):
                sp.wait_ge(plan_done, 2)
                sp.wait_ge(scattered, 16 * TILES * TOPK)
                idx_load(0)
                idx_load(1)
                idx_load(2)

            def idx_load(s):
                if s >= SLOT_TILES:
                    return
                if s >= XR:
                    sp.wait_ge(xs_in[s % XR], 16 * (s // XR))
                block_no = sp.value_load(tile_block[0:1, s:s + 1], min_val=0, max_val=EXPERTS * TILES - 1)
                sp.dma_start(idx[:, s % XR, :], table[bass.ds(block_no * P, P), :]).then_inc(idx_in[s % XR], 16)

            def e_x(b, s):
                idx_load(s + 3)

            def e_y(b, s):
                sp.wait_ge(e_y_done, s + 1)
                sp.dma_start(y_dram[s * P:(s + 1) * P, :], ys[:, s % YR, :]).then_inc(y_stored[s % YR], 16)

            def combine(b, n):
                sp.wait_ge(fin_done, n + 1)
                sp.dma_start(out[n * P:(n + 1) * P, :], fin[:, n % 2, :]).then_inc(fin_stored[n % 2], 16)

            run({"scores": next_x, "x2": x2_store, "plan": plan, "e_x": e_x, "e_y": e_y, "combine": combine})
            for r in range(2):
                sp.wait_ge(fin_stored[r], 16 * TILES // 2)

        @block.gpsimd
        def _(pool):
            pool.memset(zero_table[:, :], 0).then_inc(const_made, 1)
            pool.memset(ident[:, :], 0.0).then_inc(eye_made, 1)
            pool.wait_ge(eye_made, 1)
            pool.affine_select(out=ident[:, :], in_=ident[:, :], compare_op=ALU.not_equal, fill=1.0,
                               base=0, pattern=[[-1, P]], channel_multiplier=1).then_inc(eye_made, 1)
            pool.wait_ge(eye_made, 2)
            pool.tensor_copy(ident16[:, :], ident[:, :]).then_inc(eye_made, 1)
            pool.memset(causal[:, :], 0.0).then_inc(eye_made, 1)
            pool.memset(ones[:, :], 1.0).then_inc(eye_made, 1)
            pool.memset(minus_half[:, :], -0.5).then_inc(eye_made, 1)
            pool.wait_ge(eye_made, 6)
            pool.affine_select(out=causal[:, :], in_=causal[:, :], compare_op=ALU.is_ge, fill=MASKED,
                               base=0, pattern=[[-1, P]], channel_multiplier=1).then_inc(eye_made, 1)
            pool.affine_select(out=earlier[:, :], in_=ones[:, :], compare_op=ALU.is_gt, fill=0.0,
                               base=0, pattern=[[1, P]], channel_multiplier=-1).then_inc(eye_made, 1)
            for v, dst in ((1.0, v_hi), (0.0, v_lo)):
                pool.memset(dst[:, :, KR:KR + 2], v).then_inc(eye_made, 1)
            pool.memset(seen[:, 0, :], 0.0).then_inc(eye_made, 1)
            pool.iota(iota16[:, :], pattern=[[1, EXPERTS]], base=0, channel_multiplier=0,
                      allow_small_or_imprecise_dtypes=True).then_inc(eye_made, 1)
            pool.iota(region[:, :], pattern=[[TOKENS, EXPERTS]], base=0, channel_multiplier=0,
                      allow_small_or_imprecise_dtypes=True).then_inc(eye_made, 1)
            pool.iota(tile_starts[:, :], pattern=[[P, TILES]], base=0, channel_multiplier=0,
                      allow_small_or_imprecise_dtypes=True).then_inc(eye_made, 1)
            pool.iota(slot_iota[:, :], pattern=[[1, SLOT_TILES]], base=0, channel_multiplier=0,
                      allow_small_or_imprecise_dtypes=True).then_inc(eye_made, 1)
            pool.iota(token_id[:, :], pattern=[[P, TILES]], base=0, channel_multiplier=1).then_inc(eye_made, 1)
            pool.memset(before[:, :, :], 1.0).then_inc(eye_made, 1)
            pool.wait_ge(eye_made, 17)
            pool.affine_select(out=before[:, :, :], in_=before[:, :, :], compare_op=ALU.is_gt, fill=0.0,
                               base=0, pattern=[[1, EXPERTS], [-1, EXPERTS]],
                               channel_multiplier=0).then_inc(eye_made, 1)

            def rms_of(b, i):
                if i == 0:
                    pool.wait_ge(ssq_done, 4 * (b + 1))
                    if 2 * b > 0:
                        pool.wait_ge(qn_done, 2 * b)
                    if 2 * b > 0:
                        pool.wait_ge(kvc_done, 2 * b)
                    pool.tensor_scalar(ssq_eps[:, :], ssq[:, :], RMS_EPS, None, ALU.add).then_inc(rms_eps_done, 1)
                    pool.wait_ge(rms_eps_done, b + 1)
                    pool.tensor_tensor(rms[:, :], ssq_eps[:, :], minus_half[:, :], ALU.pow).then_inc(rms_done, 1)
                n = TPB * b + i
                pool.wait_ge(kvc_done, n + 1)
                if HEADS * b > 0:
                    pool.wait_ge(pv_done, HEADS * b)
                pool.tensor_copy(v_hi[:, i, 0:KR], kv_row[:, i, 0:KR]).then_inc(vhi_done, 1)
                pool.wait_ge(vhi_done, n + 1)
                pool.tensor_tensor(v_lo[:, i, 0:KR], kv_row[:, i, 0:KR], v_hi[:, i, 0:KR],
                                   ALU.subtract).then_inc(vlo_done, 1)

            def q_rotary(b, jg):
                j, g = jg
                i = GROUPS * (TPB * b + j) + g
                pool.wait_ge(qrope_done, i + 1)
                if i + 1 - TPB * GROUPS > 0:
                    pool.wait_ge(qturn_done, i + 1 - TPB * GROUPS)
                pool.tensor_tensor(q_row[:, j, QG * g:QG * g + QG, KR:HD], q_cos[:, i % 2], q_sin[:, i % 2],
                                   ALU.add).then_inc(qrow_done, 1)

            def rstd_of(mom, eps, inverse, j, n):
                pool.wait_ge(mom, n + 1)
                pool.tensor_scalar(var_eps[:, j, :], moments[:, j, 1:2], LN_EPS, None, ALU.add)\
                    .then_inc(eps, 1)
                pool.wait_ge(eps, n + 1)
                pool.tensor_tensor(rstd[:, j, :], var_eps[:, j, :], minus_half[:, 0:1], ALU.pow)\
                    .then_inc(inverse, 1)

            def route(b, j):
                n = TPB * b + j
                pool.wait_ge(slot_done, n + 1)
                pool.wait_ge(table_zeroed, 16)
                for k in range(TOPK):
                    pool.indirect_dma_start(out=table, out_offset=bass.IndirectOffsetOnAxis(ap=slot[:, n, k:k + 1], axis=0),
                                            in_=token_id[:, n:n + 1], in_offset=None).then_inc(scattered, 16)

            def gather_x(s):
                if s >= SLOT_TILES:
                    return
                if s == 0:
                    for n in range(TILES):
                        pool.wait_ge(x2_stored[n], 16)
                pool.wait_ge(idx_in[s % XR], 16 * (s // XR + 1))
                if s >= XR:
                    pool.wait_ge(e_turn_done, s - XR + 1)
                pool.indirect_dma_start(out=xs[:, s % XR, :], out_offset=None, in_=x2_dram,
                                        in_offset=bass.IndirectOffsetOnAxis(ap=idx[:, s % XR, :], axis=0))\
                    .then_inc(xs_in[s % XR], 16)

            def plan(b, i):
                gather_x(0)
                gather_x(1)

            def e_x(b, s):
                gather_x(s + 2)

            gathered = [0]

            def combine_gather(n):
                if n >= TILES:
                    return
                if n == 0:
                    for r in range(YR):
                        pool.wait_ge(y_stored[r], 16 * len(range(r, SLOT_TILES, YR)))
                    pool.wait_ge(y_slot_done, 1)
                if TOPK * (n - 1) > 0:
                    pool.wait_ge(sum_step, TOPK * (n - 1))
                for k in range(TOPK):
                    pool.indirect_dma_start(out=back[:, n % 2, k, :], out_offset=None, in_=y_dram,
                                            in_offset=bass.IndirectOffsetOnAxis(ap=y_slot[:, n, k:k + 1], axis=0))\
                        .then_inc(back_in[n % 2], 16)

            def combine(b, n):
                if n == 0:
                    combine_gather(0)
                combine_gather(n + 1)
                rstd_of(r3_mom, r3_eps, r3_rstd, n % 2, n)

            run({"norm": rms_of, "qproj": q_rotary,
                 "x1": lambda b, j: rstd_of(r1_mom, r1_eps, r1_rstd, j, TPB * b + j),
                 "x2": lambda b, j: rstd_of(r2_mom, r2_eps, r2_rstd, j, TPB * b + j),
                 "route": route, "plan": plan, "e_x": e_x, "combine": combine})

        @block.scalar
        def _(act):
            def mean_squares(b, j):
                n = TPB * b + j
                act.wait_ge(qkv_done, n + 1)
                if b > 0:
                    act.wait_ge(rms_eps_done, b)
                for k, (at, w) in enumerate(((0, QR), (QR, KR))):
                    act.activation(act_junk[:, j, at:at + w], bank[j][:, at:at + w], ACT.Square, scale=float(w) ** -0.5,
                                   accum_out=ssq[:, 2 * j + k:2 * j + k + 1]).then_inc(ssq_done, 1)

            def latents_t(b, j):
                n = TPB * b + j
                act.wait_ge(fturn_done, n + 1)
                if TPB * GROUPS * b > 0:
                    act.wait_ge(qproj_done, TPB * GROUPS * b)
                if HEADS * b > 0:
                    act.wait_ge(scores_done, HEADS * b)
                turned = bank[2 + j][0:QC, 0:2 * P].rearrange("p (c t) -> p c t", c=2)
                act.activation(qn_t[:, :, j * P:(j + 1) * P], turned, ACT.Copy).then_inc(fevac_done, 1)
                act.activation(k_t[:, j * P:(j + 1) * P], bank[2 + j][:, 2 * P:3 * P], ACT.Copy).then_inc(fevac_done, 1)

            def absorb(b, i):
                for c in range(2):
                    for half in range(2):
                        act.wait_ge(absorbed_q, 2 * c + half + 1)
                        act.activation(w_q[:, c, 8 * half:8 * half + 8, 0:KR], bank[4 + 2 * c + half][0:QC, :].rearrange("p (h r) -> p h r", h=8), ACT.Copy).then_inc(absorbed_q_kept, 1)
                act.wait_ge(absorbed_o, 1)
                for k in range(4):
                    act.activation(w_out[:, 2 * k:2 * k + 2, :], bank[4 + k][:, :].rearrange("p (h d) -> p h d", h=2), ACT.Copy).then_inc(absorbed_o_kept, 1)

            def q_absorbed(b, jg):
                j, g = jg
                i = GROUPS * (TPB * b + j) + g
                act.wait_ge(qrope_done, i + 1)
                if i + 1 - TPB * GROUPS > 0:
                    act.wait_ge(qturn_done, i + 1 - TPB * GROUPS)
                act.activation(q_row[:, j, QG * g:QG * g + QG, 0:KR], bank[g % 2][:, :].rearrange("p (h d) -> p h d", h=QG)[:, :, 0:KR], ACT.Copy).then_inc(abs_done, 1)

            def q_turned(b, jg):
                j, g = jg
                i = GROUPS * (TPB * b + j) + g
                act.wait_ge(qturn_done, i + 1)
                if HEADS * b > 0:
                    act.wait_ge(scores_done, HEADS * b)
                act.activation(q_t[:, QG * g:QG * g + QG, j * P:(j + 1) * P], bank[2 + g % 2][:, :].rearrange("p (h t) -> p h t", h=QG), ACT.Copy).then_inc(qt_done, 1)

            def exps(b, h):
                n = HEADS * b + h
                act.wait_ge(max_done, 2 * n + 2)
                if n - 2 > 0:
                    act.wait_ge(pturn_done, n - 2)
                if TPB * b > 0:
                    act.wait_ge(oproj_done, TPB * b)
                for q, (at, w) in enumerate(((0, P), (P, 2 * P))):
                    act.activation(probs[:, n % 3, at:at + w], bank[h % 3][:, at:at + w], ACT.Exp,
                                   bias=neg_max[:, n % 3, q:q + 1]).then_inc(exp_done, 1)

            def probs_hi(b, h):
                n = HEADS * b + h
                act.wait_ge(pturn_done, n + 1)
                if n - 1 > 0:
                    act.wait_ge(pv_done, n - 1)
                act.activation(p_hi[:, n % 2, :], bank[3 + h % 2][:, 0:3 * P], ACT.Copy).then_inc(phi_done, 1)

            def o_turned(b, j):
                n = TPB * b + j
                for half in range(2):
                    act.wait_ge(oturn_done, 2 * n + half + 1)
                    if n > 0:
                        act.wait_ge(oproj_done, n)
                    act.activation(o_t[:, 4 * half:4 * half + 4, :], bank[4 + half][:, :].rearrange("p (c t) -> p c t", c=4), ACT.Copy).then_inc(ot_done, 1)

            def turned_back(j, n, turn_done, used, done, used_n):
                act.wait_ge(turn_done, n + 1)
                if used_n > 0:
                    act.wait_ge(used, used_n)
                act.activation(turned[:, j], bank[4 + j][:, 0:D].rearrange("p (c t) -> p c t", c=DC), ACT.Copy)\
                    .then_inc(done, 1)

            def up(b, j):
                n = TPB * b + j
                turned_back(j, n, x1turn_done, gate_done, x1t_done, n - 1)
                act.wait_ge(pick_step, CTX * (n + 1))
                if n - 1 > 0:
                    act.wait_ge(a_done, n - 1)
                act.activation(gated[:, j, :], picked[:, j, :], ACT.Silu).then_inc(silu_done, 1)

            def down(b, j):
                n = TPB * b + j
                turned_back(j, n, aturn_done, up_done, at_done, n + 1)

            def route(b, j):
                n = TPB * b + j
                turned_back(j, n, x2turn_done, down_done, x2t_done, n + 1)

            def shared(b, j):
                n = TPB * b + j
                act.wait_ge(s_xturn_done, n + 1)
                if 2 * n > 0:
                    act.wait_ge(s_gu_done, 2 * n)
                act.activation(s_xt[:, :, :], bank[4][:, 0:D].rearrange("p (c t) -> p c t", c=DC), ACT.Copy).then_inc(s_xt_done, 1)
                for s in range(SHARED):
                    act.wait_ge(s_gu_done, 2 * n + s + 1)
                    if 2 * n + s - 1 > 0:
                        act.wait_ge(s_act_done, 2 * n + s - 1)
                    act.activation(s_gate[:, s, :], bank[6 + s][:, 0:INNER], ACT.Silu).then_inc(s_silu_done, 1)
                for s in range(SHARED):
                    act.wait_ge(s_turn_done, 2 * n + s + 1)
                    if n > 0:
                        act.wait_ge(s_down_done, n)
                    act.activation(s_act_t[:, s], bank[4 + s][0:HALF, 0:2 * P].rearrange("p (c t) -> p c t", c=2), ACT.Copy).then_inc(s_actt_done, 1)

            def plan(b, i):
                act.wait_ge(soft_shift, 1)
                act.activation(shifted[:, :, :], shifted[:, :, :], ACT.Exp).then_inc(soft_exp, 1)
                act.wait_ge(soft_shift, 2)
                act.activation(soft_top[:, :, :], soft_top[:, :, :], ACT.Exp).then_inc(soft_exp, 1)

            def e_x(b, s):
                act.wait_ge(e_turn_done, s + 1)
                if s - 1 > 0:
                    act.wait_ge(e_gu_done, s - 1)
                act.activation(e_xt[:, s % 2], bank[s % 2][:, 0:D].rearrange("p (c t) -> p c t", c=DC), ACT.Copy).then_inc(e_xt_done, 1)
                act.wait_ge(e_gu_done, s + 1)
                if s - 1 > 0:
                    act.wait_ge(e_act_done, s - 1)
                act.activation(e_gate[:, s % 2, :], bank[2 + s % 2][:, 0:INNER], ACT.Silu).then_inc(e_silu_done, 1)

            def e_y(b, s):
                act.wait_ge(e_down_done, s + 1)
                if s >= YR:
                    act.wait_ge(y_stored[s % YR], 16 * (s // YR))
                act.activation(ys[:, s % YR, :], bank[6 + s % 2][:, 0:D], ACT.Copy).then_inc(e_y_done, 1)

            run({"qkv": mean_squares, "norm": latents_t, "absorb": absorb, "qproj": q_absorbed, "qturn": q_turned,
                 "scores": exps, "turn": probs_hi, "oproj": o_turned, "up": up, "down": down, "route": route,
                 "shared": shared, "plan": plan, "e_x": e_x, "e_y": e_y})

        @block.tensor
        def _(pe):
            def qkv(b, j):
                n = TPB * b + j
                pe.wait_ge(in_xt, 16 * (b + 1))
                if b == 0:
                    pe.wait_ge(in_wqkv, 16)
                if 2 * HEADS * b > 0:
                    pe.wait_ge(exp_done, 2 * HEADS * b)
                for c in range(DC):
                    mm = pe.matmul(bank[j][:, 0:QR + HD], x_t[:, c, j * P:(j + 1) * P], w_qkv[:, c, :],
                                   start=(c == 0), stop=(c == DC - 1))
                mm.then_inc(qkv_done, 1)

            def latents_turn(b, j):
                n = TPB * b + j
                if n == 0:
                    pe.wait_ge(eye_made, 18)
                pe.wait_ge(qn_done, n + 1)
                pe.wait_ge(kv_done, n + 1)
                if HEADS * b > 0:
                    pe.wait_ge(phi_done, HEADS * b)
                if HEADS * b > 0:
                    pe.wait_ge(plo_done, HEADS * b)
                for c in range(2):
                    pe.transpose(bank[2 + j][0:QC, c * P:(c + 1) * P], qn[:, j, c * QC:(c + 1) * QC], ident[:, :])
                pe.transpose(bank[2 + j][:, 2 * P:3 * P], kv_row[:, j, :], ident[:, :]).then_inc(fturn_done, 1)

            def absorb(b, i):
                pe.wait_ge(in_rawq, 16)
                pe.wait_ge(in_rawkv, 16)
                for c in range(2):
                    for half in range(2):
                        for h in range(8):
                            mm = pe.matmul(bank[4 + 2 * c + half][0:QC, h * KR:(h + 1) * KR],
                                           raw_q[:, 8 * half + h, c * QC:(c + 1) * QC], raw_kv[:, 8 * half + h, 0, :],
                                           start=True, stop=True)
                        mm.then_inc(absorbed_q, 1)
                pe.wait_ge(in_rawo, 16)
                pe.wait_ge(absorbed_q_kept, 4)
                for h in range(HEADS):
                    at = KR * (h % 2)
                    mm = pe.matmul(bank[4 + h // 4][at:at + KR, (h // 2 % 2) * D:(h // 2 % 2 + 1) * D],
                                   raw_kv[:, h, 1, :], raw_o[:, h, :], start=True, stop=True)
                mm.then_inc(absorbed_o, 1)

            def qproj(b, jg):
                j, g = jg
                n = TPB * b + j
                i = GROUPS * n + g
                pe.wait_ge(fevac_done, 2 * n + 2)
                if i == 0:
                    pe.wait_ge(absorbed_q_kept, 4)
                    pe.wait_ge(in_wpe, 32)
                if i % (TPB * GROUPS) < 2:
                    pe.wait_ge(krope_done, 3 * (TPB * b + g + 1))
                if i - 1 > 0:
                    pe.wait_ge(abs_done, i - 1)
                for c in range(2):
                    mm = pe.matmul(bank[g % 2][:, :], qn_t[:, c, j * P:(j + 1) * P],
                                   w_q[:, c, QG * g:QG * g + QG, :], start=(c == 0), stop=(c == 1))
                mm.then_inc(qproj_done, 1)

            def qturn(b, jg):
                j, g = jg
                n = TPB * b + j
                i = GROUPS * n + g
                pe.wait_ge(abs_done, i + 1)
                pe.wait_ge(qrow_done, i + 1)
                if i % (TPB * GROUPS) < 2:
                    pe.wait_ge(fevac_done, 2 * (TPB * b + g + 1))
                if i - 1 > 0:
                    pe.wait_ge(qt_done, i - 1)
                for k in range(QG):
                    mm = pe.transpose(bank[2 + g % 2][:, k * P:(k + 1) * P], q_row[:, j, QG * g + k, :], ident[:, :])
                mm.then_inc(qturn_done, 1)

            def scores(b, h):
                n = HEADS * b + h
                s = bank[h % 3]
                if h == 0:
                    pe.wait_ge(qt_done, TPB * GROUPS * (b + 1))
                    pe.wait_ge(fevac_done, 2 * TPB * (b + 1))
                else:
                    if 2 * (n - 2) > 0:
                        pe.wait_ge(exp_done, 2 * (n - 2))
                pe.matmul(s[:, 0:P], q_t[:, h, 0:P], k_t[:, 0:P], start=True, stop=False)
                pe.matmul(s[:, 0:P], ident16[:, :], causal[:, :], start=False, stop=True)
                pe.matmul(s[:, P:3 * P], q_t[:, h, P:2 * P], k_t[:, :], start=True, stop=False)
                pe.matmul(s[:, 2 * P:3 * P], ident16[:, :], causal[:, :], start=False, stop=True)\
                    .then_inc(scores_done, 1)

            def turn(b, h):
                n = HEADS * b + h
                pe.wait_ge(exp_done, 2 * n + 2)
                if h == 0:
                    if TPB * b > 0:
                        pe.wait_ge(place_done, TPB * b)
                if n - 1 > 0:
                    pe.wait_ge(plo_done, n - 1)
                for k in range(3):
                    mm = pe.transpose(bank[3 + h % 2][:, k * P:(k + 1) * P], probs[:, n % 3, k * P:(k + 1) * P],
                                      ident[:, :])
                mm.then_inc(pturn_done, 1)

            def values(b, h):
                n = HEADS * b + h
                pe.wait_ge(phi_done, n + 1)
                pe.wait_ge(plo_done, n + 1)
                pe.wait_ge(vlo_done, TPB * (b + 1))
                if h % 2 == 0:
                    if n // 2 - 1 > 0:
                        pe.wait_ge(onorm_done, n // 2 - 1)
                o = bank[5 + (h // 2) % 2]
                for q, blocks in enumerate(((0,), (1, 2))):
                    at = (2 * (h % 2) + q) * (KR + 1)
                    parts = [(pp, vv, k) for k in blocks for pp, vv in ((p_hi, v_hi), (p_hi, v_lo), (p_lo, v_hi))]
                    for i, (pp, vv, k) in enumerate(parts):
                        mm = pe.matmul(o[:, at:at + KR + 1], pp[:, n % 2, k * P:(k + 1) * P],
                                       vv[:, k // 2, 0:KR + 1], start=(i == 0), stop=(i == len(parts) - 1))
                mm.then_inc(pv_done, 1)

            def oproj(b, j):
                n = TPB * b + j
                pe.wait_ge(onorm_done, HEADS // 2 * (b + 1))
                for half in range(2):
                    if 2 * n + half - 1 > 0:
                        pe.wait_ge(ot_done, 2 * n + half - 1)
                    for k in range(4):
                        at = (4 * half + k) * P
                        mm = pe.transpose(bank[4 + half][:, k * P:(k + 1) * P], o_row[:, j, at:at + P], ident[:, :])
                    mm.then_inc(oturn_done, 1)
                if n == 0:
                    pe.wait_ge(absorbed_o_kept, 4)
                pe.wait_ge(ot_done, 2 * n + 2)
                for c in range(HEADS // 2):
                    mm = pe.matmul(bank[6 + j][:, 0:D], o_t[:, c, :], w_out[:, c, :],
                                   start=(c == 0), stop=(c == HEADS // 2 - 1))
                mm.then_inc(oproj_done, 1)

            def turn2(src, j, done):
                for c in range(DC):
                    mm = pe.transpose(bank[4 + j][:, c * P:(c + 1) * P], src[:, c * P:(c + 1) * P], ident[:, :])
                mm.then_inc(done, 1)

            def ctx_product(src_t, j, done):
                for half in range(2):
                    for c in range(DC):
                        mm = pe.matmul(bank[6 + half][:, :], src_t[:, j, c, :], w_ctx[:, c, half * 512:(half + 1) * 512],
                                       start=(c == 0), stop=(c == DC - 1))
                mm.then_inc(done, 1)

            def up(b, j):
                n = TPB * b + j
                pe.wait_ge(x1_done, n + 1)
                pe.wait_ge(ot_done, 2 * TPB * (b + 1))
                turn2(res[:, j, :], j, x1turn_done)
                pe.wait_ge(x1t_done, n + 1)
                if n == 0:
                    pe.wait_ge(in_wctx, 16)
                pe.wait_ge(r1_done, TPB * (b + 1))
                if CTX * n > 0:
                    pe.wait_ge(pick_step, CTX * n)
                ctx_product(turned, j, up_done)

            def down(b, j):
                n = TPB * b + j
                pe.wait_ge(a_done, n + 1)
                turn2(a_row[:, j, :], j, aturn_done)
                pe.wait_ge(at_done, n + 1)
                pe.wait_ge(pick_step, CTX * TPB * (b + 1))
                if CTX * n > 0:
                    pe.wait_ge(sel_step, CTX * n)
                ctx_product(turned, j, down_done)

            def route(b, j):
                n = TPB * b + j
                pe.wait_ge(x2_done, n + 1)
                turn2(rows[:, n, :], j, x2turn_done)
                pe.wait_ge(x2t_done, n + 1)
                if n == 0:
                    pe.wait_ge(in_wgate, 16)
                for c in range(DC):
                    mm = pe.matmul(bank[4 + j][:, D:D + EXPERTS], turned[:, j, c, :], w_gate[:, c, :],
                                   start=(c == 0), stop=(c == DC - 1))
                mm.then_inc(gate_done, 1)
                pe.wait_ge(chosen_done, n + 1)
                if n > 0:
                    pe.wait_ge(seen_done, n)
                at = D + EXPERTS
                pe.matmul(bank[4 + j][:, at:at + EXPERTS], earlier[:, :], chosen[:, n, :], start=True, stop=False)
                pe.matmul(bank[4 + j][:, at:at + EXPERTS], ones[:, :], seen[:, n, :], start=False, stop=True)\
                    .then_inc(rank_done, 1)

            def shared(b, j):
                n = TPB * b + j
                if n == 0:
                    pe.wait_ge(in_wgu, 16)
                    pe.wait_ge(in_wdown, 16)
                    pe.wait_ge(count_kept, 1)
                if n == TPB * SHARED_EARLY:
                    pe.wait_ge(e_actt_done, SLOT_TILES)
                    pe.wait_ge(e_y_done, SLOT_TILES)
                if 2 * n > 0:
                    pe.wait_ge(s_actt_done, 2 * n)
                for c in range(DC):
                    mm = pe.transpose(bank[4][:, c * P:(c + 1) * P], rows[:, n, c * P:(c + 1) * P], ident[:, :])
                mm.then_inc(s_xturn_done, 1)
                pe.wait_ge(s_xt_done, n + 1)
                if n > 0:
                    pe.wait_ge(s_sum_done, n)
                for s in range(SHARED):
                    for c in range(DC):
                        mm = pe.matmul(bank[6 + s][:, 0:GU], s_xt[:, c, :], w_gu[:, c, EXPERTS + s, :],
                                       start=(c == 0), stop=(c == DC - 1))
                    mm.then_inc(s_gu_done, 1)
                for s in range(SHARED):
                    pe.wait_ge(s_act_done, 2 * n + s + 1)
                    if 2 * n + s - 1 > 0:
                        pe.wait_ge(s_actt_done, 2 * n + s - 1)
                    for c in range(2):
                        mm = pe.transpose(bank[4 + s][0:HALF, c * P:(c + 1) * P], s_act[:, s, c * HALF:(c + 1) * HALF],
                                          ident[:, :])
                    mm.then_inc(s_turn_done, 1)
                pe.wait_ge(s_actt_done, 2 * n + 2)
                for k in range(2 * SHARED):
                    s, c = k // 2, k % 2
                    mm = pe.matmul(bank[6][:, 0:D], s_act_t[:, s, c, :], w_down[:, EXPERTS + s, c, :],
                                   start=(k == 0), stop=(k == 2 * SHARED - 1))
                mm.then_inc(s_down_done, 1)

            def plan(b, i):
                pe.wait_ge(seen_done, TILES)
                pe.wait_ge(place_done, TILES)
                pe.matmul(bank[7][:, 0:EXPERTS], ones[:, :], seen[:, TILES, :], start=True, stop=True)\
                    .then_inc(count_done, 1)

            def e_x(b, s):
                pe.wait_ge(xs_in[s % XR], 16 * (s // XR + 1))
                if s - 1 > 0:
                    pe.wait_ge(e_xt_done, s - 1)
                for c in range(DC):
                    mm = pe.transpose(bank[s % 2][:, c * P:(c + 1) * P], xs[:, s % XR, c * P:(c + 1) * P], ident[:, :])
                mm.then_inc(e_turn_done, 1)
                if s == 0:
                    pe.wait_ge(plan_done, 2)
                e = pe.value_load(tile_expert[0:1, s:s + 1], min_val=0, max_val=EXPERTS - 1)
                pe.wait_ge(e_xt_done, s + 1)
                if s - 1 > 0:
                    pe.wait_ge(e_act_done, s - 1)
                for c in range(DC):
                    mm = pe.matmul(bank[2 + s % 2][:, 0:GU], e_xt[:, s % 2, c, :], w_gu[:, c, bass.ds(e, 1), :],
                                   start=(c == 0), stop=(c == DC - 1))
                mm.then_inc(e_gu_done, 1)

            def e_y(b, s):
                pe.wait_ge(e_act_done, s + 1)
                if s < 2:
                    pe.wait_ge(s_actt_done, 2 * TPB * SHARED_EARLY)
                    pe.wait_ge(s_sum_done, TPB * SHARED_EARLY)
                if s - 1 > 0:
                    pe.wait_ge(e_actt_done, s - 1)
                for c in range(2):
                    mm = pe.transpose(bank[4 + s % 2][0:HALF, c * P:(c + 1) * P], e_act[:, s % 2, c * HALF:(c + 1) * HALF],
                                      ident[:, :])
                mm.then_inc(e_aturn_done, 1)
                e = pe.value_load(tile_expert[0:1, s:s + 1], min_val=0, max_val=EXPERTS - 1)
                pe.wait_ge(e_actt_done, s + 1)
                if s - 1 > 0:
                    pe.wait_ge(e_y_done, s - 1)
                for c in range(2):
                    mm = pe.matmul(bank[6 + s % 2][:, 0:D], e_act_t[:, s % 2, c, :], w_down[:, bass.ds(e, 1), c, :],
                                   start=(c == 0), stop=(c == 1))
                mm.then_inc(e_down_done, 1)

            run({"qkv": qkv, "norm": latents_turn, "absorb": absorb, "qproj": qproj, "qturn": qturn, "scores": scores,
                 "turn": turn, "values": values, "oproj": oproj, "up": up, "down": down, "route": route,
                 "shared": shared, "plan": plan, "e_x": e_x, "e_y": e_y})

        @block.vector
        def _(dve):
            def masks():
                dve.wait_ge(in_ids, 16)
                dve.tensor_copy(ids_f[:, :], ids_i[:, :]).then_inc(masks_step, 1)
                dve.wait_ge(masks_step, 1)
                for e in range(CTX):
                    if e == 0:
                        dve.tensor_scalar(picks[:, :, 0], ids_f[:, :], float(CTX_STEP), None, ALU.is_lt).then_inc(masks_step, 1)
                    elif e == CTX - 1:
                        dve.tensor_scalar(picks[:, :, e], ids_f[:, :], float(e * CTX_STEP), None, ALU.is_ge).then_inc(masks_step, 1)
                    else:
                        dve.wait_ge(masks_step, 2 * e)
                        dve.tensor_scalar(above[:, :], ids_f[:, :], float(e * CTX_STEP), None, ALU.is_ge).then_inc(masks_step, 1)
                        dve.wait_ge(masks_step, 2 * e + 1)
                        dve.scalar_tensor_tensor(out=picks[:, :, e], in0=ids_f[:, :], scalar=float((e + 1) * CTX_STEP),
                                                     in1=above[:, :], op0=ALU.is_lt, op1=ALU.mult).then_inc(masks_step, 1)

            def norm(b, j):
                n = TPB * b + j
                if n == 0:
                    dve.wait_ge(in_norms, 32)
                    dve.tensor_scalar(w_qn[:, :], w_qn[:, :], SCALE, None, ALU.mult).then_inc(norms_scaled, 1)
                    dve.wait_ge(norms_scaled, 1)
                    dve.wait_ge(in_rope, 32)
                q = bank[j]
                dve.wait_ge(rms_done, b + 1)
                if n - 1 > 0:
                    dve.wait_ge(fturn_done, n - 1)
                if n - 1 > 0:
                    dve.wait_ge(vlo_done, n - 1)
                dve.scalar_tensor_tensor(out=qn[:, j, :], in0=q[:, 0:QR], scalar=rms[:, 2 * j:2 * j + 1],
                                             in1=w_qn[:, :], op0=ALU.mult, op1=ALU.mult).then_inc(qn_done, 1)
                dve.scalar_tensor_tensor(out=kv_row[:, j, 0:KR], in0=q[:, QR:QR + KR],
                                             scalar=rms[:, 2 * j + 1:2 * j + 2], in1=w_kn[:, :],
                                             op0=ALU.mult, op1=ALU.mult).then_inc(kvc_done, 1)
                pe_at, half = QR + KR, ROPE // 2
                if n - 1 > 0:
                    dve.wait_ge(kv_done, n - 1)
                dve.tensor_tensor(k_cos[:, j, :], q[:, pe_at:pe_at + ROPE], cos[:, j, :], ALU.mult).then_inc(krope_done, 1)
                for a, c in ((0, half), (half, 0)):
                    dve.tensor_tensor(k_sin[:, j, a:a + half], q[:, pe_at + c:pe_at + c + half],
                                          sin[:, j, a:a + half], ALU.mult).then_inc(krope_done, 1)
                dve.wait_ge(krope_done, 3 * (n + 1))
                dve.tensor_tensor(kv_row[:, j, KR:HD], k_cos[:, j, :], k_sin[:, j, :], ALU.add).then_inc(kv_done, 1)

            def q_rope(b, jg):
                j, g = jg
                i = GROUPS * (TPB * b + j) + g
                dve.wait_ge(qproj_done, i + 1)
                if i - 1 > 0:
                    dve.wait_ge(qrow_done, i - 1)
                half = ROPE // 2
                q = bank[g % 2][:, :].rearrange("p (h d) -> p h d", h=QG)

                def table(t, a, w):
                    return t[:, j, a:a + w].unsqueeze(1).broadcast_to([P, QG, w])

                dve.tensor_tensor(q_cos[:, i % 2], q[:, :, KR:HD], table(cos, 0, ROPE), ALU.mult)
                dve.tensor_tensor(q_sin[:, i % 2, :, 0:half], q[:, :, KR + half:HD], table(sin, 0, half), ALU.mult)
                dve.tensor_tensor(q_sin[:, i % 2, :, half:ROPE], q[:, :, KR:KR + half], table(sin, half, half),
                                      ALU.mult).then_inc(qrope_done, 1)

            def maxima(b, h):
                n = HEADS * b + h
                dve.wait_ge(scores_done, n + 1)
                if 2 * (n - 2) > 0:
                    dve.wait_ge(exp_done, 2 * (n - 2))
                for q, (at, w) in enumerate(((0, P), (P, 2 * P))):
                    dve.tensor_reduce(neg_max[:, n % 3, q:q + 1], bank[h % 3][:, at:at + w], AX, ALU.max,
                                          negate=True).then_inc(max_done, 1)

            def probs_lo(b, h):
                n = HEADS * b + h
                dve.wait_ge(phi_done, n + 1)
                if n - 1 > 0:
                    dve.wait_ge(pv_done, n - 1)
                dve.tensor_tensor(p_lo[:, n % 2, :], bank[3 + h % 2][:, 0:3 * P], p_hi[:, n % 2, :],
                                      ALU.subtract).then_inc(plo_done, 1)

            def head_out(b, h):
                if h % 2 == 0:
                    return
                n = HEADS * b + h
                pair = n // 2
                o = bank[5 + (h // 2) % 2][:, 0:4 * (KR + 1)].rearrange("p (h q r) -> p h q r", h=2, q=2)
                dve.wait_ge(pv_done, n + 1)
                if 2 * TPB * b > 0:
                    dve.wait_ge(oturn_done, 2 * TPB * b)
                if pair - 1 > 0:
                    dve.wait_ge(onorm_done, pair - 1)
                dve.reciprocal(inv_sum[:, pair % 2, :], o[:, :, :, KR]).then_inc(inv_done, 1)
                dve.wait_ge(inv_done, pair + 1)
                inv = inv_sum[:, pair % 2, :].rearrange("p (h q) -> p h q", h=2).unsqueeze(3).broadcast_to([P, 2, 2, KR])
                dst = o_row[:, :, (h - 1) * KR:(h + 1) * KR].rearrange("p q (h r) -> p h q r", h=2)
                dve.tensor_tensor(dst, o[:, :, :, 0:KR], inv, ALU.mult).then_inc(onorm_done, 1)

            def stats_of(stat, mom, j, n, src):
                dve.bn_stats(stats[:, j, :], src).then_inc(stat, 1)
                dve.wait_ge(stat, n + 1)
                dve.bn_aggr(moments[:, j, :], stats[:, j, :]).then_inc(mom, 1)

            def normed(inverse, j, n, dst, src, done):
                dve.wait_ge(inverse, n + 1)
                dve.tensor_scalar(dst, src, moments[:, j, 0:1], rstd[:, j, :], ALU.subtract, ALU.mult).then_inc(done, 1)

            def oproj(b, j):
                n = TPB * b + j
                dve.wait_ge(in_x, 16)
                dve.wait_ge(oproj_done, n + 1)
                dve.tensor_tensor(res[:, j, :], bank[6 + j][:, 0:D], rows[:, n, :], ALU.add).then_inc(r1_done, 1)
                dve.wait_ge(r1_done, n + 1)
                stats_of(r1_stat, r1_mom, j, n, res[:, j, :])

            def x1_norm(b, j):
                n = TPB * b + j
                if n - 1 > 0:
                    dve.wait_ge(x1turn_done, n - 1)
                normed(r1_rstd, j, n, res[:, j, :], res[:, j, :], x1_done)

            def expert_cols(e):
                return bank[6 + e // 2][:, (e % 2) * D:(e % 2 + 1) * D]

            def up(b, j):
                n = TPB * b + j
                if n == 0:
                    dve.wait_ge(masks_step, 7)
                dve.wait_ge(up_done, n + 1)
                if n - 1 > 0:
                    dve.wait_ge(silu_done, n - 1)
                if n - 1 > 0:
                    dve.wait_ge(a_done, n - 1)
                dve.tensor_scalar(picked[:, j, :], expert_cols(0), picks[:, n, 0:1], None, ALU.mult).then_inc(pick_step, 1)
                for e in range(1, CTX):
                    if CTX * n + e > 0:
                        dve.wait_ge(pick_step, CTX * n + e)
                    dve.scalar_tensor_tensor(out=picked[:, j, :], in0=expert_cols(e), scalar=picks[:, n, e:e + 1],
                                                 in1=picked[:, j, :], op0=ALU.mult, op1=ALU.add).then_inc(pick_step, 1)
                dve.wait_ge(silu_done, n + 1)
                dve.wait_ge(pick_step, CTX * (n + 1))
                if n - 1 > 0:
                    dve.wait_ge(aturn_done, n - 1)
                dve.tensor_tensor(a_row[:, j, :], gated[:, j, :], picked[:, j, :], ALU.mult).then_inc(a_done, 1)

            def down(b, j):
                n = TPB * b + j
                dve.wait_ge(down_done, n + 1)
                dve.wait_ge(x1_done, n + 1)
                for e in range(CTX):
                    if CTX * n + e > 0:
                        dve.wait_ge(sel_step, CTX * n + e)
                    dve.scalar_tensor_tensor(out=res[:, j, :], in0=expert_cols(e), scalar=picks[:, n, e:e + 1],
                                                 in1=res[:, j, :],
                                                 op0=ALU.mult, op1=ALU.add).then_inc(sel_step, 1)
                dve.wait_ge(sel_step, CTX * (n + 1))
                stats_of(r2_stat, r2_mom, j, n, res[:, j, :])

            def x2_norm(b, j):
                n = TPB * b + j
                normed(r2_rstd, j, n, rows[:, n, :], res[:, j, :], x2_done)

            def route(b, j):
                n = TPB * b + j
                step = [5 * n]

                def then(ins):
                    step[0] += 1
                    ins.then_inc(route_step, 1)
                    dve.wait_ge(route_step, step[0])

                dve.wait_ge(gate_done, n + 1)
                dve.tensor_copy(logits[:, n, :], bank[4 + j][:, D:D + EXPERTS]).then_inc(logits_done, 1)
                dve.wait_ge(logits_done, n + 1)
                then(dve.max(top[:, n, :], logits[:, n, :]))
                then(dve.max_index(top_i[:, n, :], top[:, n, :], logits[:, n, :]))
                then(dve.tensor_copy(top_f[:, n, :], top_i[:, n, 0:TOPK]))
                dve.wait_ge(eye_made, 18)
                then(dve.tensor_tensor(onehot[:, j], iota16[:, :].unsqueeze(1).broadcast_to([P, TOPK, EXPERTS]),
                                       top_f[:, n, :].unsqueeze(2).broadcast_to([P, TOPK, EXPERTS]), ALU.is_equal))
                with nc.allow_low_precision(reason="sums of at most 8 ones are exact"):
                    dve.tensor_reduce(chosen[:, n, :], onehot[:, j].rearrange("p k e -> p e k"), AX, ALU.add).then_inc(chosen_done, 1)
                    dve.wait_ge(chosen_done, n + 1)
                    dve.tensor_tensor(seen[:, n + 1, :], seen[:, n, :], chosen[:, n, :], ALU.add).then_inc(seen_done, 1)
                dve.wait_ge(rank_done, n + 1)
                at = D + EXPERTS
                dve.tensor_tensor(place[:, n, :], bank[4 + j][:, at:at + EXPERTS], region[:, :], ALU.add).then_inc(place_done, 1)
                dve.wait_ge(place_done, n + 1)
                dve.tensor_tensor(placed[:, j], onehot[:, j],
                                      place[:, n, :].unsqueeze(1).broadcast_to([P, TOPK, EXPERTS]), ALU.mult).then_inc(placed_done, 1)
                dve.wait_ge(placed_done, n + 1)
                then(dve.tensor_reduce(slot_f[:, n, :], placed[:, j], AX, ALU.add))
                dve.tensor_copy(slot[:, n, :], slot_f[:, n, :]).then_inc(slot_done, 1)

            def shared(b, j):
                n = TPB * b + j
                for s in range(SHARED):
                    dve.wait_ge(s_silu_done, 2 * n + s + 1)
                    if 2 * n + s - 1 > 0:
                        dve.wait_ge(s_turn_done, 2 * n + s - 1)
                    dve.tensor_tensor(s_act[:, s, :], bank[6 + s][:, INNER:GU], s_gate[:, s, :], ALU.mult).then_inc(s_act_done, 1)
                dve.wait_ge(s_down_done, n + 1)
                dve.wait_ge(x2_stored[n], 16)
                dve.tensor_tensor(rows[:, n, :], bank[6][:, 0:D], rows[:, n, :], ALU.add).then_inc(s_sum_done, 1)

            def plan(b, i):
                step = [0]

                def then(ins):
                    step[0] += 1
                    ins.then_inc(plan_step, 1)
                    dve.wait_ge(plan_step, step[0])

                dve.wait_ge(count_done, 1)
                dve.tensor_copy(count[:, :], bank[7][:, 0:EXPERTS]).then_inc(count_kept, 1)
                dve.wait_ge(count_kept, 1)
                then(dve.tensor_tensor(full[:, :, :], count[:, :].unsqueeze(2).broadcast_to([P, EXPERTS, TILES]),
                                       tile_starts[:, :].unsqueeze(1).broadcast_to([P, EXPERTS, TILES]), ALU.is_gt))
                then(dve.tensor_reduce(tiles_of[:, :], full[:, :, :], AX, ALU.add))
                then(dve.tensor_tensor(prior[:, :, :], before[:, :, :],
                                       tiles_of[:, :].unsqueeze(1).broadcast_to([P, EXPERTS, EXPERTS]), ALU.mult))
                then(dve.tensor_reduce(base[:, :], prior[:, :, :], AX, ALU.add))
                wide = [P, SLOT_TILES, EXPERTS]
                then(dve.tensor_tensor(begun[:, :, :], slot_iota[:, :].unsqueeze(2).broadcast_to(wide),
                                       base[:, :].unsqueeze(1).broadcast_to(wide), ALU.is_ge))
                then(dve.tensor_reduce(t_expert[:, :], begun[:, :, :], AX, ALU.add))
                then(dve.tensor_tensor(begun[:, :, :], begun[:, :, :], base[:, :].unsqueeze(1).broadcast_to(wide),
                                       ALU.mult))
                then(dve.tensor_reduce(t_first[:, :], begun[:, :, :], AX, ALU.max))
                then(dve.tensor_tensor(t_within[:, :], slot_iota[:, :], t_first[:, :], ALU.subtract))
                then(dve.tensor_scalar(t_expert[:, :], t_expert[:, :], -1.0, None, ALU.add))
                then(dve.tensor_scalar(t_within[:, :], t_within[:, :], float(TILES - 1), None, ALU.min))
                then(dve.scalar_tensor_tensor(out=t_row[:, :], in0=t_expert[:, :], scalar=float(TILES),
                                              in1=t_within[:, :], op0=ALU.mult, op1=ALU.add))
                dve.tensor_copy(tile_block[:, :], t_row[:, :]).then_inc(plan_done, 1)
                dve.tensor_copy(tile_expert[:, :], t_expert[:, :]).then_inc(plan_done, 1)
                all_k = [P, TILES * TOPK, EXPERTS]
                then(dve.scalar_tensor_tensor(out=shift[:, :], in0=base[:, :], scalar=float(P), in1=region[:, :],
                                              op0=ALU.mult, op1=ALU.subtract))
                dve.tensor_copy(top_f[:, :, :], top_i[:, :, 0:TOPK]).then_inc(y_slot_step, 1)
                dve.wait_ge(y_slot_step, 1)
                dve.tensor_tensor(onehots[:, :, :], iota16[:, :].unsqueeze(1).broadcast_to(all_k),
                                      top_f[:, :, :].rearrange("p n k -> p (n k)").unsqueeze(2).broadcast_to(all_k),
                                      ALU.is_equal).then_inc(y_slot_step, 1)
                dve.wait_ge(y_slot_step, 2)
                dve.tensor_tensor(onehots[:, :, :], onehots[:, :, :], shift[:, :].unsqueeze(1).broadcast_to(all_k),
                                      ALU.mult).then_inc(y_slot_step, 1)
                dve.wait_ge(y_slot_step, 3)
                dve.tensor_reduce(top_f[:, :, :].rearrange("p n k -> p (n k)"), onehots[:, :, :], AX, ALU.add).then_inc(y_slot_step, 1)
                dve.wait_ge(y_slot_step, 4)
                dve.tensor_tensor(top_f[:, :, :], top_f[:, :, :], slot_f[:, :, :], ALU.add).then_inc(y_slot_step, 1)
                dve.wait_ge(y_slot_step, 5)
                dve.tensor_copy(y_slot[:, :, :], top_f[:, :, :]).then_inc(y_slot_done, 1)
                best = top[:, :, 0:1]
                dve.tensor_tensor(shifted[:, :, :], logits[:, :, :], best.broadcast_to([P, TILES, EXPERTS]),
                                      ALU.subtract).then_inc(soft_shift, 1)
                dve.tensor_tensor(soft_top[:, :, :], top[:, :, 0:TOPK], best.broadcast_to([P, TILES, TOPK]),
                                      ALU.subtract).then_inc(soft_shift, 1)
                dve.wait_ge(soft_exp, 2)
                dve.tensor_reduce(soft_sum[:, :], shifted[:, :, :], AX, ALU.add).then_inc(soft_step, 1)
                dve.wait_ge(soft_step, 1)
                dve.reciprocal(soft_inv[:, :], soft_sum[:, :]).then_inc(soft_step, 1)
                dve.wait_ge(soft_step, 2)
                dve.tensor_tensor(weight[:, :, :], soft_top[:, :, :],
                                      soft_inv[:, :].unsqueeze(2).broadcast_to([P, TILES, TOPK]), ALU.mult).then_inc(weight_done, 1)

            def e_x(b, s):
                dve.wait_ge(e_silu_done, s + 1)
                if s - 1 > 0:
                    dve.wait_ge(e_aturn_done, s - 1)
                dve.tensor_tensor(e_act[:, s % 2, :], bank[2 + s % 2][:, INNER:GU], e_gate[:, s % 2, :], ALU.mult).then_inc(e_act_done, 1)

            def e_y(b, s):
                dve.wait_ge(e_aturn_done, s + 1)
                if s - 1 > 0:
                    dve.wait_ge(e_down_done, s - 1)
                dve.tensor_copy(e_act_t[:, s % 2],
                                    bank[4 + s % 2][0:HALF, 0:2 * P].rearrange("p (c t) -> p c t", c=2)).then_inc(e_actt_done, 1)

            def combine(b, n):
                if n == 0:
                    dve.wait_ge(weight_done, 1)
                j = n % 2
                dve.wait_ge(back_in[j], 16 * TOPK * (n // 2 + 1))
                dve.wait_ge(s_sum_done, n + 1)
                for k in range(TOPK):
                    if TOPK * n + k > 0:
                        dve.wait_ge(sum_step, TOPK * n + k)
                    dve.scalar_tensor_tensor(out=rows[:, n, :], in0=back[:, j, k, :], scalar=weight[:, n, k:k + 1],
                                                 in1=rows[:, n, :], op0=ALU.mult, op1=ALU.add).then_inc(sum_step, 1)
                dve.wait_ge(sum_step, TOPK * (n + 1))
                stats_of(r3_stat, r3_mom, j, n, rows[:, n, :])
                if n >= 2:
                    dve.wait_ge(fin_stored[j], 16 * (n // 2))
                normed(r3_rstd, j, n, fin[:, j, :], rows[:, n, :], fin_done)

            masks()
            run({"norm": norm, "qproj": q_rope, "scores": maxima, "turn": probs_lo, "values": head_out,
                 "oproj": oproj, "x1": x1_norm, "up": up, "down": down, "x2": x2_norm, "route": route,
                 "shared": shared, "plan": plan, "e_x": e_x, "e_y": e_y, "combine": combine})


def kernel(**inputs):
    import numpy as np
    import concourse.bacc as bacc
    from concourse.bass_utils import run_bass_kernel_spmd

    a = {k: np.asarray(v) for k, v in inputs.items()}
    qb = a["L0_attn_q_b_w"].reshape(HEADS, QHD, QR)
    inv = np.float32(1.0) / np.float32(10000.0) ** (np.arange(0, ROPE, 2, dtype=np.float32) / np.float32(ROPE))
    freqs = np.outer(np.arange(SEQ, dtype=np.float32), inv.astype(np.float32)).astype(np.float32)
    cos = np.concatenate([np.cos(freqs), np.cos(freqs)], 1)
    sin = np.concatenate([-np.sin(freqs), np.sin(freqs)], 1)
    sg, su = a["L0_ffn_sg"], a["L0_ffn_su"]
    gate_up = np.concatenate([a["L0_ffn_wg"], a["L0_ffn_wu"]], 2)
    halves = [np.concatenate([sg[:, h * INNER:(h + 1) * INNER], su[:, h * INNER:(h + 1) * INNER]], 1)
              for h in range(SHARED)]
    laid = {
        "xT": a["x"].reshape(TOKENS, D).T,
        "x": a["x"].reshape(TOKENS, D),
        "ids": a["itok_BxS_13_99985"].reshape(TILES, P).T,
        "wqkvT": np.concatenate([a["L0_attn_q_a_w"], a["L0_attn_kv_a_w"]], 0).T,
        "qlnw": a["L0_attn_q_a_ln_w"],
        "kvlnw": a["L0_attn_kv_a_ln_w"],
        "qnope": qb[:, 0:NOPE, :],
        "qpeT": qb[:, NOPE:QHD, :].transpose(2, 0, 1),
        "kvb": a["L0_attn_kv_b_w"],
        "woT": a["L0_attn_o_w"].T,
        "cosT": cos,
        "sinT": sin,
        "ctxT": a["ctx_2048"].transpose(2, 0, 1).reshape(D, CTX * D),
        "wgateT": a["L0_ffn_w_gate"].T,
        "wgu": np.concatenate([gate_up, np.stack(halves)], 0).transpose(1, 0, 2),
        "wd": np.concatenate([a["L0_ffn_wd"], a["L0_ffn_sd"].reshape(SHARED, INNER, D)], 0),
    }
    nc = bacc.Bacc("TRN2", target_bir_lowering=False, num_devices=1)
    arrays, aps = {}, {}
    for name, v in laid.items():
        v = np.ascontiguousarray(v)
        arrays[f"in_{name}"] = v
        aps[name] = nc.dram_tensor(f"in_{name}", v.shape, mybir.dt.from_np(v.dtype), kind="ExternalInput").ap()
    aps["out"] = nc.dram_tensor("out_0", (TOKENS, D), F32, kind="ExternalOutput").ap()
    decoder_layer(nc, **aps)
    r = run_bass_kernel_spmd(nc, [arrays], core_ids=[0])
    return r.results[0]["out_0"].reshape(BATCH, SEQ, D)
```

```python
from contextlib import ExitStack

import concourse.bass as bass
from concourse import mybir

ALU = mybir.AluOpType
ACT = mybir.ActivationFunctionType
AX = mybir.AxisListType.X
F32 = mybir.dt.float32
F16 = mybir.dt.float16
BF16 = mybir.dt.bfloat16
I32 = mybir.dt.int32
U32 = mybir.dt.uint32

P = 128
BATCH, SEQ, D = 4, 256, 256
TOKENS = BATCH * SEQ
TILES = TOKENS // P
TPB = SEQ // P
DC = D // P
HEADS, NOPE, ROPE, VD = 16, 128, 64, 128
QHD = NOPE + ROPE
SCALE = float(QHD) ** -0.5
QR, KR = 192, 64
QC = QR // 2
HD = KR + ROPE
QG = 4
GROUPS = HEADS // QG
CTX = 4
CTX_STEP = 12500 // CTX
EXPERTS, TOPK, INNER = 16, 4, 176
HALF = INNER // 2
SHARED = 2
GU = 2 * INNER
RMS_EPS, LN_EPS = 1e-6, 1e-5
MASKED = -1e30
SLOT_TILES = (TOKENS * TOPK + EXPERTS * (P - 1)) // P


def decoder_layer(nc, xT, x, ids, wqkvT, qlnw, kvlnw, qnope, qpeT, kvb, woT, cosT, sinT, ctxT,
                  wgateT, wgu, wd, out):
    x2_dram = nc.dram_tensor("x2_dram", (TOKENS, D), F32, kind="Internal").ap()
    table = nc.dram_tensor("table", (EXPERTS * TOKENS, 1), U32, kind="Internal").ap()
    y_dram = nc.dram_tensor("y_dram", (SLOT_TILES * P, D), F32, kind="Internal").ap()

    with ExitStack() as ctx:
        def sb(name, shape, dt=F32):
            return ctx.enter_context(nc.sbuf_tensor(name, shape, dt))

        def sem(name):
            return ctx.enter_context(nc.semaphore(name))

        bank = [ctx.enter_context(nc.psum_tensor(f"bank{i}", [P, 512], F32)) for i in range(8)]

        ident = sb("ident", [P, P])
        ident16 = sb("ident16", [P, P], BF16)
        causal = sb("causal", [P, P], BF16)
        earlier = sb("earlier", [P, P], BF16)
        ones = sb("ones", [P, P], BF16)
        iota16 = sb("iota16", [P, EXPERTS])
        region = sb("region", [P, EXPERTS])
        before = sb("before", [P, EXPERTS, EXPERTS])
        tile_starts = sb("tile_starts", [P, TILES])
        slot_iota = sb("slot_iota", [P, SLOT_TILES])
        token_id = sb("token_id", [P, TILES], U32)
        cos = sb("cos", [P, TPB, ROPE])
        sin = sb("sin", [P, TPB, ROPE])
        w_qkv = sb("w_qkv", [P, DC, QR + KR + ROPE])
        w_qn = sb("w_qn", [P, QR])
        w_kn = sb("w_kn", [P, KR])
        w_q = sb("w_q", [QC, 2, HEADS, HD])
        w_out = sb("w_out", [P, HEADS // 2, D])
        w_ctx = sb("w_ctx", [P, DC, CTX * D])
        w_gate = sb("w_gate", [P, DC, EXPERTS])
        w_gu = sb("w_gu", [P, DC, EXPERTS + SHARED, GU])
        area = sb("area", [P, (EXPERTS + SHARED) * 2 * D])
        w_down = area[0:HALF, :].rearrange("p (e c d) -> p e c d", e=EXPERTS + SHARED, c=2)
        raw_q = area[:, 0:HEADS * QR].rearrange("p (h r) -> p h r", h=HEADS)
        raw_kv = area[:, HEADS * QR:HEADS * (QR + 2 * KR)].rearrange("p (h t r) -> p h t r", h=HEADS, t=2)
        raw_o = area[:, HEADS * (QR + 2 * KR):HEADS * (QR + 2 * KR + D)].rearrange("p (h d) -> p h d", h=HEADS)
        x_t = sb("x_t", [P, DC, SEQ])
        rows = sb("rows", [P, TILES, D])
        ssq = sb("ssq", [P, 2 * TPB])
        ssq_eps = sb("ssq_eps", [P, 2 * TPB])
        minus_half = sb("minus_half", [P, 2 * TPB])
        rms = sb("rms", [P, 2 * TPB])
        qn = sb("qn", [P, TPB, QR])
        kv_row = sb("kv_row", [P, TPB, HD])
        v_hi = sb("v_hi", [P, TPB, KR + 2], F16)
        v_lo = sb("v_lo", [P, TPB, KR + 2], F16)
        qn_t = sb("qn_t", [QC, 2, SEQ])
        k_t = sb("k_t", [P, SEQ])
        q_row_mem = sb("q_row_mem", [P, TPB * HEADS * HD])
        q_t_mem = sb("q_t_mem", [P, HEADS * SEQ])
        o_row_mem = sb("o_row_mem", [P, TPB * HEADS * KR])
        probs_mem = sb("probs_mem", [P, 3 * 3 * P])

        def carve(mem, parts):
            at, views = 0, []
            for width, pattern, sizes in parts:
                views.append(mem[:, at:at + width].rearrange(pattern, **sizes))
                at += width
            return views

        q_row, = carve(q_row_mem, [(TPB * HEADS * HD, "p (j h d) -> p j h d", dict(j=TPB, h=HEADS))])
        act_junk, k_cos, k_sin = carve(q_row_mem, [
            (TPB * (QR + KR), "p (j r) -> p j r", dict(j=TPB)), (TPB * ROPE, "p (j r) -> p j r", dict(j=TPB)),
            (TPB * ROPE, "p (j r) -> p j r", dict(j=TPB))])
        q_t, = carve(q_t_mem, [(HEADS * SEQ, "p (h t) -> p h t", dict(h=HEADS))])
        o_row, = carve(o_row_mem, [(TPB * HEADS * KR, "p (j o) -> p j o", dict(j=TPB))])
        probs, = carve(probs_mem, [(9 * P, "p (r k) -> p r k", dict(r=3))])
        o_t, = carve(probs_mem, [(HEADS // 2 * P, "p (c t) -> p c t", dict(c=HEADS // 2))])
        pair = "p (r d) -> p r d", dict(r=2)
        picked, gated, a_row, s_act_t = carve(o_row_mem, [(2 * D, *pair)] * 3 + [
            (4 * P, "p (s c t) -> p s c t", dict(s=2, c=2))])
        s_act_t = s_act_t[0:HALF]
        XR, YR, IR = 5, 3, 8
        back, fin, s_gate, s_act, begun = carve(q_row_mem, [
            (2 * TOPK * D, "p (r k d) -> p r k d", dict(r=2, k=TOPK)), (2 * D, *pair),
            (2 * INNER, *pair), (2 * INNER, *pair),
            (SLOT_TILES * EXPERTS, "p (s e) -> p s e", dict(s=SLOT_TILES))])
        onehots, = carve(q_row_mem, [(TILES * TOPK * EXPERTS, "p (n e) -> p n e", dict(e=EXPERTS))])
        xs, e_xt, e_gate, e_act, e_act_t, ys, s_xt = carve(q_t_mem, [
            (XR * D, "p (r d) -> p r d", dict(r=XR)), (4 * P, "p (r c t) -> p r c t", dict(r=2, c=2)),
            (2 * INNER, *pair), (2 * INNER, *pair), (4 * P, "p (r c t) -> p r c t", dict(r=2, c=2)),
            (YR * D, "p (r d) -> p r d", dict(r=YR)), (DC * P, "p (c t) -> p c t", dict(c=DC))])
        e_act_t = e_act_t[0:HALF]
        q_cos = sb("q_cos", [P, 2, QG, ROPE])
        q_sin = sb("q_sin", [P, 2, QG, ROPE])
        neg_max = sb("neg_max", [P, 3, TPB])
        p_hi = sb("p_hi", [P, 3, 3 * P], F16)
        p_lo = sb("p_lo", [P, 3, 3 * P], F16)
        inv_sum = sb("inv_sum", [P, 2, 2 * TPB])
        res = sb("res", [P, TPB, D])
        turned = sb("turned", [P, TPB, DC, P])
        stats = sb("stats", [P, TPB, 6])
        moments = sb("moments", [P, TPB, 2])
        var_eps = sb("var_eps", [P, TPB, 1])
        rstd = sb("rstd", [P, TPB, 1])
        ids_i = sb("ids_i", [P, TILES], I32)
        ids_f = sb("ids_f", [P, TILES])
        above = sb("above", [P, TILES])
        picks = sb("picks", [P, TILES, CTX])
        logits = sb("logits", [P, TILES, EXPERTS])
        top = sb("top", [P, TILES, 8])
        top_i = sb("top_i", [P, TILES, 8], U32)
        top_f = sb("top_f", [P, TILES, TOPK])
        onehot = sb("onehot", [P, 2, TOPK, EXPERTS])
        chosen = sb("chosen", [P, TILES, EXPERTS], BF16)
        seen = sb("seen", [P, TILES + 1, EXPERTS], BF16)
        place = sb("place", [P, TILES, EXPERTS])
        placed = sb("placed", [P, 2, TOPK, EXPERTS])
        slot_f = sb("slot_f", [P, TILES, TOPK])
        slot = sb("slot", [P, TILES, TOPK], U32)
        count = sb("count", [P, EXPERTS])
        full = sb("full", [P, EXPERTS, TILES])
        tiles_of = sb("tiles_of", [P, EXPERTS])
        prior = sb("prior", [P, EXPERTS, EXPERTS])
        base = sb("base", [P, EXPERTS])
        t_expert = sb("t_expert", [P, SLOT_TILES])
        t_first = sb("t_first", [P, SLOT_TILES])
        t_within = sb("t_within", [P, SLOT_TILES])
        t_row = sb("t_row", [P, SLOT_TILES])
        tile_expert = sb("tile_expert", [P, SLOT_TILES], I32)
        shift = sb("shift", [P, EXPERTS])
        y_slot = sb("y_slot", [P, TILES, TOPK], U32)
        tile_block = sb("tile_block", [P, SLOT_TILES], I32)
        shifted = sb("shifted", [P, TILES, EXPERTS])
        soft_sum = sb("soft_sum", [P, TILES])
        soft_inv = sb("soft_inv", [P, TILES])
        soft_top = sb("soft_top", [P, TILES, TOPK])
        weight = sb("weight", [P, TILES, TOPK])

        zero_table = full[:, :, :].rearrange("p e n -> p (e n)").bitcast(U32)
        idx = sb("idx", [P, IR, 1], U32)

        in_xt = sem("in_xt")
        in_wqkv = sem("in_wqkv")
        in_norms = sem("in_norms")
        in_rope = sem("in_rope")
        in_rawq = sem("in_rawq")
        in_rawkv = sem("in_rawkv")
        in_wpe = sem("in_wpe")
        in_rawo = sem("in_rawo")
        in_x = sem("in_x")
        in_ids = sem("in_ids")
        in_wctx = sem("in_wctx")
        in_wgate = sem("in_wgate")
        in_wshared = sem("in_wshared")
        in_wgu = sem("in_wgu")
        in_wdown = sem("in_wdown")
        table_zeroed = sem("table_zeroed")
        const_made = sem("const_made")
        eye_made = sem("eye_made")
        norms_scaled = sem("norms_scaled")
        qkv_done = sem("qkv_done")
        ssq_done = sem("ssq_done")
        rms_eps_done = sem("rms_eps_done")
        rms_done = sem("rms_done")
        qn_done = sem("qn_done")
        kvc_done = sem("kvc_done")
        krope_done = sem("krope_done")
        kv_done = sem("kv_done")
        vhi_done = sem("vhi_done")
        vlo_done = sem("vlo_done")
        fturn_done = sem("fturn_done")
        fevac_done = sem("fevac_done")
        qproj_done = sem("qproj_done")
        qrope_done = sem("qrope_done")
        abs_done = sem("abs_done")
        qrow_done = sem("qrow_done")
        qturn_done = sem("qturn_done")
        qt_done = sem("qt_done")
        absorbed_q = sem("absorbed_q")
        absorbed_q_kept = sem("absorbed_q_kept")
        absorbed_o = sem("absorbed_o")
        absorbed_o_kept = sem("absorbed_o_kept")
        scores_done = sem("scores_done")
        max_done = sem("max_done")
        exp_done = sem("exp_done")
        pturn_done = sem("pturn_done")
        phi_done = sem("phi_done")
        plo_done = sem("plo_done")
        pv_done = sem("pv_done")
        inv_done = sem("inv_done")
        onorm_done = sem("onorm_done")
        oturn_done = sem("oturn_done")
        ot_done = sem("ot_done")
        oproj_done = sem("oproj_done")
        r1_done = sem("r1_done")
        r1_stat = sem("r1_stat")
        r1_mom = sem("r1_mom")
        r1_eps = sem("r1_eps")
        r1_rstd = sem("r1_rstd")
        x1_done = sem("x1_done")
        x1turn_done = sem("x1turn_done")
        x1t_done = sem("x1t_done")
        up_done = sem("up_done")
        pick_step = sem("pick_step")
        silu_done = sem("silu_done")
        a_done = sem("a_done")
        aturn_done = sem("aturn_done")
        at_done = sem("at_done")
        down_done = sem("down_done")
        sel_step = sem("sel_step")
        r2_stat = sem("r2_stat")
        r2_mom = sem("r2_mom")
        r2_eps = sem("r2_eps")
        r2_rstd = sem("r2_rstd")
        x2_done = sem("x2_done")
        x2turn_done = sem("x2turn_done")
        x2t_done = sem("x2t_done")
        gate_done = sem("gate_done")
        logits_done = sem("logits_done")
        masks_step = sem("masks_step")
        route_step = sem("route_step")
        chosen_done = sem("chosen_done")
        seen_done = sem("seen_done")
        rank_done = sem("rank_done")
        place_done = sem("place_done")
        placed_done = sem("placed_done")
        slotf_done = sem("slotf_done")
        slot_done = sem("slot_done")
        scattered = sem("scattered")
        s_xturn_done = sem("s_xturn_done")
        s_xt_done = sem("s_xt_done")
        s_gu_done = sem("s_gu_done")
        s_silu_done = sem("s_silu_done")
        s_act_done = sem("s_act_done")
        s_turn_done = sem("s_turn_done")
        s_actt_done = sem("s_actt_done")
        s_down_done = sem("s_down_done")
        s_sum_done = sem("s_sum_done")
        count_done = sem("count_done")
        count_kept = sem("count_kept")
        plan_step = sem("plan_step")
        plan_done = sem("plan_done")
        y_slot_step = sem("y_slot_step")
        y_slot_done = sem("y_slot_done")
        soft_step = sem("soft_step")
        soft_shift = sem("soft_shift")
        soft_exp = sem("soft_exp")
        weight_done = sem("weight_done")
        e_turn_done = sem("e_turn_done")
        e_xt_done = sem("e_xt_done")
        e_gu_done = sem("e_gu_done")
        e_silu_done = sem("e_silu_done")
        e_act_done = sem("e_act_done")
        e_aturn_done = sem("e_aturn_done")
        e_actt_done = sem("e_actt_done")
        e_down_done = sem("e_down_done")
        e_y_done = sem("e_y_done")
        sum_step = sem("sum_step")
        r3_stat = sem("r3_stat")
        r3_mom = sem("r3_mom")
        r3_eps = sem("r3_eps")
        r3_rstd = sem("r3_rstd")
        fin_done = sem("fin_done")
        x2_stored = [sem(f"x2_stored{n}") for n in range(TILES)]
        idx_in = [sem(f"idx_in{r}") for r in range(IR)]
        xs_in = [sem(f"xs_in{r}") for r in range(XR)]
        y_stored = [sem(f"y_stored{r}") for r in range(YR)]
        back_in = [sem(f"back_in{r}") for r in range(2)]
        fin_stored = [sem(f"fin_stored{r}") for r in range(2)]

        def core_order(b, tail=()):
            for h in range(HEADS + 6):
                for behind, step in enumerate(("scores", "exp", None, "turn", "low", "values", "out")):
                    if step and 0 <= h - behind < HEADS:
                        yield step, b, h - behind
                yield from (step for at, step in tail if at == h)

        def front_tail(b):
            return [(HEADS + 1, ("qkv", b, 0)), (HEADS + 1, ("qkv", b, 1)),
                    (HEADS + 4, ("norm", b, 0)), (HEADS + 4, ("norm", b, 1))]

        def qproj_order(b):
            groups = [(j, g) for j in range(TPB) for g in range(GROUPS)]
            return [("qproj", b, jg) for jg in groups], [("qturn", b, jg) for jg in groups]

        def back_and_front(b):
            q, t = qproj_order(b + 1)
            yield from (("oturn", b, (0, 0)), ("oturn", b, (0, 1)), ("fturn", b + 1, 0), ("oproj", b, 0),
                        ("oturn", b, (1, 0)), ("oturn", b, (1, 1)), ("fturn", b + 1, 1), q[0], ("oproj", b, 1),
                        ("x1", b, 0), q[1], ("x1turn", b, 0), ("x1", b, 1), t[0], ("up", b, 0), ("x1turn", b, 1),
                        q[2], ("act", b, 0), t[1], ("up", b, 1), q[3], ("aturn", b, 0), ("act", b, 1), t[2],
                        ("down", b, 0), ("aturn", b, 1), q[4], t[3], ("down", b, 1), q[5], ("x2", b, 0), t[4],
                        ("x2turn", b, 0), ("x2", b, 1), q[6], ("gate", b, 0), ("x2turn", b, 1), t[5],
                        ("gate", b, 1), q[7], ("rank", b, 0), t[6], ("rank", b, 1), t[7])

        def back_alone(b):
            yield from (("oturn", b, (0, 0)), ("oturn", b, (0, 1)), ("oproj", b, 0),
                        ("oturn", b, (1, 0)), ("oturn", b, (1, 1)), ("oproj", b, 1),
                        ("x1", b, 0), ("x1turn", b, 0), ("up", b, 0), ("x1", b, 1), ("x1turn", b, 1),
                        ("act", b, 0), ("up", b, 1), ("aturn", b, 0), ("act", b, 1), ("down", b, 0),
                        ("aturn", b, 1), ("down", b, 1), ("x2", b, 0), ("x2turn", b, 0), ("gate", b, 0),
                        ("x2", b, 1), ("x2turn", b, 1), ("gate", b, 1), ("rank", b, 0), ("rank", b, 1))

        def shared_order(b):
            for j in range(TPB):
                yield "shared", b, j

        def weave(long, short):
            long, short = list(long), list(short)
            done = 0
            for i, step in enumerate(long):
                yield step
                upto = (i + 1) * len(short) // len(long)
                yield from short[done:upto]
                done = upto

        def order():
            yield from ((step, 0, j) for step in ("qkv", "norm", "fturn") for j in range(TPB))
            yield "absorb", 0, 0
            q, t = qproj_order(0)
            yield from (step for i in range(len(q) + 2) for step in q[i:i + 1] + t[i - 2:i - 1] if i >= 2 or step in q)
            for b in range(BATCH):
                if b + 1 < BATCH:
                    yield from core_order(b, front_tail(b + 1))
                    yield from back_and_front(b)
                else:
                    yield from core_order(b)
                    yield from back_alone(b)
            yield "plan", 0, 0
            for b in range(SHARED_EARLY):
                yield from shared_order(b)
            for s in range(SLOT_TILES + 3):
                for behind, stage in enumerate(("e_turn", "e_gate_up", "e_act_turn", "e_down")):
                    if 0 <= s - behind < SLOT_TILES:
                        yield stage, 0, s - behind
            late = [step for b in range(SHARED_EARLY, BATCH) for step in shared_order(b)]
            yield from weave([("combine", 0, n) for n in range(len(late))], late)
            for n in range(len(late), TILES):
                yield "combine", 0, n

        SHARED_EARLY = 2
        IDX_AHEAD, X_AHEAD = 7, 4
        ORDER = list(order())

        def run(steps):
            for name, b, i in ORDER:
                if name in steps:
                    steps[name](b, i)

        block = ctx.enter_context(nc.Block())

        @block.sync
        def _(sp):
            xt_v = xT.rearrange("(c p) t -> p c t", p=P)
            sp.dma_start(x_t[:, :, :], xt_v[:, :, 0:SEQ]).then_inc(in_xt, 16)
            sp.dma_start(w_qkv[:, :, :], wqkvT.rearrange("(c p) n -> p c n", p=P)).then_inc(in_wqkv, 16)
            sp.dma_start(w_qn[:, :], qlnw.partition_broadcast(P)).then_inc(in_norms, 16)
            sp.dma_start(w_kn[:, :], kvlnw.partition_broadcast(P)).then_inc(in_norms, 16)
            sp.dma_start(raw_kv, kvb.rearrange("(h t p) r -> p h t r", h=HEADS, t=2)).then_inc(in_rawkv, 16)
            sp.dma_start(raw_q, qnope.rearrange("h p r -> p h r")).then_inc(in_rawq, 16)
            sp.dma_start(cos[:, :, :], cosT.rearrange("(j p) r -> p j r", p=P)).then_inc(in_rope, 16)
            sp.dma_start(sin[:, :, :], sinT.rearrange("(j p) r -> p j r", p=P)).then_inc(in_rope, 16)
            qpe_v = qpeT.rearrange("(c p) h r -> p c h r", p=QC)
            for c in range(2):
                sp.dma_start(w_q[:, c, :, KR:HD], qpe_v[:, c]).then_inc(in_wpe, 16)
            sp.dma_start(raw_o, woT.rearrange("(h p) d -> p h d", p=P)).then_inc(in_rawo, 16)
            sp.dma_start(rows[:, :, :], x.rearrange("(n p) d -> p n d", p=P)).then_inc(in_x, 16)
            sp.dma_start(ids_i[:, :], ids).then_inc(in_ids, 16)
            sp.dma_start(w_ctx[:, :, :], ctxT.rearrange("(c p) n -> p c n", p=P)).then_inc(in_wctx, 16)
            sp.dma_start(w_gate[:, :, :], wgateT.rearrange("(c p) n -> p c n", p=P)).then_inc(in_wgate, 16)
            sp.wait_ge(const_made, 1)
            sp.dma_start(table.rearrange("(p n) o -> p (n o)", p=P), zero_table[:, :]).then_inc(table_zeroed, 16)
            sp.dma_start(w_gu[:, :, :, :], wgu.rearrange("(c p) e n -> p c e n", p=P)).then_inc(in_wgu, 16)
            sp.wait_ge(absorbed_o, 1)
            sp.dma_start(w_down, wd.rearrange("e (c p) d -> p e c d", p=HALF)).then_inc(in_wdown, 16)

            def next_x(b, h):
                if h == 0 and b + 1 < BATCH:
                    sp.wait_ge(qkv_done, TPB * (b + 1))
                    sp.dma_start(x_t[:, :, :], xt_v[:, :, (b + 1) * SEQ:(b + 2) * SEQ]).then_inc(in_xt, 16)

            def x2_store(b, j):
                n = TPB * b + j
                sp.wait_ge(x2_done, n + 1)
                sp.dma_start(x2_dram[n * P:(n + 1) * P, :], rows[:, n, :]).then_inc(x2_stored[n], 16)

            def plan(b, i):
                sp.wait_ge(plan_done, 2)
                sp.wait_ge(scattered, 16 * TILES * TOPK)
                for s in range(IDX_AHEAD):
                    idx_load(s)

            def idx_load(s):
                if s >= SLOT_TILES:
                    return
                if s >= IR:
                    used = s - IR
                    sp.wait_ge(xs_in[used % XR], 16 * (used // XR + 1))
                block_no = sp.value_load(tile_block[0:1, s:s + 1], min_val=0, max_val=EXPERTS * TILES - 1)
                sp.dma_start(idx[:, s % IR, :], table[bass.ds(block_no * P, P), :]).then_inc(idx_in[s % IR], 16)

            def e_turn(b, s):
                idx_load(s + IDX_AHEAD)

            def e_down(b, s):
                sp.wait_ge(e_y_done, s + 1)
                sp.dma_start(y_dram[s * P:(s + 1) * P, :], ys[:, s % YR, :]).then_inc(y_stored[s % YR], 16)

            def combine(b, n):
                sp.wait_ge(fin_done, n + 1)
                sp.dma_start(out[n * P:(n + 1) * P, :], fin[:, n % 2, :]).then_inc(fin_stored[n % 2], 16)

            run({"scores": next_x, "x2": x2_store, "plan": plan, "e_turn": e_turn, "e_down": e_down,
                 "combine": combine})
            for r in range(2):
                sp.wait_ge(fin_stored[r], 16 * TILES // 2)

        @block.gpsimd
        def _(pool):
            pool.memset(zero_table[:, :], 0).then_inc(const_made, 1)
            pool.memset(ident[:, :], 0.0).then_inc(eye_made, 1)
            pool.wait_ge(eye_made, 1)
            pool.affine_select(out=ident[:, :], in_=ident[:, :], compare_op=ALU.not_equal, fill=1.0,
                               base=0, pattern=[[-1, P]], channel_multiplier=1).then_inc(eye_made, 1)
            pool.wait_ge(eye_made, 2)
            pool.tensor_copy(ident16[:, :], ident[:, :]).then_inc(eye_made, 1)
            pool.memset(causal[:, :], 0.0).then_inc(eye_made, 1)
            pool.memset(ones[:, :], 1.0).then_inc(eye_made, 1)
            pool.memset(minus_half[:, :], -0.5).then_inc(eye_made, 1)
            pool.wait_ge(eye_made, 6)
            pool.affine_select(out=causal[:, :], in_=causal[:, :], compare_op=ALU.is_ge, fill=MASKED,
                               base=0, pattern=[[-1, P]], channel_multiplier=1).then_inc(eye_made, 1)
            pool.affine_select(out=earlier[:, :], in_=ones[:, :], compare_op=ALU.is_gt, fill=0.0,
                               base=0, pattern=[[1, P]], channel_multiplier=-1).then_inc(eye_made, 1)
            for v, dst in ((1.0, v_hi), (0.0, v_lo)):
                pool.memset(dst[:, :, KR:KR + 2], v).then_inc(eye_made, 1)
            pool.memset(seen[:, 0, :], 0.0).then_inc(eye_made, 1)
            pool.iota(iota16[:, :], pattern=[[1, EXPERTS]], base=0, channel_multiplier=0,
                      allow_small_or_imprecise_dtypes=True).then_inc(eye_made, 1)
            pool.iota(region[:, :], pattern=[[TOKENS, EXPERTS]], base=0, channel_multiplier=0,
                      allow_small_or_imprecise_dtypes=True).then_inc(eye_made, 1)
            pool.iota(tile_starts[:, :], pattern=[[P, TILES]], base=0, channel_multiplier=0,
                      allow_small_or_imprecise_dtypes=True).then_inc(eye_made, 1)
            pool.iota(slot_iota[:, :], pattern=[[1, SLOT_TILES]], base=0, channel_multiplier=0,
                      allow_small_or_imprecise_dtypes=True).then_inc(eye_made, 1)
            pool.iota(token_id[:, :], pattern=[[P, TILES]], base=0, channel_multiplier=1).then_inc(eye_made, 1)
            pool.memset(before[:, :, :], 1.0).then_inc(eye_made, 1)
            pool.wait_ge(eye_made, 17)
            pool.affine_select(out=before[:, :, :], in_=before[:, :, :], compare_op=ALU.is_gt, fill=0.0,
                               base=0, pattern=[[1, EXPERTS], [-1, EXPERTS]],
                               channel_multiplier=0).then_inc(eye_made, 1)

            def rms_of(b, i):
                if i == 0:
                    pool.wait_ge(ssq_done, 4 * (b + 1))
                    if 2 * b > 0:
                        pool.wait_ge(qn_done, 2 * b)
                    if 2 * b > 0:
                        pool.wait_ge(kvc_done, 2 * b)
                    pool.tensor_scalar(ssq_eps[:, :], ssq[:, :], RMS_EPS, None, ALU.add).then_inc(rms_eps_done, 1)
                    pool.wait_ge(rms_eps_done, b + 1)
                    pool.tensor_tensor(rms[:, :], ssq_eps[:, :], minus_half[:, :], ALU.pow).then_inc(rms_done, 1)
                n = TPB * b + i
                pool.wait_ge(kvc_done, n + 1)
                if HEADS * b > 0:
                    pool.wait_ge(pv_done, HEADS * b)
                pool.tensor_copy(v_hi[:, i, 0:KR], kv_row[:, i, 0:KR]).then_inc(vhi_done, 1)
                pool.wait_ge(vhi_done, n + 1)
                pool.tensor_tensor(v_lo[:, i, 0:KR], kv_row[:, i, 0:KR], v_hi[:, i, 0:KR],
                                   ALU.subtract).then_inc(vlo_done, 1)

            def q_rotary(b, jg):
                j, g = jg
                i = GROUPS * (TPB * b + j) + g
                pool.wait_ge(qrope_done, i + 1)
                if i + 1 - TPB * GROUPS > 0:
                    pool.wait_ge(qturn_done, i + 1 - TPB * GROUPS)
                pool.tensor_tensor(q_row[:, j, QG * g:QG * g + QG, KR:HD], q_cos[:, i % 2], q_sin[:, i % 2],
                                   ALU.add).then_inc(qrow_done, 1)

            def rstd_of(mom, eps, inverse, j, n):
                pool.wait_ge(mom, n + 1)
                pool.tensor_scalar(var_eps[:, j, :], moments[:, j, 1:2], LN_EPS, None, ALU.add)\
                    .then_inc(eps, 1)
                pool.wait_ge(eps, n + 1)
                pool.tensor_tensor(rstd[:, j, :], var_eps[:, j, :], minus_half[:, 0:1], ALU.pow)\
                    .then_inc(inverse, 1)

            def route(b, j):
                n = TPB * b + j
                pool.wait_ge(slot_done, n + 1)
                pool.wait_ge(table_zeroed, 16)
                for k in range(TOPK):
                    pool.indirect_dma_start(out=table, out_offset=bass.IndirectOffsetOnAxis(ap=slot[:, n, k:k + 1], axis=0),
                                            in_=token_id[:, n:n + 1], in_offset=None).then_inc(scattered, 16)

            def gather_x(s):
                if s >= SLOT_TILES:
                    return
                if s == 0:
                    for n in range(TILES):
                        pool.wait_ge(x2_stored[n], 16)
                pool.wait_ge(idx_in[s % IR], 16 * (s // IR + 1))
                if s >= XR:
                    pool.wait_ge(e_turn_done, s - XR + 1)
                pool.indirect_dma_start(out=xs[:, s % XR, :], out_offset=None, in_=x2_dram,
                                        in_offset=bass.IndirectOffsetOnAxis(ap=idx[:, s % IR, :], axis=0))\
                    .then_inc(xs_in[s % XR], 16)

            def plan(b, i):
                for s in range(X_AHEAD):
                    gather_x(s)

            def e_turn(b, s):
                gather_x(s + X_AHEAD)

            gathered = [0]

            def combine_gather(n):
                if n >= TILES:
                    return
                if n == 0:
                    for r in range(YR):
                        pool.wait_ge(y_stored[r], 16 * len(range(r, SLOT_TILES, YR)))
                    pool.wait_ge(y_slot_done, 1)
                if TOPK * (n - 1) > 0:
                    pool.wait_ge(sum_step, TOPK * (n - 1))
                for k in range(TOPK):
                    pool.indirect_dma_start(out=back[:, n % 2, k, :], out_offset=None, in_=y_dram,
                                            in_offset=bass.IndirectOffsetOnAxis(ap=y_slot[:, n, k:k + 1], axis=0))\
                        .then_inc(back_in[n % 2], 16)

            def combine(b, n):
                if n == 0:
                    combine_gather(0)
                combine_gather(n + 1)
                rstd_of(r3_mom, r3_eps, r3_rstd, n % 2, n)

            run({"norm": rms_of, "qproj": q_rotary,
                 "oproj": lambda b, j: rstd_of(r1_mom, r1_eps, r1_rstd, j, TPB * b + j),
                 "down": lambda b, j: rstd_of(r2_mom, r2_eps, r2_rstd, j, TPB * b + j),
                 "rank": route, "plan": plan, "e_turn": e_turn, "combine": combine})

        @block.scalar
        def _(act):
            def mean_squares(b, j):
                n = TPB * b + j
                act.wait_ge(qkv_done, n + 1)
                if b > 0:
                    act.wait_ge(rms_eps_done, b)
                for k, (at, w) in enumerate(((0, QR), (QR, KR))):
                    act.activation(act_junk[:, j, at:at + w], bank[j][:, at:at + w], ACT.Square, scale=float(w) ** -0.5,
                                   accum_out=ssq[:, 2 * j + k:2 * j + k + 1]).then_inc(ssq_done, 1)

            def latents_t(b, j):
                n = TPB * b + j
                act.wait_ge(fturn_done, n + 1)
                if TPB * GROUPS * b > 0:
                    act.wait_ge(qproj_done, TPB * GROUPS * b)
                if HEADS * b > 0:
                    act.wait_ge(scores_done, HEADS * b)
                turned = bank[2 + j][0:QC, 0:2 * P].rearrange("p (c t) -> p c t", c=2)
                act.activation(qn_t[:, :, j * P:(j + 1) * P], turned, ACT.Copy).then_inc(fevac_done, 1)
                act.activation(k_t[:, j * P:(j + 1) * P], bank[2 + j][:, 2 * P:3 * P], ACT.Copy).then_inc(fevac_done, 1)

            def absorb(b, i):
                for c in range(2):
                    for half in range(2):
                        act.wait_ge(absorbed_q, 2 * c + half + 1)
                        act.activation(w_q[:, c, 8 * half:8 * half + 8, 0:KR], bank[4 + 2 * c + half][0:QC, :].rearrange("p (h r) -> p h r", h=8), ACT.Copy).then_inc(absorbed_q_kept, 1)
                act.wait_ge(absorbed_o, 1)
                for k in range(4):
                    act.activation(w_out[:, 2 * k:2 * k + 2, :], bank[4 + k][:, :].rearrange("p (h d) -> p h d", h=2), ACT.Copy).then_inc(absorbed_o_kept, 1)

            def q_absorbed(b, jg):
                j, g = jg
                i = GROUPS * (TPB * b + j) + g
                act.wait_ge(qrope_done, i + 1)
                if i + 1 - TPB * GROUPS > 0:
                    act.wait_ge(qturn_done, i + 1 - TPB * GROUPS)
                act.activation(q_row[:, j, QG * g:QG * g + QG, 0:KR], bank[g % 2][:, :].rearrange("p (h d) -> p h d", h=QG)[:, :, 0:KR], ACT.Copy).then_inc(abs_done, 1)

            def q_turned(b, jg):
                j, g = jg
                i = GROUPS * (TPB * b + j) + g
                act.wait_ge(qturn_done, i + 1)
                if HEADS * b > 0:
                    act.wait_ge(scores_done, HEADS * b)
                act.activation(q_t[:, QG * g:QG * g + QG, j * P:(j + 1) * P], bank[2 + g % 2][:, :].rearrange("p (h t) -> p h t", h=QG), ACT.Copy).then_inc(qt_done, 1)

            def exps(b, h):
                n = HEADS * b + h
                act.wait_ge(max_done, 2 * n + 2)
                if n - 2 > 0:
                    act.wait_ge(pturn_done, n - 2)
                if TPB * b > 0:
                    act.wait_ge(oproj_done, 2 * TPB * b)
                for q, (at, w) in enumerate(((0, P), (P, 2 * P))):
                    act.activation(probs[:, n % 3, at:at + w], bank[h % 3][:, at:at + w], ACT.Exp,
                                   bias=neg_max[:, n % 3, q:q + 1]).then_inc(exp_done, 1)

            def probs_hi(b, h):
                n = HEADS * b + h
                act.wait_ge(pturn_done, n + 1)
                if n - 2 > 0:
                    act.wait_ge(pv_done, n - 2)
                act.activation(p_hi[:, n % 3, :], bank[3 + h % 2][:, 0:3 * P], ACT.Copy).then_inc(phi_done, 1)

            def o_turned(b, jh):
                j, half = jh
                n = TPB * b + j
                act.wait_ge(oturn_done, 2 * n + half + 1)
                if n > 0:
                    act.wait_ge(oproj_done, 2 * (n - 1) + half + 1)
                act.activation(o_t[:, 4 * half:4 * half + 4, :], bank[4 + half][:, :].rearrange("p (c t) -> p c t", c=4), ACT.Copy).then_inc(ot_done, 1)

            def turned_back(j, n, turn_done, used, done, used_n):
                act.wait_ge(turn_done, n + 1)
                if used_n > 0:
                    act.wait_ge(used, used_n)
                act.activation(turned[:, j], bank[4 + j][:, 0:D].rearrange("p (c t) -> p c t", c=DC), ACT.Copy)\
                    .then_inc(done, 1)

            def x1_turned(b, j):
                n = TPB * b + j
                turned_back(j, n, x1turn_done, gate_done, x1t_done, n - 1)

            def gate_act(b, j):
                n = TPB * b + j
                act.wait_ge(pick_step, CTX * (n + 1))
                if n - 1 > 0:
                    act.wait_ge(a_done, n - 1)
                act.activation(gated[:, j, :], picked[:, j, :], ACT.Silu).then_inc(silu_done, 1)

            def a_turned(b, j):
                n = TPB * b + j
                turned_back(j, n, aturn_done, up_done, at_done, n + 1)

            def x2_turned(b, j):
                n = TPB * b + j
                turned_back(j, n, x2turn_done, down_done, x2t_done, n + 1)

            def shared(b, j):
                n = TPB * b + j
                act.wait_ge(s_xturn_done, n + 1)
                if 2 * n > 0:
                    act.wait_ge(s_gu_done, 2 * n)
                act.activation(s_xt[:, :, :], bank[4][:, 0:D].rearrange("p (c t) -> p c t", c=DC), ACT.Copy).then_inc(s_xt_done, 1)
                for s in range(SHARED):
                    act.wait_ge(s_gu_done, 2 * n + s + 1)
                    if 2 * n + s - 1 > 0:
                        act.wait_ge(s_act_done, 2 * n + s - 1)
                    act.activation(s_gate[:, s, :], bank[6 + s][:, 0:INNER], ACT.Silu).then_inc(s_silu_done, 1)
                for s in range(SHARED):
                    act.wait_ge(s_turn_done, 2 * n + s + 1)
                    if n > 0:
                        act.wait_ge(s_down_done, n)
                    act.activation(s_act_t[:, s], bank[4 + s][0:HALF, 0:2 * P].rearrange("p (c t) -> p c t", c=2), ACT.Copy).then_inc(s_actt_done, 1)

            def plan(b, i):
                act.wait_ge(soft_shift, 1)
                act.activation(shifted[:, :, :], shifted[:, :, :], ACT.Exp).then_inc(soft_exp, 1)
                act.wait_ge(soft_shift, 2)
                act.activation(soft_top[:, :, :], soft_top[:, :, :], ACT.Exp).then_inc(soft_exp, 1)

            def e_turn(b, s):
                act.wait_ge(e_turn_done, s + 1)
                if s - 1 > 0:
                    act.wait_ge(e_gu_done, s - 1)
                act.activation(e_xt[:, s % 2], bank[s % 2][:, 0:D].rearrange("p (c t) -> p c t", c=DC), ACT.Copy).then_inc(e_xt_done, 1)

            def e_gate_up(b, s):
                act.wait_ge(e_gu_done, s + 1)
                if s - 1 > 0:
                    act.wait_ge(e_act_done, s - 1)
                act.activation(e_gate[:, s % 2, :], bank[2 + s % 2][:, 0:INNER], ACT.Silu).then_inc(e_silu_done, 1)

            def e_down(b, s):
                act.wait_ge(e_down_done, s + 1)
                if s >= YR:
                    act.wait_ge(y_stored[s % YR], 16 * (s // YR))
                act.activation(ys[:, s % YR, :], bank[6 + s % 2][:, 0:D], ACT.Copy).then_inc(e_y_done, 1)

            run({"qkv": mean_squares, "fturn": latents_t, "absorb": absorb, "qproj": q_absorbed, "qturn": q_turned,
                 "exp": exps, "turn": probs_hi, "oturn": o_turned, "x1turn": x1_turned, "act": gate_act,
                 "aturn": a_turned, "x2turn": x2_turned,
                 "shared": shared, "plan": plan, "e_turn": e_turn, "e_gate_up": e_gate_up, "e_down": e_down})

        @block.tensor
        def _(pe):
            def qkv(b, j):
                n = TPB * b + j
                pe.wait_ge(in_xt, 16 * (b + 1))
                if b == 0:
                    pe.wait_ge(in_wqkv, 16)
                if 2 * HEADS * b > 0:
                    pe.wait_ge(exp_done, 2 * HEADS * b)
                for c in range(DC):
                    mm = pe.matmul(bank[j][:, 0:QR + HD], x_t[:, c, j * P:(j + 1) * P], w_qkv[:, c, :],
                                   start=(c == 0), stop=(c == DC - 1))
                mm.then_inc(qkv_done, 1)

            def latents_turn(b, j):
                n = TPB * b + j
                if n == 0:
                    pe.wait_ge(eye_made, 18)
                pe.wait_ge(qn_done, n + 1)
                pe.wait_ge(kv_done, n + 1)
                if HEADS * b > 0:
                    pe.wait_ge(phi_done, HEADS * b)
                if HEADS * b > 0:
                    pe.wait_ge(plo_done, HEADS * b)
                for c in range(2):
                    pe.transpose(bank[2 + j][0:QC, c * P:(c + 1) * P], qn[:, j, c * QC:(c + 1) * QC], ident[:, :])
                pe.transpose(bank[2 + j][:, 2 * P:3 * P], kv_row[:, j, :], ident[:, :]).then_inc(fturn_done, 1)

            def absorb(b, i):
                pe.wait_ge(in_rawq, 16)
                pe.wait_ge(in_rawkv, 16)
                for c in range(2):
                    for half in range(2):
                        for h in range(8):
                            mm = pe.matmul(bank[4 + 2 * c + half][0:QC, h * KR:(h + 1) * KR],
                                           raw_q[:, 8 * half + h, c * QC:(c + 1) * QC], raw_kv[:, 8 * half + h, 0, :],
                                           start=True, stop=True)
                        mm.then_inc(absorbed_q, 1)
                pe.wait_ge(in_rawo, 16)
                pe.wait_ge(absorbed_q_kept, 4)
                for h in range(HEADS):
                    at = KR * (h % 2)
                    mm = pe.matmul(bank[4 + h // 4][at:at + KR, (h // 2 % 2) * D:(h // 2 % 2 + 1) * D],
                                   raw_kv[:, h, 1, :], raw_o[:, h, :], start=True, stop=True)
                mm.then_inc(absorbed_o, 1)

            def qproj(b, jg):
                j, g = jg
                n = TPB * b + j
                i = GROUPS * n + g
                pe.wait_ge(fevac_done, 2 * n + 2)
                if i == 0:
                    pe.wait_ge(absorbed_q_kept, 4)
                    pe.wait_ge(in_wpe, 32)
                if i % (TPB * GROUPS) < 2:
                    pe.wait_ge(krope_done, 3 * (TPB * b + g + 1))
                if i - 1 > 0:
                    pe.wait_ge(abs_done, i - 1)
                for c in range(2):
                    mm = pe.matmul(bank[g % 2][:, :], qn_t[:, c, j * P:(j + 1) * P],
                                   w_q[:, c, QG * g:QG * g + QG, :], start=(c == 0), stop=(c == 1))
                mm.then_inc(qproj_done, 1)

            def qturn(b, jg):
                j, g = jg
                n = TPB * b + j
                i = GROUPS * n + g
                pe.wait_ge(abs_done, i + 1)
                pe.wait_ge(qrow_done, i + 1)
                if i % (TPB * GROUPS) < 2:
                    pe.wait_ge(fevac_done, 2 * (TPB * b + g + 1))
                if i - 1 > 0:
                    pe.wait_ge(qt_done, i - 1)
                for k in range(QG):
                    mm = pe.transpose(bank[2 + g % 2][:, k * P:(k + 1) * P], q_row[:, j, QG * g + k, :], ident[:, :])
                mm.then_inc(qturn_done, 1)

            def scores(b, h):
                n = HEADS * b + h
                s = bank[h % 3]
                if h == 0:
                    pe.wait_ge(qt_done, TPB * GROUPS * (b + 1))
                    pe.wait_ge(fevac_done, 2 * TPB * (b + 1))
                else:
                    if 2 * (n - 2) > 0:
                        pe.wait_ge(exp_done, 2 * (n - 2))
                pe.matmul(s[:, 0:P], q_t[:, h, 0:P], k_t[:, 0:P], start=True, stop=False)
                pe.matmul(s[:, 0:P], ident16[:, :], causal[:, :], start=False, stop=True)
                pe.matmul(s[:, P:3 * P], q_t[:, h, P:2 * P], k_t[:, :], start=True, stop=False)
                pe.matmul(s[:, 2 * P:3 * P], ident16[:, :], causal[:, :], start=False, stop=True)\
                    .then_inc(scores_done, 1)

            def turn(b, h):
                n = HEADS * b + h
                pe.wait_ge(exp_done, 2 * n + 2)
                if h == 0:
                    if TPB * b > 0:
                        pe.wait_ge(place_done, TPB * b)
                if n - 1 > 0:
                    pe.wait_ge(plo_done, n - 1)
                for k in range(3):
                    mm = pe.transpose(bank[3 + h % 2][:, k * P:(k + 1) * P], probs[:, n % 3, k * P:(k + 1) * P],
                                      ident[:, :])
                mm.then_inc(pturn_done, 1)

            def values(b, h):
                n = HEADS * b + h
                pe.wait_ge(phi_done, n + 1)
                pe.wait_ge(plo_done, n + 1)
                pe.wait_ge(vlo_done, TPB * (b + 1))
                if h % 2 == 0:
                    if n // 2 - 1 > 0:
                        pe.wait_ge(onorm_done, n // 2 - 1)
                o = bank[5 + (h // 2) % 2]
                for q, blocks in enumerate(((0,), (1, 2))):
                    at = (2 * (h % 2) + q) * (KR + 1)
                    parts = [(pp, vv, k) for k in blocks for pp, vv in ((p_hi, v_hi), (p_hi, v_lo), (p_lo, v_hi))]
                    for i, (pp, vv, k) in enumerate(parts):
                        mm = pe.matmul(o[:, at:at + KR + 1], pp[:, n % 3, k * P:(k + 1) * P],
                                       vv[:, k // 2, 0:KR + 1], start=(i == 0), stop=(i == len(parts) - 1))
                mm.then_inc(pv_done, 1)

            def oturn(b, jh):
                j, half = jh
                n = TPB * b + j
                pe.wait_ge(onorm_done, HEADS // 2 * (b + 1))
                if 2 * n + half - 1 > 0:
                    pe.wait_ge(ot_done, 2 * n + half - 1)
                for k in range(4):
                    at = (4 * half + k) * P
                    mm = pe.transpose(bank[4 + half][:, k * P:(k + 1) * P], o_row[:, j, at:at + P], ident[:, :])
                mm.then_inc(oturn_done, 1)

            def oproj(b, j):
                n = TPB * b + j
                if n == 0:
                    pe.wait_ge(absorbed_o_kept, 4)
                for half in range(2):
                    pe.wait_ge(ot_done, 2 * n + half + 1)
                    for c in range(4 * half, 4 * half + 4):
                        mm = pe.matmul(bank[6 + j][:, 0:D], o_t[:, c, :], w_out[:, c, :],
                                       start=(c == 0), stop=(c == HEADS // 2 - 1))
                    mm.then_inc(oproj_done, 1)

            def turn2(src, j, done):
                for c in range(DC):
                    mm = pe.transpose(bank[4 + j][:, c * P:(c + 1) * P], src[:, c * P:(c + 1) * P], ident[:, :])
                mm.then_inc(done, 1)

            def ctx_product(src_t, j, done):
                for half in range(2):
                    for c in range(DC):
                        mm = pe.matmul(bank[6 + half][:, :], src_t[:, j, c, :], w_ctx[:, c, half * 512:(half + 1) * 512],
                                       start=(c == 0), stop=(c == DC - 1))
                mm.then_inc(done, 1)

            def x1turn(b, j):
                n = TPB * b + j
                pe.wait_ge(x1_done, n + 1)
                pe.wait_ge(ot_done, 2 * TPB * (b + 1))
                turn2(res[:, j, :], j, x1turn_done)

            def up(b, j):
                n = TPB * b + j
                pe.wait_ge(x1t_done, n + 1)
                if n == 0:
                    pe.wait_ge(in_wctx, 16)
                pe.wait_ge(r1_done, TPB * (b + 1))
                if CTX * n > 0:
                    pe.wait_ge(pick_step, CTX * n)
                ctx_product(turned, j, up_done)

            def aturn(b, j):
                n = TPB * b + j
                pe.wait_ge(a_done, n + 1)
                turn2(a_row[:, j, :], j, aturn_done)

            def down(b, j):
                n = TPB * b + j
                pe.wait_ge(at_done, n + 1)
                pe.wait_ge(pick_step, CTX * TPB * (b + 1))
                if CTX * n > 0:
                    pe.wait_ge(sel_step, CTX * n)
                ctx_product(turned, j, down_done)

            def x2turn(b, j):
                n = TPB * b + j
                pe.wait_ge(x2_done, n + 1)
                turn2(rows[:, n, :], j, x2turn_done)

            def gate(b, j):
                n = TPB * b + j
                pe.wait_ge(x2t_done, n + 1)
                if n == 0:
                    pe.wait_ge(in_wgate, 16)
                for c in range(DC):
                    mm = pe.matmul(bank[4 + j][:, D:D + EXPERTS], turned[:, j, c, :], w_gate[:, c, :],
                                   start=(c == 0), stop=(c == DC - 1))
                mm.then_inc(gate_done, 1)

            def rank(b, j):
                n = TPB * b + j
                pe.wait_ge(chosen_done, n + 1)
                if n > 0:
                    pe.wait_ge(seen_done, n)
                at = D + EXPERTS
                pe.matmul(bank[4 + j][:, at:at + EXPERTS], earlier[:, :], chosen[:, n, :], start=True, stop=False)
                pe.matmul(bank[4 + j][:, at:at + EXPERTS], ones[:, :], seen[:, n, :], start=False, stop=True)\
                    .then_inc(rank_done, 1)

            def shared(b, j):
                n = TPB * b + j
                if n == 0:
                    pe.wait_ge(in_wgu, 16)
                    pe.wait_ge(in_wdown, 16)
                    pe.wait_ge(count_kept, 1)
                if n == TPB * SHARED_EARLY:
                    pe.wait_ge(e_actt_done, SLOT_TILES)
                    pe.wait_ge(e_y_done, SLOT_TILES)
                if 2 * n > 0:
                    pe.wait_ge(s_actt_done, 2 * n)
                for c in range(DC):
                    mm = pe.transpose(bank[4][:, c * P:(c + 1) * P], rows[:, n, c * P:(c + 1) * P], ident[:, :])
                mm.then_inc(s_xturn_done, 1)
                pe.wait_ge(s_xt_done, n + 1)
                if n > 0:
                    pe.wait_ge(s_sum_done, n)
                for s in range(SHARED):
                    for c in range(DC):
                        mm = pe.matmul(bank[6 + s][:, 0:GU], s_xt[:, c, :], w_gu[:, c, EXPERTS + s, :],
                                       start=(c == 0), stop=(c == DC - 1))
                    mm.then_inc(s_gu_done, 1)
                for s in range(SHARED):
                    pe.wait_ge(s_act_done, 2 * n + s + 1)
                    if 2 * n + s - 1 > 0:
                        pe.wait_ge(s_actt_done, 2 * n + s - 1)
                    for c in range(2):
                        mm = pe.transpose(bank[4 + s][0:HALF, c * P:(c + 1) * P], s_act[:, s, c * HALF:(c + 1) * HALF],
                                          ident[:, :])
                    mm.then_inc(s_turn_done, 1)
                pe.wait_ge(s_actt_done, 2 * n + 2)
                for k in range(2 * SHARED):
                    s, c = k // 2, k % 2
                    mm = pe.matmul(bank[6][:, 0:D], s_act_t[:, s, c, :], w_down[:, EXPERTS + s, c, :],
                                   start=(k == 0), stop=(k == 2 * SHARED - 1))
                mm.then_inc(s_down_done, 1)

            def plan(b, i):
                pe.wait_ge(seen_done, TILES)
                pe.wait_ge(place_done, TILES)
                pe.matmul(bank[7][:, 0:EXPERTS], ones[:, :], seen[:, TILES, :], start=True, stop=True)\
                    .then_inc(count_done, 1)

            def e_turn(b, s):
                pe.wait_ge(xs_in[s % XR], 16 * (s // XR + 1))
                if s - 1 > 0:
                    pe.wait_ge(e_xt_done, s - 1)
                for c in range(DC):
                    mm = pe.transpose(bank[s % 2][:, c * P:(c + 1) * P], xs[:, s % XR, c * P:(c + 1) * P], ident[:, :])
                mm.then_inc(e_turn_done, 1)

            expert_of = {}

            def e_gate_up(b, s):
                if s == 0:
                    pe.wait_ge(plan_done, 2)
                expert_of[s] = pe.value_load(tile_expert[0:1, s:s + 1], min_val=0, max_val=EXPERTS - 1)
                pe.wait_ge(e_xt_done, s + 1)
                if s - 1 > 0:
                    pe.wait_ge(e_act_done, s - 1)
                for c in range(DC):
                    mm = pe.matmul(bank[2 + s % 2][:, 0:GU], e_xt[:, s % 2, c, :], w_gu[:, c, bass.ds(expert_of[s], 1), :],
                                   start=(c == 0), stop=(c == DC - 1))
                mm.then_inc(e_gu_done, 1)

            def e_act_turn(b, s):
                pe.wait_ge(e_act_done, s + 1)
                if s < 2:
                    pe.wait_ge(s_actt_done, 2 * TPB * SHARED_EARLY)
                if s - 1 > 0:
                    pe.wait_ge(e_actt_done, s - 1)
                for c in range(2):
                    mm = pe.transpose(bank[4 + s % 2][0:HALF, c * P:(c + 1) * P], e_act[:, s % 2, c * HALF:(c + 1) * HALF],
                                      ident[:, :])
                mm.then_inc(e_aturn_done, 1)

            def e_down(b, s):
                pe.wait_ge(e_actt_done, s + 1)
                if s < 2:
                    pe.wait_ge(s_sum_done, TPB * SHARED_EARLY)
                if s - 1 > 0:
                    pe.wait_ge(e_y_done, s - 1)
                for c in range(2):
                    mm = pe.matmul(bank[6 + s % 2][:, 0:D], e_act_t[:, s % 2, c, :], w_down[:, bass.ds(expert_of[s], 1), c, :],
                                   start=(c == 0), stop=(c == 1))
                mm.then_inc(e_down_done, 1)

            run({"qkv": qkv, "fturn": latents_turn, "absorb": absorb, "qproj": qproj, "qturn": qturn, "scores": scores,
                 "turn": turn, "values": values, "oturn": oturn, "oproj": oproj, "x1turn": x1turn, "up": up,
                 "aturn": aturn, "down": down, "x2turn": x2turn, "gate": gate, "rank": rank,
                 "shared": shared, "plan": plan, "e_turn": e_turn, "e_gate_up": e_gate_up, "e_act_turn": e_act_turn,
                 "e_down": e_down})

        @block.vector
        def _(dve):
            def masks():
                dve.wait_ge(in_ids, 16)
                dve.tensor_copy(ids_f[:, :], ids_i[:, :]).then_inc(masks_step, 1)
                dve.wait_ge(masks_step, 1)
                for e in range(CTX):
                    if e == 0:
                        dve.tensor_scalar(picks[:, :, 0], ids_f[:, :], float(CTX_STEP), None, ALU.is_lt).then_inc(masks_step, 1)
                    elif e == CTX - 1:
                        dve.tensor_scalar(picks[:, :, e], ids_f[:, :], float(e * CTX_STEP), None, ALU.is_ge).then_inc(masks_step, 1)
                    else:
                        dve.wait_ge(masks_step, 2 * e)
                        dve.tensor_scalar(above[:, :], ids_f[:, :], float(e * CTX_STEP), None, ALU.is_ge).then_inc(masks_step, 1)
                        dve.wait_ge(masks_step, 2 * e + 1)
                        dve.scalar_tensor_tensor(out=picks[:, :, e], in0=ids_f[:, :], scalar=float((e + 1) * CTX_STEP),
                                                     in1=above[:, :], op0=ALU.is_lt, op1=ALU.mult).then_inc(masks_step, 1)

            def norm(b, j):
                n = TPB * b + j
                if n == 0:
                    dve.wait_ge(in_norms, 32)
                    dve.tensor_scalar(w_qn[:, :], w_qn[:, :], SCALE, None, ALU.mult).then_inc(norms_scaled, 1)
                    dve.wait_ge(norms_scaled, 1)
                    dve.wait_ge(in_rope, 32)
                q = bank[j]
                dve.wait_ge(rms_done, b + 1)
                if n - 1 > 0:
                    dve.wait_ge(fturn_done, n - 1)
                if n - 1 > 0:
                    dve.wait_ge(vlo_done, n - 1)
                dve.scalar_tensor_tensor(out=qn[:, j, :], in0=q[:, 0:QR], scalar=rms[:, 2 * j:2 * j + 1],
                                             in1=w_qn[:, :], op0=ALU.mult, op1=ALU.mult).then_inc(qn_done, 1)
                dve.scalar_tensor_tensor(out=kv_row[:, j, 0:KR], in0=q[:, QR:QR + KR],
                                             scalar=rms[:, 2 * j + 1:2 * j + 2], in1=w_kn[:, :],
                                             op0=ALU.mult, op1=ALU.mult).then_inc(kvc_done, 1)
                pe_at, half = QR + KR, ROPE // 2
                if n - 1 > 0:
                    dve.wait_ge(kv_done, n - 1)
                dve.tensor_tensor(k_cos[:, j, :], q[:, pe_at:pe_at + ROPE], cos[:, j, :], ALU.mult).then_inc(krope_done, 1)
                for a, c in ((0, half), (half, 0)):
                    dve.tensor_tensor(k_sin[:, j, a:a + half], q[:, pe_at + c:pe_at + c + half],
                                          sin[:, j, a:a + half], ALU.mult).then_inc(krope_done, 1)
                dve.wait_ge(krope_done, 3 * (n + 1))
                dve.tensor_tensor(kv_row[:, j, KR:HD], k_cos[:, j, :], k_sin[:, j, :], ALU.add).then_inc(kv_done, 1)

            def q_rope(b, jg):
                j, g = jg
                i = GROUPS * (TPB * b + j) + g
                dve.wait_ge(qproj_done, i + 1)
                if i - 1 > 0:
                    dve.wait_ge(qrow_done, i - 1)
                half = ROPE // 2
                q = bank[g % 2][:, :].rearrange("p (h d) -> p h d", h=QG)

                def table(t, a, w):
                    return t[:, j, a:a + w].unsqueeze(1).broadcast_to([P, QG, w])

                dve.tensor_tensor(q_cos[:, i % 2], q[:, :, KR:HD], table(cos, 0, ROPE), ALU.mult)
                dve.tensor_tensor(q_sin[:, i % 2, :, 0:half], q[:, :, KR + half:HD], table(sin, 0, half), ALU.mult)
                dve.tensor_tensor(q_sin[:, i % 2, :, half:ROPE], q[:, :, KR:KR + half], table(sin, half, half),
                                      ALU.mult).then_inc(qrope_done, 1)

            def maxima(b, h):
                n = HEADS * b + h
                dve.wait_ge(scores_done, n + 1)
                if 2 * (n - 2) > 0:
                    dve.wait_ge(exp_done, 2 * (n - 2))
                for q, (at, w) in enumerate(((0, P), (P, 2 * P))):
                    dve.tensor_reduce(neg_max[:, n % 3, q:q + 1], bank[h % 3][:, at:at + w], AX, ALU.max,
                                          negate=True).then_inc(max_done, 1)

            def probs_lo(b, h):
                n = HEADS * b + h
                dve.wait_ge(phi_done, n + 1)
                if n - 2 > 0:
                    dve.wait_ge(pv_done, n - 2)
                dve.tensor_tensor(p_lo[:, n % 3, :], bank[3 + h % 2][:, 0:3 * P], p_hi[:, n % 3, :],
                                      ALU.subtract).then_inc(plo_done, 1)

            def head_out(b, h):
                if h % 2 == 0:
                    return
                n = HEADS * b + h
                pair = n // 2
                o = bank[5 + (h // 2) % 2][:, 0:4 * (KR + 1)].rearrange("p (h q r) -> p h q r", h=2, q=2)
                dve.wait_ge(pv_done, n + 1)
                if 2 * TPB * b > 0:
                    dve.wait_ge(oturn_done, 2 * TPB * b)
                if pair - 1 > 0:
                    dve.wait_ge(onorm_done, pair - 1)
                dve.reciprocal(inv_sum[:, pair % 2, :], o[:, :, :, KR]).then_inc(inv_done, 1)
                dve.wait_ge(inv_done, pair + 1)
                inv = inv_sum[:, pair % 2, :].rearrange("p (h q) -> p h q", h=2).unsqueeze(3).broadcast_to([P, 2, 2, KR])
                dst = o_row[:, :, (h - 1) * KR:(h + 1) * KR].rearrange("p q (h r) -> p h q r", h=2)
                dve.tensor_tensor(dst, o[:, :, :, 0:KR], inv, ALU.mult).then_inc(onorm_done, 1)

            def stats_of(stat, mom, j, n, src):
                dve.bn_stats(stats[:, j, :], src).then_inc(stat, 1)
                dve.wait_ge(stat, n + 1)
                dve.bn_aggr(moments[:, j, :], stats[:, j, :]).then_inc(mom, 1)

            def normed(inverse, j, n, dst, src, done):
                dve.wait_ge(inverse, n + 1)
                dve.tensor_scalar(dst, src, moments[:, j, 0:1], rstd[:, j, :], ALU.subtract, ALU.mult).then_inc(done, 1)

            def oproj(b, j):
                n = TPB * b + j
                dve.wait_ge(in_x, 16)
                dve.wait_ge(oproj_done, 2 * n + 2)
                dve.tensor_tensor(res[:, j, :], bank[6 + j][:, 0:D], rows[:, n, :], ALU.add).then_inc(r1_done, 1)
                dve.wait_ge(r1_done, n + 1)
                stats_of(r1_stat, r1_mom, j, n, res[:, j, :])

            def x1_norm(b, j):
                n = TPB * b + j
                if n - 1 > 0:
                    dve.wait_ge(x1turn_done, n - 1)
                normed(r1_rstd, j, n, res[:, j, :], res[:, j, :], x1_done)

            def expert_cols(e):
                return bank[6 + e // 2][:, (e % 2) * D:(e % 2 + 1) * D]

            def up(b, j):
                n = TPB * b + j
                if n == 0:
                    dve.wait_ge(masks_step, 7)
                dve.wait_ge(up_done, n + 1)
                if n - 1 > 0:
                    dve.wait_ge(silu_done, n - 1)
                if n - 1 > 0:
                    dve.wait_ge(a_done, n - 1)
                dve.tensor_scalar(picked[:, j, :], expert_cols(0), picks[:, n, 0:1], None, ALU.mult).then_inc(pick_step, 1)
                for e in range(1, CTX):
                    if CTX * n + e > 0:
                        dve.wait_ge(pick_step, CTX * n + e)
                    dve.scalar_tensor_tensor(out=picked[:, j, :], in0=expert_cols(e), scalar=picks[:, n, e:e + 1],
                                                 in1=picked[:, j, :], op0=ALU.mult, op1=ALU.add).then_inc(pick_step, 1)

            def act_product(b, j):
                n = TPB * b + j
                dve.wait_ge(silu_done, n + 1)
                dve.wait_ge(pick_step, CTX * (n + 1))
                if n - 1 > 0:
                    dve.wait_ge(aturn_done, n - 1)
                dve.tensor_tensor(a_row[:, j, :], gated[:, j, :], picked[:, j, :], ALU.mult).then_inc(a_done, 1)

            def down(b, j):
                n = TPB * b + j
                dve.wait_ge(down_done, n + 1)
                dve.wait_ge(x1_done, n + 1)
                for e in range(CTX):
                    if CTX * n + e > 0:
                        dve.wait_ge(sel_step, CTX * n + e)
                    dve.scalar_tensor_tensor(out=res[:, j, :], in0=expert_cols(e), scalar=picks[:, n, e:e + 1],
                                                 in1=res[:, j, :],
                                                 op0=ALU.mult, op1=ALU.add).then_inc(sel_step, 1)
                dve.wait_ge(sel_step, CTX * (n + 1))
                stats_of(r2_stat, r2_mom, j, n, res[:, j, :])

            def x2_norm(b, j):
                n = TPB * b + j
                normed(r2_rstd, j, n, rows[:, n, :], res[:, j, :], x2_done)

            def gate(b, j):
                n = TPB * b + j
                dve.wait_ge(gate_done, n + 1)
                dve.tensor_copy(logits[:, n, :], bank[4 + j][:, D:D + EXPERTS]).then_inc(logits_done, 1)
                dve.wait_ge(logits_done, n + 1)
                dve.max(top[:, n, :], logits[:, n, :]).then_inc(route_step, 1)
                dve.wait_ge(route_step, 4 * n + 1)
                dve.max_index(top_i[:, n, :], top[:, n, :], logits[:, n, :]).then_inc(route_step, 1)
                dve.wait_ge(route_step, 4 * n + 2)
                dve.tensor_copy(top_f[:, n, :], top_i[:, n, 0:TOPK]).then_inc(route_step, 1)
                dve.wait_ge(route_step, 4 * n + 3)
                dve.wait_ge(eye_made, 18)
                dve.tensor_tensor(onehot[:, j], iota16[:, :].unsqueeze(1).broadcast_to([P, TOPK, EXPERTS]),
                                  top_f[:, n, :].unsqueeze(2).broadcast_to([P, TOPK, EXPERTS]), ALU.is_equal)\
                    .then_inc(route_step, 1)
                dve.wait_ge(route_step, 4 * n + 4)
                with nc.allow_low_precision(reason="sums of at most 8 ones are exact"):
                    dve.tensor_reduce(chosen[:, n, :], onehot[:, j].rearrange("p k e -> p e k"), AX, ALU.add).then_inc(chosen_done, 1)
                    dve.wait_ge(chosen_done, n + 1)
                    dve.tensor_tensor(seen[:, n + 1, :], seen[:, n, :], chosen[:, n, :], ALU.add).then_inc(seen_done, 1)

            def rank(b, j):
                n = TPB * b + j
                dve.wait_ge(rank_done, n + 1)
                at = D + EXPERTS
                dve.tensor_tensor(place[:, n, :], bank[4 + j][:, at:at + EXPERTS], region[:, :], ALU.add).then_inc(place_done, 1)
                dve.wait_ge(place_done, n + 1)
                dve.tensor_tensor(placed[:, j], onehot[:, j],
                                      place[:, n, :].unsqueeze(1).broadcast_to([P, TOPK, EXPERTS]), ALU.mult).then_inc(placed_done, 1)
                dve.wait_ge(placed_done, n + 1)
                dve.tensor_reduce(slot_f[:, n, :], placed[:, j], AX, ALU.add).then_inc(slotf_done, 1)
                dve.wait_ge(slotf_done, n + 1)
                dve.tensor_copy(slot[:, n, :], slot_f[:, n, :]).then_inc(slot_done, 1)

            def shared(b, j):
                n = TPB * b + j
                for s in range(SHARED):
                    dve.wait_ge(s_silu_done, 2 * n + s + 1)
                    if 2 * n + s - 1 > 0:
                        dve.wait_ge(s_turn_done, 2 * n + s - 1)
                    dve.tensor_tensor(s_act[:, s, :], bank[6 + s][:, INNER:GU], s_gate[:, s, :], ALU.mult).then_inc(s_act_done, 1)
                dve.wait_ge(s_down_done, n + 1)
                dve.wait_ge(x2_stored[n], 16)
                dve.tensor_tensor(rows[:, n, :], bank[6][:, 0:D], rows[:, n, :], ALU.add).then_inc(s_sum_done, 1)

            def plan(b, i):
                step = [0]

                def then(ins):
                    step[0] += 1
                    ins.then_inc(plan_step, 1)
                    dve.wait_ge(plan_step, step[0])

                dve.wait_ge(count_done, 1)
                dve.tensor_copy(count[:, :], bank[7][:, 0:EXPERTS]).then_inc(count_kept, 1)
                dve.wait_ge(count_kept, 1)
                then(dve.tensor_tensor(full[:, :, :], count[:, :].unsqueeze(2).broadcast_to([P, EXPERTS, TILES]),
                                       tile_starts[:, :].unsqueeze(1).broadcast_to([P, EXPERTS, TILES]), ALU.is_gt))
                then(dve.tensor_reduce(tiles_of[:, :], full[:, :, :], AX, ALU.add))
                then(dve.tensor_tensor(prior[:, :, :], before[:, :, :],
                                       tiles_of[:, :].unsqueeze(1).broadcast_to([P, EXPERTS, EXPERTS]), ALU.mult))
                then(dve.tensor_reduce(base[:, :], prior[:, :, :], AX, ALU.add))
                wide = [P, SLOT_TILES, EXPERTS]
                then(dve.tensor_tensor(begun[:, :, :], slot_iota[:, :].unsqueeze(2).broadcast_to(wide),
                                       base[:, :].unsqueeze(1).broadcast_to(wide), ALU.is_ge))
                then(dve.tensor_reduce(t_expert[:, :], begun[:, :, :], AX, ALU.add))
                then(dve.tensor_tensor(begun[:, :, :], begun[:, :, :], base[:, :].unsqueeze(1).broadcast_to(wide),
                                       ALU.mult))
                then(dve.tensor_reduce(t_first[:, :], begun[:, :, :], AX, ALU.max))
                then(dve.tensor_tensor(t_within[:, :], slot_iota[:, :], t_first[:, :], ALU.subtract))
                then(dve.tensor_scalar(t_expert[:, :], t_expert[:, :], -1.0, None, ALU.add))
                then(dve.tensor_scalar(t_within[:, :], t_within[:, :], float(TILES - 1), None, ALU.min))
                then(dve.scalar_tensor_tensor(out=t_row[:, :], in0=t_expert[:, :], scalar=float(TILES),
                                              in1=t_within[:, :], op0=ALU.mult, op1=ALU.add))
                dve.tensor_copy(tile_block[:, :], t_row[:, :]).then_inc(plan_done, 1)
                dve.tensor_copy(tile_expert[:, :], t_expert[:, :]).then_inc(plan_done, 1)
                all_k = [P, TILES * TOPK, EXPERTS]
                then(dve.scalar_tensor_tensor(out=shift[:, :], in0=base[:, :], scalar=float(P), in1=region[:, :],
                                              op0=ALU.mult, op1=ALU.subtract))
                dve.tensor_copy(top_f[:, :, :], top_i[:, :, 0:TOPK]).then_inc(y_slot_step, 1)
                dve.wait_ge(y_slot_step, 1)
                dve.tensor_tensor(onehots[:, :, :], iota16[:, :].unsqueeze(1).broadcast_to(all_k),
                                      top_f[:, :, :].rearrange("p n k -> p (n k)").unsqueeze(2).broadcast_to(all_k),
                                      ALU.is_equal).then_inc(y_slot_step, 1)
                dve.wait_ge(y_slot_step, 2)
                dve.tensor_tensor(onehots[:, :, :], onehots[:, :, :], shift[:, :].unsqueeze(1).broadcast_to(all_k),
                                      ALU.mult).then_inc(y_slot_step, 1)
                dve.wait_ge(y_slot_step, 3)
                dve.tensor_reduce(top_f[:, :, :].rearrange("p n k -> p (n k)"), onehots[:, :, :], AX, ALU.add).then_inc(y_slot_step, 1)
                dve.wait_ge(y_slot_step, 4)
                dve.tensor_tensor(top_f[:, :, :], top_f[:, :, :], slot_f[:, :, :], ALU.add).then_inc(y_slot_step, 1)
                dve.wait_ge(y_slot_step, 5)
                dve.tensor_copy(y_slot[:, :, :], top_f[:, :, :]).then_inc(y_slot_done, 1)
                best = top[:, :, 0:1]
                dve.tensor_tensor(shifted[:, :, :], logits[:, :, :], best.broadcast_to([P, TILES, EXPERTS]),
                                      ALU.subtract).then_inc(soft_shift, 1)
                dve.tensor_tensor(soft_top[:, :, :], top[:, :, 0:TOPK], best.broadcast_to([P, TILES, TOPK]),
                                      ALU.subtract).then_inc(soft_shift, 1)
                dve.wait_ge(soft_exp, 2)
                dve.tensor_reduce(soft_sum[:, :], shifted[:, :, :], AX, ALU.add).then_inc(soft_step, 1)
                dve.wait_ge(soft_step, 1)
                dve.reciprocal(soft_inv[:, :], soft_sum[:, :]).then_inc(soft_step, 1)
                dve.wait_ge(soft_step, 2)
                dve.tensor_tensor(weight[:, :, :], soft_top[:, :, :],
                                      soft_inv[:, :].unsqueeze(2).broadcast_to([P, TILES, TOPK]), ALU.mult).then_inc(weight_done, 1)

            def e_gate_up(b, s):
                dve.wait_ge(e_silu_done, s + 1)
                if s - 1 > 0:
                    dve.wait_ge(e_aturn_done, s - 1)
                dve.tensor_tensor(e_act[:, s % 2, :], bank[2 + s % 2][:, INNER:GU], e_gate[:, s % 2, :], ALU.mult).then_inc(e_act_done, 1)

            def e_act_turn(b, s):
                dve.wait_ge(e_aturn_done, s + 1)
                if s - 1 > 0:
                    dve.wait_ge(e_down_done, s - 1)
                dve.tensor_copy(e_act_t[:, s % 2],
                                    bank[4 + s % 2][0:HALF, 0:2 * P].rearrange("p (c t) -> p c t", c=2)).then_inc(e_actt_done, 1)

            def combine(b, n):
                if n == 0:
                    dve.wait_ge(weight_done, 1)
                j = n % 2
                dve.wait_ge(back_in[j], 16 * TOPK * (n // 2 + 1))
                dve.wait_ge(s_sum_done, n + 1)
                for k in range(TOPK):
                    if TOPK * n + k > 0:
                        dve.wait_ge(sum_step, TOPK * n + k)
                    dve.scalar_tensor_tensor(out=rows[:, n, :], in0=back[:, j, k, :], scalar=weight[:, n, k:k + 1],
                                                 in1=rows[:, n, :], op0=ALU.mult, op1=ALU.add).then_inc(sum_step, 1)
                dve.wait_ge(sum_step, TOPK * (n + 1))
                stats_of(r3_stat, r3_mom, j, n, rows[:, n, :])
                if n >= 2:
                    dve.wait_ge(fin_stored[j], 16 * (n // 2))
                normed(r3_rstd, j, n, fin[:, j, :], rows[:, n, :], fin_done)

            masks()
            run({"norm": norm, "qproj": q_rope, "scores": maxima, "low": probs_lo, "out": head_out,
                 "oproj": oproj, "x1": x1_norm, "up": up, "act": act_product, "down": down, "x2": x2_norm,
                 "gate": gate, "rank": rank,
                 "shared": shared, "plan": plan, "e_gate_up": e_gate_up, "e_act_turn": e_act_turn,
                 "combine": combine})


def kernel(**inputs):
    import numpy as np
    import concourse.bacc as bacc
    from concourse.bass_utils import run_bass_kernel_spmd

    a = {k: np.asarray(v) for k, v in inputs.items()}
    qb = a["L0_attn_q_b_w"].reshape(HEADS, QHD, QR)
    inv = np.float32(1.0) / np.float32(10000.0) ** (np.arange(0, ROPE, 2, dtype=np.float32) / np.float32(ROPE))
    freqs = np.outer(np.arange(SEQ, dtype=np.float32), inv.astype(np.float32)).astype(np.float32)
    cos = np.concatenate([np.cos(freqs), np.cos(freqs)], 1)
    sin = np.concatenate([-np.sin(freqs), np.sin(freqs)], 1)
    sg, su = a["L0_ffn_sg"], a["L0_ffn_su"]
    gate_up = np.concatenate([a["L0_ffn_wg"], a["L0_ffn_wu"]], 2)
    halves = [np.concatenate([sg[:, h * INNER:(h + 1) * INNER], su[:, h * INNER:(h + 1) * INNER]], 1)
              for h in range(SHARED)]
    laid = {
        "xT": a["x"].reshape(TOKENS, D).T,
        "x": a["x"].reshape(TOKENS, D),
        "ids": a["itok_BxS_13_99985"].reshape(TILES, P).T,
        "wqkvT": np.concatenate([a["L0_attn_q_a_w"], a["L0_attn_kv_a_w"]], 0).T,
        "qlnw": a["L0_attn_q_a_ln_w"],
        "kvlnw": a["L0_attn_kv_a_ln_w"],
        "qnope": qb[:, 0:NOPE, :],
        "qpeT": qb[:, NOPE:QHD, :].transpose(2, 0, 1),
        "kvb": a["L0_attn_kv_b_w"],
        "woT": a["L0_attn_o_w"].T,
        "cosT": cos,
        "sinT": sin,
        "ctxT": a["ctx_2048"].transpose(2, 0, 1).reshape(D, CTX * D),
        "wgateT": a["L0_ffn_w_gate"].T,
        "wgu": np.concatenate([gate_up, np.stack(halves)], 0).transpose(1, 0, 2),
        "wd": np.concatenate([a["L0_ffn_wd"], a["L0_ffn_sd"].reshape(SHARED, INNER, D)], 0),
    }
    nc = bacc.Bacc("TRN2", target_bir_lowering=False, num_devices=1)
    arrays, aps = {}, {}
    for name, v in laid.items():
        v = np.ascontiguousarray(v)
        arrays[f"in_{name}"] = v
        aps[name] = nc.dram_tensor(f"in_{name}", v.shape, mybir.dt.from_np(v.dtype), kind="ExternalInput").ap()
    aps["out"] = nc.dram_tensor("out_0", (TOKENS, D), F32, kind="ExternalOutput").ap()
    decoder_layer(nc, **aps)
    r = run_bass_kernel_spmd(nc, [arrays], core_ids=[0])
    return r.results[0]["out_0"].reshape(BATCH, SEQ, D)
```

```python
from contextlib import ExitStack

import concourse.bass as bass
from concourse import mybir

ALU = mybir.AluOpType
ACT = mybir.ActivationFunctionType
AX = mybir.AxisListType.X
F32 = mybir.dt.float32
F16 = mybir.dt.float16
BF16 = mybir.dt.bfloat16
I32 = mybir.dt.int32
U32 = mybir.dt.uint32

P = 128
BATCH, SEQ, D = 4, 256, 256
TOKENS = BATCH * SEQ
TILES = TOKENS // P
TPB = SEQ // P
DC = D // P
HEADS, NOPE, ROPE, VD = 16, 128, 64, 128
QHD = NOPE + ROPE
SCALE = float(QHD) ** -0.5
QR, KR = 192, 64
QC = QR // 2
HD = KR + ROPE
QG = 4
GROUPS = HEADS // QG
CTX = 4
CTX_STEP = 12500 // CTX
EXPERTS, TOPK, INNER = 16, 4, 176
HALF = INNER // 2
SHARED = 2
GU = 2 * INNER
RMS_EPS, LN_EPS = 1e-6, 1e-5
MASKED = -1e30
EYES, MASKS = 5, 15
SLOT_TILES = (TOKENS * TOPK + EXPERTS * (P - 1)) // P
BLOCKS = (EXPERTS - 1) * TILES + SLOT_TILES


def decoder_layer(nc, xT, x, ids, wqkvT, qlnw, kvlnw, qnope, qpeT, kvb, woT, cosT, sinT, ctxT,
                  wgateT, wgu, wd, out):
    x2_dram = nc.dram_tensor("x2_dram", (TOKENS, D), F32, kind="Internal").ap()
    table = nc.dram_tensor("table", (BLOCKS * P, 2), U32, kind="Internal").ap()
    y_dram = nc.dram_tensor("y_dram", (TOKENS * TOPK + BLOCKS * P, D), F32, kind="Internal").ap()

    with ExitStack() as ctx:
        def sb(name, shape, dt=F32):
            return ctx.enter_context(nc.sbuf_tensor(name, shape, dt))

        def sem(name):
            return ctx.enter_context(nc.semaphore(name))

        bank = [ctx.enter_context(nc.psum_tensor(f"bank{i}", [P, 512], F32)) for i in range(8)]

        ident = sb("ident", [P, P])
        ident16 = sb("ident16", [P, P], BF16)
        causal = sb("causal", [P, P], BF16)
        earlier = sb("earlier", [P, P], BF16)
        ones = sb("ones", [P, P], BF16)
        iota16 = sb("iota16", [P, EXPERTS])
        region = sb("region", [P, EXPERTS])
        before = sb("before", [P, EXPERTS, EXPERTS])
        tile_starts = sb("tile_starts", [P, TILES])
        slot_iota = sb("slot_iota", [P, 1])
        token_pair = sb("token_pair", [P, TILES, TOPK, 2], U32)
        cos = sb("cos", [P, TPB, ROPE])
        sin = sb("sin", [P, TPB, ROPE])
        w_qkv = sb("w_qkv", [P, DC, QR + KR + ROPE])
        w_qn = sb("w_qn", [P, QR])
        w_kn = sb("w_kn", [P, KR])
        w_kn_column = sb("w_kn_column", [P, 1])
        w_q = sb("w_q", [QC, 2, HEADS, HD])
        w_out = sb("w_out", [P, HEADS // 2, D])
        w_ctx = sb("w_ctx", [P, DC, CTX * D])
        w_gate = sb("w_gate", [P, DC, EXPERTS])
        w_gu = sb("w_gu", [P, DC, EXPERTS + SHARED, GU])
        w_gu_parts = w_gu[:, :, :, :].bitcast(F16).rearrange("p c e (h n) -> p c e h n", h=2)
        gu_temp = sb("gu_temp", [P, 2, DC, GU], F16)
        gu_squares = sb("gu_squares", [P, EXPERTS + SHARED])
        gu_sum = sb("gu_sum", [P, 1], BF16)
        gu_norm = sb("gu_norm", [P, 1])
        gu_inverse = sb("gu_inverse", [P, 1])
        gu_power = sb("gu_power", [P, 2])
        gu_scale = sb("gu_scale", [P, 2])
        area = sb("area", [P, (EXPERTS + SHARED) * 2 * D])
        w_down = area[0:HALF, :].rearrange("p (e c d) -> p e c d", e=EXPERTS + SHARED, c=2)
        raw_q = area[:, 0:HEADS * QR].rearrange("p (h r) -> p h r", h=HEADS)
        raw_kv = area[:, HEADS * QR:HEADS * (QR + 2 * KR)].rearrange("p (h t r) -> p h t r", h=HEADS, t=2)
        raw_o = area[:, HEADS * (QR + 2 * KR):HEADS * (QR + 2 * KR + D)].rearrange("p (h d) -> p h d", h=HEADS)
        x_t = sb("x_t", [P, DC, SEQ])
        rows = sb("rows", [P, TILES, D])
        ssq = sb("ssq", [P, 2 * TPB])
        ssq_eps = sb("ssq_eps", [P, 2 * TPB])
        minus_half = sb("minus_half", [P, 2 * TPB])
        rms = sb("rms", [P, 2 * TPB])
        qn = sb("qn", [P, TPB, QR])
        kv_row = sb("kv_row", [P, TPB, HD])
        v_hi = sb("v_hi", [P, TPB, KR + 2], F16)
        v_lo = sb("v_lo", [P, TPB, KR + 2], F16)
        qn_t = sb("qn_t", [QC, 2, SEQ])
        k_t = sb("k_t", [P, SEQ])
        q_row_mem = sb("q_row_mem", [P, TPB * HEADS * HD])
        q_t_mem = sb("q_t_mem", [P, HEADS * SEQ])
        o_row_mem = sb("o_row_mem", [P, TPB * HEADS * KR])
        probs_mem = sb("probs_mem", [P, 3 * 3 * P])

        def carve(mem, parts):
            at, views = 0, []
            for width, pattern, sizes in parts:
                views.append(mem[:, at:at + width].rearrange(pattern, **sizes))
                at += width
            return views

        q_row, = carve(q_row_mem, [(TPB * HEADS * HD, "p (j h d) -> p j h d", dict(j=TPB, h=HEADS))])
        act_junk, k_cos, k_sin = carve(q_row_mem, [
            (TPB * (QR + KR), "p (j r) -> p j r", dict(j=TPB)), (TPB * ROPE, "p (j r) -> p j r", dict(j=TPB)),
            (TPB * ROPE, "p (j r) -> p j r", dict(j=TPB))])
        q_t, = carve(q_t_mem, [(HEADS * SEQ, "p (h t) -> p h t", dict(h=HEADS))])
        o_row, = carve(o_row_mem, [(TPB * HEADS * KR, "p (j o) -> p j o", dict(j=TPB))])
        probs, = carve(probs_mem, [(9 * P, "p (r k) -> p r k", dict(r=3))])
        o_t, = carve(probs_mem, [(HEADS // 2 * P, "p (c t) -> p c t", dict(c=HEADS // 2))])
        pair = "p (r d) -> p r d", dict(r=2)
        picked, gated, a_row, s_act_t = carve(o_row_mem, [(2 * D, *pair)] * 3 + [
            (4 * P, "p (s c t) -> p s c t", dict(s=2, c=2))])
        s_act_t = s_act_t[0:HALF]
        XR, YR, IR = 5, 3, 12
        IS = 8
        s_gate, = carve(x_t[:, :, :].rearrange("p c t -> p (c t)"), [(2 * INNER, *pair)])
        s_act, = carve(w_qkv[:, :, :].rearrange("p c n -> p (c n)"), [(2 * INNER, *pair)])
        back, = carve(area, [(TILES * TOPK * D, "p (n k d) -> p n k d", dict(n=TILES, k=TOPK))])
        fin, = carve(o_row_mem, [(2 * D, *pair)])
        mix_weight, = carve(q_row_mem, [(TILES * TOPK * P, "p (n k t) -> p n k t", dict(n=TILES, k=TOPK))])
        xs, e_xt_mem, e_gate, e_act, e_act_t, ys, s_xt = carve(q_t_mem, [
            (XR * D, "p (r d) -> p r d", dict(r=XR)), (4 * P, "p (r c t) -> p r c t", dict(r=2, c=2)),
            (2 * INNER, *pair), (2 * INNER, *pair), (4 * P, "p (r c t) -> p r c t", dict(r=2, c=2)),
            (YR * D, "p (r d) -> p r d", dict(r=YR)), (DC * P, "p (c t) -> p c t", dict(c=DC))])
        e_act_t = e_act_t[0:HALF]
        e_xt = e_xt_mem.rearrange("p r c t -> p (r c t)").bitcast(F16).rearrange(
            "p (r h c t) -> p r h c t", r=2, h=2, c=DC)
        s_xt = s_xt.rearrange("p c t -> p (c t)").bitcast(F16).rearrange("p (h c t) -> p h c t", h=2, c=DC)
        q_cos = sb("q_cos", [P, 2, QG, ROPE])
        q_sin = sb("q_sin", [P, 2, QG, ROPE])
        neg_max = sb("neg_max", [P, 3, TPB])
        p_hi = sb("p_hi", [P, 3, 3 * P], F16)
        p_lo = sb("p_lo", [P, 3, 3 * P], F16)
        inv_sum = sb("inv_sum", [P, 2, 2 * TPB])
        res = sb("res", [P, TPB, D])
        turned = sb("turned", [P, TPB, DC, P])
        stats = sb("stats", [P, TPB, 6])
        moments = sb("moments", [P, TPB, 2])
        var_eps = sb("var_eps", [P, TPB, 1])
        rstd = sb("rstd", [P, TPB, 1])
        ids_i = sb("ids_i", [P, TILES], I32)
        ids_f = sb("ids_f", [P, TILES])
        above = sb("above", [P, TILES])
        picks = sb("picks", [P, TILES, CTX])
        logits = sb("logits", [P, TILES, EXPERTS])
        top = sb("top", [P, TILES, 8])
        top_i = sb("top_i", [P, TILES, 8], U32)
        top_f = sb("top_f", [P, TILES, TOPK])
        onehot = sb("onehot", [P, 2, TOPK, EXPERTS])
        chosen = sb("chosen", [P, TILES, EXPERTS], BF16)
        seen = sb("seen", [P, TILES + 1, EXPERTS], BF16)
        place = sb("place", [P, TILES, EXPERTS])
        placed = sb("placed", [P, 2, TOPK, EXPERTS])
        slot_f = sb("slot_f", [P, TILES, TOPK])
        slot = sb("slot", [P, TILES, TOPK], U32)
        count = sb("count", [P, EXPERTS])
        full = sb("full", [P, EXPERTS, TILES])
        tiles_of = sb("tiles_of", [P, EXPERTS])
        step_up = sb("step_up", [P, EXPERTS])
        prior = sb("prior", [P, EXPERTS, EXPERTS])
        base = sb("base", [P, EXPERTS])
        begun = sb("begun", [P, EXPERTS])
        begun_step = sb("begun_step", [P, EXPERTS])
        t_expert = sb("t_expert", [P, 1])
        t_row = sb("t_row", [P, 1])
        tile_expert = sb("tile_expert", [P, 1], I32)
        tile_block = sb("tile_block", [P, 1], I32)
        shifted, = carve(probs_mem, [(TILES * EXPERTS, "p (n e) -> p n e", dict(n=TILES))])
        soft_sum = sb("soft_sum", [P, TILES])
        soft_inv = sb("soft_inv", [P, TILES])
        soft_top = sb("soft_top", [P, TILES, TOPK])
        weight = sb("weight", [P, TILES, TOPK])

        table_init = q_t_mem[:, 0:4 * P].bitcast(U32).rearrange("p (a n o) -> p a n o", a=2, o=2)
        idx = sb("idx", [P, IR, 2], U32)

        in_xt = sem("in_xt")
        in_wqkv = sem("in_wqkv")
        in_norms = sem("in_norms")
        in_rope = sem("in_rope")
        in_rawqk = [sem(f"in_rawqk{half}") for half in range(2)]
        in_rawv = sem("in_rawv")
        in_wpe = sem("in_wpe")
        in_rawo = sem("in_rawo")
        in_x = sem("in_x")
        in_ids = sem("in_ids")
        in_wctx = sem("in_wctx")
        in_wgate = sem("in_wgate")
        in_wshared = sem("in_wshared")
        in_wgu = sem("in_wgu")
        in_wdown = sem("in_wdown")
        table_filled = sem("table_filled")
        const_made = sem("const_made")
        masks_made = sem("masks_made")
        eye_made = sem("eye_made")
        norms_scaled = sem("norms_scaled")
        qkv_done = sem("qkv_done")
        ssq_done = sem("ssq_done")
        rms_eps_done = sem("rms_eps_done")
        rms_done = sem("rms_done")
        qn_done = sem("qn_done")
        kvc_done = sem("kvc_done")
        krope_done = sem("krope_done")
        kv_done = sem("kv_done")
        vhi_done = sem("vhi_done")
        vlo_done = sem("vlo_done")
        fturn_done = sem("fturn_done")
        fevac_done = sem("fevac_done")
        qproj_done = sem("qproj_done")
        qrope_done = sem("qrope_done")
        abs_done = sem("abs_done")
        qrow_done = sem("qrow_done")
        qturn_done = sem("qturn_done")
        qt_done = sem("qt_done")
        absorbed_q = sem("absorbed_q")
        absorbed_q_kept = sem("absorbed_q_kept")
        absorbed_o = sem("absorbed_o")
        absorbed_o_kept = sem("absorbed_o_kept")
        scores_done = sem("scores_done")
        max_done = sem("max_done")
        exp_done = sem("exp_done")
        pturn_done = sem("pturn_done")
        phi_done = sem("phi_done")
        plo_done = sem("plo_done")
        pv_done = sem("pv_done")
        inv_done = sem("inv_done")
        onorm_done = sem("onorm_done")
        oturn_done = sem("oturn_done")
        ot_done = sem("ot_done")
        oproj_done = sem("oproj_done")
        r1_done = sem("r1_done")
        r1_mom = sem("r1_mom")
        r1_rstd = sem("r1_rstd")
        x1_done = sem("x1_done")
        x1turn_done = sem("x1turn_done")
        x1t_done = sem("x1t_done")
        up_done = sem("up_done")
        pick_step = sem("pick_step")
        silu_done = sem("silu_done")
        a_done = sem("a_done")
        aturn_done = sem("aturn_done")
        at_done = sem("at_done")
        down_done = sem("down_done")
        sel_step = sem("sel_step")
        r2_mom = sem("r2_mom")
        r2_rstd = sem("r2_rstd")
        x2_done = sem("x2_done")
        x2turn_done = sem("x2turn_done")
        x2t_done = sem("x2t_done")
        gate_done = sem("gate_done")
        masks_step = sem("masks_step")
        route_step = sem("route_step")
        chosen_done = sem("chosen_done")
        seen_done = sem("seen_done")
        rank_done = sem("rank_done")
        place_done = sem("place_done")
        place_step = sem("place_step")
        stats_done = sem("stats_done")
        eps_added = sem("eps_added")
        slot_done = sem("slot_done")
        scattered = sem("scattered")
        s_xturn_done = sem("s_xturn_done")
        s_xt_done = sem("s_xt_done")
        s_gu_done = sem("s_gu_done")
        s_silu_done = sem("s_silu_done")
        s_act_done = sem("s_act_done")
        s_turn_done = sem("s_turn_done")
        s_actt_done = sem("s_actt_done")
        s_down_done = sem("s_down_done")
        s_sum_done = sem("s_sum_done")
        count_done = sem("count_done")
        plan_step = sem("plan_step")
        plan_done = sem("plan_done")
        soft_step = sem("soft_step")
        soft_shift = sem("soft_shift")
        soft_exp = sem("soft_exp")
        weight_done = sem("weight_done")
        e_turn_done = sem("e_turn_done")
        e_xt_done = sem("e_xt_done")
        e_xt_low_done = sem("e_xt_low_done")
        s_xt_low_done = sem("s_xt_low_done")
        gu_squared = sem("gu_squared")
        gu_norm_done = sem("gu_norm_done")
        gu_inverse_done = sem("gu_inverse_done")
        gu_scale_step = sem("gu_scale_step")
        gu_scale_summed = sem("gu_scale_summed")
        gu_high_done = sem("gu_high_done")
        gu_low_done = sem("gu_low_done")
        gu_kept = sem("gu_kept")
        e_gu_done = sem("e_gu_done")
        e_silu_done = sem("e_silu_done")
        e_act_done = sem("e_act_done")
        e_aturn_done = sem("e_aturn_done")
        e_actt_done = sem("e_actt_done")
        e_down_done = sem("e_down_done")
        e_y_done = sem("e_y_done")
        mix_weight_made = sem("mix_weight_made")
        mix_done = sem("mix_done")
        mix_sum_done = sem("mix_sum_done")
        r3_mom = sem("r3_mom")
        r3_rstd = sem("r3_rstd")
        fin_done = sem("fin_done")
        x2_stored = [sem(f"x2_stored{r}") for r in range(2)]
        idx_in = [sem(f"idx_in{r}") for r in range(IS)]
        xs_in = [sem(f"xs_in{r}") for r in range(XR)]
        y_stored = [sem(f"y_stored{r}") for r in range(YR)]
        back_in = [sem(f"back_in{r}") for r in range(TILES)]
        fin_stored = [sem(f"fin_stored{r}") for r in range(2)]

        LATE = 4

        def core_order(b, tail=()):
            for h in range(HEADS + 6):
                for behind, step in enumerate(("scores", "exp", None, "turn", "low", "values", "out")):
                    if step and 0 <= h - behind < HEADS:
                        yield step, b, h - behind
                yield from (step for at, step in tail if at == h)

        def back_tail(b):
            tail = [(0, ("rank", b, 0)), (1, ("rank", b, 1))] if b >= 0 else []
            return tail + [(4 + 2 * part, ("gu_scale", 0, part)) for part in range(4)] if b == 0 else tail

        def front_tail(b):
            return [(HEADS, ("qkv", b, 0)), (HEADS, ("qkv", b, 1)), (HEADS + 2, ("norm", b, 0)),
                    (HEADS + 3, ("oturn", b - 1, (0, 0))), (HEADS + 5, ("norm", b, 1))]

        def qproj_order(b):
            groups = [(j, g) for j in range(TPB) for g in range(GROUPS)]
            return [("qproj", b, jg) for jg in groups], [("qturn", b, jg) for jg in groups]

        SPLIT, HALF_SPLIT = "split", (EXPERTS + SHARED) // 2

        def back_and_front(b):
            q, t = qproj_order(b + 1)
            yield from (("fturn", b + 1, 0), ("oturn", b, (0, 1)), SPLIT, SPLIT, ("oproj", b, 0),
                        ("oturn", b, (1, 0)), ("fturn", b + 1, 1), SPLIT, ("oturn", b, (1, 1)), q[0],
                        SPLIT, ("oproj", b, 1), ("x1", b, 0), SPLIT, q[1], SPLIT, ("x1turn", b, 0),
                        ("x1", b, 1), SPLIT, t[0], q[2], SPLIT, t[1], SPLIT, ("x1turn", b, 1),
                        ("up", b, 0), SPLIT, ("act", b, 0), SPLIT, q[3], SPLIT, t[2], ("up", b, 1),
                        ("aturn", b, 0), SPLIT, q[4], ("act", b, 1), SPLIT, t[3], SPLIT, ("down", b, 0),
                        ("aturn", b, 1), SPLIT, t[4], q[5], SPLIT, ("x2", b, 0), SPLIT, ("down", b, 1),
                        t[5], ("x2turn", b, 0), q[6], q[7], ("x2", b, 1), ("gate", b, 0), t[6],
                        ("x2turn", b, 1), t[7], ("gate", b, 1))

        def with_split(b, steps):
            if b == 0:
                extra = iter([("gu_square", 0, i) for i in range(EXPERTS + SHARED)])
            else:
                begin, end = (b - 1) * HALF_SPLIT, b * HALF_SPLIT
                highs = [("gu_high", 0, i) for i in range(begin, end)]
                lows = [("gu_low", 0, i) for i in range(begin, end)]
                extra = iter([highs[0], *(step for pair in zip(highs[1:], lows) for step in pair), lows[-1]])
            for step in steps:
                yield next(extra) if step == SPLIT else step

        def shared_order():
            for n in range(TILES + 1):
                if n == 0:
                    yield "s_turn", 0, 0
                if n < TILES:
                    yield "s_gate_up", 0, n
                    if n + 1 < TILES:
                        yield "s_turn", 0, n + 1
                if n >= 1:
                    yield "s_down", 0, n - 1
                if n < TILES:
                    yield "s_act_turn", 0, n

        def last_back(b):
            back = (("oturn", (0, 1)), 1, ("oproj", 0), ("oturn", (1, 0)), ("oturn", (1, 1)),
                    ("oproj", 1), ("x1", 0), 2, ("x1turn", 0), ("x1", 1), ("up", 0), 1, ("x1turn", 1),
                    1, ("act", 0), ("up", 1), ("aturn", 0), 1, ("act", 1), 1, ("down", 0), 1,
                    ("aturn", 1), 2, ("x2", 0), ("down", 1), 1, ("x2turn", 0), 1, ("x2", 1),
                    ("gate", 0), 1, ("x2turn", 1), ("rank", 0), 1, ("gate", 1), 2, ("rank", 1),
                    ("count", 0), 1, ("plan", 0), 2, ("plan", 1), ("prepare", 0), 3, ("weights", 0))
            shared = list(shared_order())
            for step in back:
                if isinstance(step, int):
                    yield from shared[:step]
                    del shared[:step]
                else:
                    yield step[0], b, step[1]
            yield from shared[:-LATE]

        def order():
            yield from (("qkv", 0, 0), ("qkv", 0, 1), ("norm", 0, 0), ("norm", 0, 1), ("absorb_q", 0, 0),
                        ("fturn", 0, 0), ("fturn", 0, 1))
            q, t = qproj_order(0)
            for i in range(len(q) + 2):
                yield from q[i:i + 1]
                if i == len(q):
                    yield "absorb_o", 0, 0
                if i >= 2:
                    yield t[i - 2]
            yield "keep_o", 0, 0
            for b in range(BATCH):
                if b + 1 < BATCH:
                    yield from core_order(b, back_tail(b - 1) + front_tail(b + 1))
                    yield from with_split(b, back_and_front(b))
                else:
                    yield from core_order(b, back_tail(b - 1) + [(HEADS + 3, ("oturn", b, (0, 0)))])
                    yield from last_back(b)
            for s in range(SLOT_TILES + 3):
                for behind, stage in enumerate(("e_turn", "e_gate_up", "e_act_turn", "e_down")):
                    if 0 <= s - behind < SLOT_TILES:
                        yield stage, 0, s - behind
                if s % 5 == 4 and s // 5 < TILES:
                    yield "diagonals", 0, s // 5
            yield "back", 0, 0
            yield from list(shared_order())[-LATE:]
            for n in range(TILES + 1):
                if n < TILES:
                    yield "mix", 0, n
                if n >= 1:
                    yield "fin", 0, n - 1

        IDX_AHEAD, X_AHEAD = 7, 4
        ORDER = list(order())

        def run(steps):
            for name, b, i in ORDER:
                if name in steps:
                    steps[name](b, i)

        block = ctx.enter_context(nc.Block())

        @block.sync
        def _(sp):
            xt_v = xT.rearrange("(c p) t -> p c t", p=P)
            sp.dma_start(x_t[:, :, :], xt_v[:, :, 0:SEQ]).then_inc(in_xt, 16)
            sp.dma_start(w_qkv[:, :, :], wqkvT.rearrange("(c p) n -> p c n", p=P)).then_inc(in_wqkv, 16)
            sp.dma_start(w_qn[:, :], qlnw.partition_broadcast(P)).then_inc(in_norms, 16)
            sp.dma_start(w_kn[:, :], kvlnw.partition_broadcast(P)).then_inc(in_norms, 16)
            sp.dma_start(cos[:, :, :], cosT.rearrange("(j p) r -> p j r", p=P)).then_inc(in_rope, 16)
            sp.dma_start(sin[:, :, :], sinT.rearrange("(j p) r -> p j r", p=P)).then_inc(in_rope, 16)
            kvb_v = kvb.rearrange("(h t p) r -> p h t r", h=HEADS, t=2)
            for half in range(2):
                heads = slice(half * HEADS // 2, (half + 1) * HEADS // 2)
                sp.dma_start(raw_q[:, heads], qnope.rearrange("h p r -> p h r")[:, heads]).then_inc(in_rawqk[half], 16)
                sp.dma_start(raw_kv[:, heads, 0], kvb_v[:, heads, 0]).then_inc(in_rawqk[half], 16)
            qpe_v = qpeT.rearrange("(c p) h r -> p c h r", p=QC)
            for c in range(2):
                sp.dma_start(w_q[:, c, :, KR:HD], qpe_v[:, c]).then_inc(in_wpe, 16)
            sp.wait_ge(const_made, 2)
            for a, blocks in enumerate((P, BLOCKS - P)):
                sp.dma_start(table[a * P * P:(a * P + blocks) * P, :].rearrange("(b n) o -> b n o", n=P),
                             table_init[0:blocks, a]).then_inc(table_filled, 16)
            sp.dma_start(raw_kv[:, :, 1], kvb_v[:, :, 1]).then_inc(in_rawv, 16)
            for half in range(2):
                sp.dma_start(w_kn_column[half * KR:(half + 1) * KR, :],
                             kvlnw.rearrange("(r o) -> r o", o=1)).then_inc(in_rawv, 16)
            sp.dma_start(raw_o, woT.rearrange("(h p) d -> p h d", p=P)).then_inc(in_rawo, 16)
            sp.dma_start(rows[:, :, :], x.rearrange("(n p) d -> p n d", p=P)).then_inc(in_x, 16)
            sp.dma_start(ids_i[:, :], ids).then_inc(in_ids, 16)
            sp.dma_start(w_ctx[:, :, :], ctxT.rearrange("(c p) n -> p c n", p=P)).then_inc(in_wctx, 16)
            sp.dma_start(w_gate[:, :, :], wgateT.rearrange("(c p) n -> p c n", p=P)).then_inc(in_wgate, 16)
            sp.dma_start(w_gu[:, :, :, :], wgu.rearrange("(c p) e n -> p c e n", p=P)).then_inc(in_wgu, 16)
            sp.wait_ge(absorbed_o, 1)
            sp.dma_start(w_down, wd.rearrange("e (c p) d -> p e c d", p=HALF)).then_inc(in_wdown, 16)

            def next_x(b, h):
                if h == 0 and b + 1 < BATCH:
                    sp.wait_ge(qkv_done, TPB * (b + 1))
                    sp.dma_start(x_t[:, :, :], xt_v[:, :, (b + 1) * SEQ:(b + 2) * SEQ]).then_inc(in_xt, 16)

            def x2_store(b, j):
                n = TPB * b + j
                sp.wait_ge(x2_done, n + 1)
                if n >= 2:
                    sp.wait_ge(x2_stored[n % 2], 16 * (n // 2))
                sp.dma_start(x2_dram[n * P:(n + 1) * P, :], rows[:, n, :]).then_inc(x2_stored[n % 2], 16)

            def plan(b, i):
                sp.wait_ge(plan_done, 2)
                sp.wait_ge(scattered, 16 * TILES * TOPK)
                for s in range(IDX_AHEAD):
                    idx_load(s)

            def idx_load(s):
                if s >= SLOT_TILES:
                    return
                if s >= IR:
                    used = s - IR
                    sp.wait_ge(y_stored[used % YR], 16 * (used // YR + 1))
                if s >= IS:
                    sp.wait_ge(xs_in[(s - IS) % XR], 16 * ((s - IS) // XR + 1))
                block_no = sp.value_load(tile_block[s:s + 1, 0:1], min_val=0, max_val=BLOCKS - 1)
                sp.dma_start(idx[:, s % IR, :], table[bass.ds(block_no * P, P), :]).then_inc(idx_in[s % IS], 16)

            def e_turn(b, s):
                idx_load(s + IDX_AHEAD)

            def results_back(b, i):
                for r in range(YR):
                    sp.wait_ge(y_stored[r], 16 * len(range(r, SLOT_TILES, YR)))
                for n in range(TILES):
                    sp.dma_start(back[:, n], y_dram[n * P * TOPK:(n + 1) * P * TOPK, :]
                                 .rearrange("(p k) d -> p k d", k=TOPK)).then_inc(back_in[n], 16)

            def store(b, n):
                sp.wait_ge(fin_done, n + 1)
                sp.dma_start(out[n * P:(n + 1) * P, :], fin[:, n % 2, :]).then_inc(fin_stored[n % 2], 16)

            run({"scores": next_x, "x2": x2_store, "prepare": plan, "e_turn": e_turn, "back": results_back, "fin": store})
            for r in range(2):
                sp.wait_ge(fin_stored[r], 16 * TILES // 2)

        @block.gpsimd
        def _(pool):
            def first_constants():
                pool.memset(minus_half[:, :], -0.5).then_inc(eye_made, 1)
                pool.memset(ident[:, :], 0.0).then_inc(eye_made, 1)
                pool.wait_ge(eye_made, 2)
                pool.affine_select(out=ident[:, :], in_=ident[:, :], compare_op=ALU.not_equal, fill=1.0,
                                   base=0, pattern=[[-1, P]], channel_multiplier=1).then_inc(eye_made, 1)
                for v, dst in ((1.0, v_hi), (0.0, v_lo)):
                    pool.memset(dst[:, :, KR:KR + 2], v).then_inc(eye_made, 1)
                pool.memset(table_init[:, :, :, 0], 0).then_inc(const_made, 1)
                pool.iota(table_init[:, :, :, 1], pattern=[[P * P, 2], [1, P]], base=TOKENS * TOPK,
                          channel_multiplier=P).then_inc(const_made, 1)

            def constants(b, i):
                pool.wait_ge(eye_made, EYES)
                pool.tensor_copy(ident16[:, :], ident[:, :]).then_inc(masks_made, 1)
                pool.memset(causal[:, :], 0.0).then_inc(masks_made, 1)
                pool.memset(ones[:, :], 1.0).then_inc(masks_made, 1)
                pool.memset(before[:, :, :], 1.0).then_inc(masks_made, 1)
                pool.wait_ge(masks_made, 4)
                pool.affine_select(out=causal[:, :], in_=causal[:, :], compare_op=ALU.is_ge, fill=MASKED,
                                   base=0, pattern=[[-1, P]], channel_multiplier=1).then_inc(masks_made, 1)
                pool.affine_select(out=earlier[:, :], in_=ones[:, :], compare_op=ALU.is_gt, fill=0.0,
                                   base=0, pattern=[[1, P]], channel_multiplier=-1).then_inc(masks_made, 1)
                pool.affine_select(out=before[:, :, :], in_=before[:, :, :], compare_op=ALU.is_gt, fill=0.0,
                                   base=0, pattern=[[1, EXPERTS], [-1, EXPERTS]],
                                   channel_multiplier=0).then_inc(masks_made, 1)
                pool.memset(seen[:, 0, :], 0.0).then_inc(masks_made, 1)
                pool.memset(step_up[:, 0:1], 0.0).then_inc(masks_made, 1)
                for dst, pattern in ((iota16, [[1, EXPERTS]]), (region, [[TOKENS, EXPERTS]]),
                                     (tile_starts, [[P, TILES]])):
                    pool.iota(dst[:, :], pattern=pattern, base=0, channel_multiplier=0,
                              allow_small_or_imprecise_dtypes=True).then_inc(masks_made, 1)
                pool.iota(slot_iota[:, :], pattern=[[0, 1]], base=0, channel_multiplier=1,
                          allow_small_or_imprecise_dtypes=True).then_inc(masks_made, 1)
                pool.iota(token_pair[:, :, :, 0], pattern=[[P, TILES], [0, TOPK]], base=0,
                          channel_multiplier=1).then_inc(masks_made, 1)
                pool.iota(token_pair[:, :, :, 1], pattern=[[P * TOPK, TILES], [1, TOPK]], base=0,
                          channel_multiplier=TOPK).then_inc(masks_made, 1)

            def rms_of(b, i):
                if i == 0:
                    pool.wait_ge(ssq_done, 4 * (b + 1))
                    if 2 * b > 0:
                        pool.wait_ge(qn_done, 2 * b)
                    if 2 * b > 0:
                        pool.wait_ge(kvc_done, 2 * b)
                    pool.tensor_scalar(ssq_eps[:, :], ssq[:, :], RMS_EPS, None, ALU.add).then_inc(rms_eps_done, 1)
                    pool.wait_ge(rms_eps_done, b + 1)
                    pool.tensor_tensor(rms[:, :], ssq_eps[:, :], minus_half[:, :], ALU.pow).then_inc(rms_done, 1)
                n = TPB * b + i
                pool.wait_ge(kvc_done, n + 1)
                if HEADS * b > 0:
                    pool.wait_ge(pv_done, HEADS * b)
                pool.tensor_copy(v_hi[:, i, 0:KR], kv_row[:, i, 0:KR]).then_inc(vhi_done, 1)
                pool.wait_ge(vhi_done, n + 1)
                pool.tensor_tensor(v_lo[:, i, 0:KR], kv_row[:, i, 0:KR], v_hi[:, i, 0:KR],
                                   ALU.subtract).then_inc(vlo_done, 1)

            def q_rotary(b, jg):
                j, g = jg
                i = GROUPS * (TPB * b + j) + g
                pool.wait_ge(qrope_done, i + 1)
                if i + 1 - TPB * GROUPS > 0:
                    pool.wait_ge(qturn_done, i + 1 - TPB * GROUPS)
                pool.tensor_tensor(q_row[:, j, QG * g:QG * g + QG, KR:HD], q_cos[:, i % 2], q_sin[:, i % 2],
                                   ALU.add).then_inc(qrow_done, 1)

            rstds = [0]

            def rstd_of(mom, inverse, j, n):
                rstds[0] += 1
                pool.wait_ge(mom, n + 1)
                pool.tensor_scalar(var_eps[:, j, :], moments[:, j, 1:2], LN_EPS, None, ALU.add)\
                    .then_inc(eps_added, 1)
                pool.wait_ge(eps_added, rstds[0])
                pool.tensor_tensor(rstd[:, j, :], var_eps[:, j, :], minus_half[:, 0:1], ALU.pow)\
                    .then_inc(inverse, 1)

            def route(b, j):
                n = TPB * b + j
                pool.wait_ge(slot_done, n + 1)
                pool.wait_ge(table_filled, 32)
                for k in range(TOPK):
                    pool.indirect_dma_start(out=table, out_offset=bass.IndirectOffsetOnAxis(ap=slot[:, n, k:k + 1], axis=0),
                                            in_=token_pair[:, n, k, :], in_offset=None).then_inc(scattered, 16)

            def gu_scale_pool(b, part):
                if part == 2:
                    pool.wait_ge(gu_norm_done, 2)
                    pool.tensor_tensor(gu_inverse[:, :], gu_norm[:, :], minus_half[:, 0:1], ALU.pow)\
                        .then_inc(gu_inverse_done, 1)

            def gather_x(s):
                if s >= SLOT_TILES:
                    return
                if s == 0:
                    for r in range(2):
                        pool.wait_ge(x2_stored[r], 16 * TILES // 2)
                pool.wait_ge(idx_in[s % IS], 16 * (s // IS + 1))
                if s >= XR:
                    pool.wait_ge(e_turn_done, s - XR + 1)
                pool.indirect_dma_start(out=xs[:, s % XR, :], out_offset=None, in_=x2_dram,
                                        in_offset=bass.IndirectOffsetOnAxis(ap=idx[:, s % IR, 0:1], axis=0))\
                    .then_inc(xs_in[s % XR], 16)

            def plan(b, i):
                for s in range(X_AHEAD):
                    gather_x(s)

            def e_turn(b, s):
                gather_x(s + X_AHEAD)

            def scatter_y(b, s):
                pool.wait_ge(e_y_done, s + 1)
                pool.indirect_dma_start(out=y_dram, out_offset=bass.IndirectOffsetOnAxis(ap=idx[:, s % IR, 1:2], axis=0),
                                        in_=ys[:, s % YR, :], in_offset=None).then_inc(y_stored[s % YR], 16)

            first_constants()
            run({"norm": rms_of, "absorb_q": constants, "qproj": q_rotary,
                 "oproj": lambda b, j: rstd_of(r1_mom, r1_rstd, j, TPB * b + j),
                 "down": lambda b, j: rstd_of(r2_mom, r2_rstd, j, TPB * b + j),
                 "rank": route, "prepare": plan, "e_turn": e_turn, "e_down": scatter_y,
                 "gu_scale": gu_scale_pool,
                 "mix": lambda b, n: rstd_of(r3_mom, r3_rstd, n % 2, n)})

        @block.scalar
        def _(act):
            def mean_squares(b, j):
                n = TPB * b + j
                act.wait_ge(qkv_done, n + 1)
                if b > 0:
                    act.wait_ge(rms_eps_done, b)
                for k, (at, w) in enumerate(((0, QR), (QR, KR))):
                    act.activation(act_junk[:, j, at:at + w], bank[1 + j][:, at:at + w], ACT.Square, scale=float(w) ** -0.5,
                                   accum_out=ssq[:, 2 * j + k:2 * j + k + 1]).then_inc(ssq_done, 1)

            def latents_t(b, j):
                n = TPB * b + j
                act.wait_ge(fturn_done, n + 1)
                if TPB * GROUPS * b > 0:
                    act.wait_ge(qproj_done, TPB * GROUPS * b)
                if HEADS * b > 0:
                    act.wait_ge(scores_done, HEADS * b)
                turned = bank[3 - j][0:QC, 0:2 * P].rearrange("p (c t) -> p c t", c=2)
                act.activation(qn_t[:, :, j * P:(j + 1) * P], turned, ACT.Copy).then_inc(fevac_done, 1)
                act.activation(k_t[:, j * P:(j + 1) * P], bank[3 - j][:, 2 * P:3 * P], ACT.Copy).then_inc(fevac_done, 1)

            def keep_o(b, i):
                act.wait_ge(in_rawv, 48)
                act.wait_ge(absorbed_o, 1)
                for k in range(4):
                    act.activation(w_out[:, 2 * k:2 * k + 2, :], bank[4 + k][:, :].rearrange("p (h d) -> p h d", h=2),
                                   ACT.Copy, scale=w_kn_column[:, 0:1]).then_inc(absorbed_o_kept, 1)

            def q_absorbed(b, jg):
                j, g = jg
                i = GROUPS * (TPB * b + j) + g
                act.wait_ge(qrope_done, i + 1)
                if i + 1 - TPB * GROUPS > 0:
                    act.wait_ge(qturn_done, i + 1 - TPB * GROUPS)
                act.activation(q_row[:, j, QG * g:QG * g + QG, 0:KR], bank[g % 2][:, :].rearrange("p (h d) -> p h d", h=QG)[:, :, 0:KR], ACT.Copy).then_inc(abs_done, 1)

            def q_turned(b, jg):
                j, g = jg
                i = GROUPS * (TPB * b + j) + g
                act.wait_ge(qturn_done, i + 1)
                if i == 0:
                    act.wait_ge(table_filled, 32)
                if HEADS * b > 0:
                    act.wait_ge(scores_done, HEADS * b)
                act.activation(q_t[:, QG * g:QG * g + QG, j * P:(j + 1) * P], bank[2 + g % 2][:, :].rearrange("p (h t) -> p h t", h=QG), ACT.Copy).then_inc(qt_done, 1)

            def exps(b, h):
                n = HEADS * b + h
                act.wait_ge(max_done, 2 * n + 2)
                if n - 2 > 0:
                    act.wait_ge(pturn_done, n - 2)
                if TPB * b > 0:
                    act.wait_ge(oproj_done, 2 * TPB * b)
                for q, (at, w) in enumerate(((0, P), (P, 2 * P))):
                    act.activation(probs[:, n % 3, at:at + w], bank[h % 3][:, at:at + w], ACT.Exp,
                                   bias=neg_max[:, n % 3, q:q + 1]).then_inc(exp_done, 1)

            def probs_hi(b, h):
                n = HEADS * b + h
                act.wait_ge(pturn_done, n + 1)
                if n - 2 > 0:
                    act.wait_ge(pv_done, n - 2)
                act.activation(p_hi[:, n % 3, :], bank[3 + h % 2][:, 0:3 * P], ACT.Copy).then_inc(phi_done, 1)

            def o_turned(b, jh):
                j, half = jh
                n = TPB * b + j
                act.wait_ge(oturn_done, 2 * n + half + 1)
                if n > 0:
                    act.wait_ge(oproj_done, 2 * (n - 1) + half + 1)
                act.activation(o_t[:, 4 * half:4 * half + 4, :], bank[7 - 3 * half][:, :].rearrange("p (c t) -> p c t", c=4), ACT.Copy).then_inc(ot_done, 1)

            def turned_back(j, n, turn_done, used, done, used_n):
                act.wait_ge(turn_done, n + 1)
                if used_n > 0:
                    act.wait_ge(used, used_n)
                act.activation(turned[:, j], bank[4 + j][:, 0:D].rearrange("p (c t) -> p c t", c=DC), ACT.Copy)\
                    .then_inc(done, 1)

            def x1_turned(b, j):
                n = TPB * b + j
                turned_back(j, n, x1turn_done, gate_done, x1t_done, n - 1)

            def gate_act(b, j):
                n = TPB * b + j
                act.wait_ge(pick_step, CTX * (n + 1))
                if n - 1 > 0:
                    act.wait_ge(a_done, n - 1)
                act.activation(gated[:, j, :], picked[:, j, :], ACT.Silu).then_inc(silu_done, 1)

            def a_turned(b, j):
                n = TPB * b + j
                turned_back(j, n, aturn_done, up_done, at_done, n + 1)

            def x2_turned(b, j):
                n = TPB * b + j
                turned_back(j, n, x2turn_done, down_done, x2t_done, n + 1)

            def gu_square(b, e):
                act.wait_ge(in_wgu, 16)
                if e > 0:
                    act.wait_ge(gu_squared, e)
                act.activation(gu_temp[:, 0].bitcast(BF16), w_gu[:, :, e, :], ACT.Square,
                               accum_out=gu_squares[:, e:e + 1]).then_inc(gu_squared, 1)

            def gu_high(b, i):
                e = (i + EXPERTS) % (EXPERTS + SHARED)
                if i == 0:
                    act.wait_ge(gu_scale_step, 4)
                if i >= 2:
                    act.wait_ge(gu_kept, i - 1)
                act.activation(gu_temp[:, i % 2], w_gu[:, :, e, :], ACT.Copy, scale=gu_scale[:, 0:1])\
                    .then_inc(gu_high_done, 1)

            def s_turn(b, n):
                act.wait_ge(s_xturn_done, n + 1)
                if n > 0:
                    act.wait_ge(s_gu_done, 2 * n)
                act.activation(s_xt[:, 0], bank[3][:, 0:D].rearrange("p (c t) -> p c t", c=DC), ACT.Copy).then_inc(s_xt_done, 1)

            def s_gate_up(b, n):
                for s in range(SHARED):
                    act.wait_ge(s_gu_done, 2 * n + s + 1)
                    if n > 0:
                        act.wait_ge(s_act_done, 2 * n + s - 1)
                    act.activation(s_gate[:, s, :], bank[s][:, 0:INNER], ACT.Silu, scale=gu_scale[:, 1:2]).then_inc(s_silu_done, 1)

            def s_act_turn(b, n):
                act.wait_ge(s_turn_done, n + 1)
                if n > 0:
                    act.wait_ge(s_down_done, n)
                act.activation(s_act_t, bank[3][0:HALF, :].rearrange("p (s c t) -> p s c t", s=2, c=2), ACT.Copy).then_inc(s_actt_done, 1)

            def weights(b, i):
                act.wait_ge(soft_shift, 1)
                act.activation(shifted[:, :, :], shifted[:, :, :], ACT.Exp).then_inc(soft_exp, 1)
                act.wait_ge(soft_shift, 2)
                act.activation(soft_top[:, :, :], soft_top[:, :, :], ACT.Exp).then_inc(soft_exp, 1)

            def e_turn(b, s):
                act.wait_ge(e_turn_done, s + 1)
                if s - 1 > 0:
                    act.wait_ge(e_gu_done, s - 1)
                act.activation(e_xt[:, s % 2, 0], bank[s % 2][:, 0:D].rearrange("p (c t) -> p c t", c=DC), ACT.Copy).then_inc(e_xt_done, 1)

            def e_gate_up(b, s):
                act.wait_ge(e_gu_done, s + 1)
                if s - 1 > 0:
                    act.wait_ge(e_act_done, s - 1)
                act.activation(e_gate[:, s % 2, :], bank[2 + s % 2][:, 0:INNER], ACT.Silu, scale=gu_scale[:, 1:2]).then_inc(e_silu_done, 1)

            def e_down(b, s):
                act.wait_ge(e_down_done, s + 1)
                if s >= YR:
                    act.wait_ge(y_stored[s % YR], 16 * (s // YR))
                act.activation(ys[:, s % YR, :], bank[6 + s % 2][:, 0:D], ACT.Copy).then_inc(e_y_done, 1)

            def diagonals(b, n):
                if n == 0:
                    act.wait_ge(weight_done, 1)
                for k in range(TOPK):
                    act.activation(mix_weight[:, n, k, :], ident[:, :], ACT.Copy, scale=weight[:, n, k:k + 1])\
                        .then_inc(mix_weight_made, 1)

            run({"qkv": mean_squares, "fturn": latents_t, "keep_o": keep_o, "qproj": q_absorbed, "qturn": q_turned,
                 "exp": exps, "turn": probs_hi, "oturn": o_turned, "x1turn": x1_turned, "act": gate_act,
                 "aturn": a_turned, "x2turn": x2_turned, "s_turn": s_turn, "s_gate_up": s_gate_up,
                 "s_act_turn": s_act_turn, "gu_square": gu_square, "gu_high": gu_high, "weights": weights, "e_turn": e_turn, "e_gate_up": e_gate_up,
                 "e_down": e_down, "diagonals": diagonals})

        @block.tensor
        def _(pe):
            def qkv(b, j):
                n = TPB * b + j
                pe.wait_ge(in_xt, 16 * (b + 1))
                if b == 0:
                    pe.wait_ge(in_wqkv, 16)
                if b > 0:
                    pe.wait_ge(exp_done, 2 * (HEADS * b - 2 + j))
                for c in range(DC):
                    mm = pe.matmul(bank[1 + j][:, 0:QR + HD], x_t[:, c, j * P:(j + 1) * P], w_qkv[:, c, :],
                                   start=(c == 0), stop=(c == DC - 1))
                mm.then_inc(qkv_done, 1)

            def latents_turn(b, j):
                n = TPB * b + j
                if n == 0:
                    pe.wait_ge(eye_made, EYES)
                pe.wait_ge(qn_done, n + 1)
                pe.wait_ge(kv_done, n + 1)
                if HEADS * b > 0:
                    pe.wait_ge(phi_done, HEADS * b)
                if HEADS * b > 0:
                    pe.wait_ge(plo_done, HEADS * b)
                for c in range(2):
                    pe.transpose(bank[3 - j][0:QC, c * P:(c + 1) * P], qn[:, j, c * QC:(c + 1) * QC], ident[:, :])
                pe.transpose(bank[3 - j][:, 2 * P:3 * P], kv_row[:, j, :], ident[:, :]).then_inc(fturn_done, 1)

            def absorb_q(b, i):
                for half in range(2):
                    pe.wait_ge(in_rawqk[half], 32)
                    for c in range(2):
                        for h in range(8):
                            mm = pe.matmul(bank[4 + 2 * half + c][0:QC, h * KR:(h + 1) * KR],
                                           raw_q[:, 8 * half + h, c * QC:(c + 1) * QC], raw_kv[:, 8 * half + h, 0, :],
                                           start=True, stop=True)
                        mm.then_inc(absorbed_q, 1)

            def absorb_o(b, i):
                pe.wait_ge(in_rawo, 16)
                pe.wait_ge(in_rawv, 48)
                pe.wait_ge(absorbed_q_kept, 4)
                for h in range(HEADS):
                    at = KR * (h % 2)
                    mm = pe.matmul(bank[4 + h // 4][at:at + KR, (h // 2 % 2) * D:(h // 2 % 2 + 1) * D],
                                   raw_kv[:, h, 1, :], raw_o[:, h, :], start=True, stop=True)
                mm.then_inc(absorbed_o, 1)

            def qproj(b, jg):
                j, g = jg
                n = TPB * b + j
                i = GROUPS * n + g
                pe.wait_ge(fevac_done, 2 * n + 2)
                if i == 0:
                    pe.wait_ge(absorbed_q_kept, 4)
                    pe.wait_ge(in_wpe, 32)
                if i % (TPB * GROUPS) == 0 and b > 0:
                    pe.wait_ge(exp_done, 2 * HEADS * b)
                if i % (TPB * GROUPS) < 2:
                    pe.wait_ge(krope_done, 3 * TPB * b + 3)
                if i - 1 > 0:
                    pe.wait_ge(abs_done, i - 1)
                for c in range(2):
                    mm = pe.matmul(bank[g % 2][:, :], qn_t[:, c, j * P:(j + 1) * P],
                                   w_q[:, c, QG * g:QG * g + QG, :], start=(c == 0), stop=(c == 1))
                mm.then_inc(qproj_done, 1)

            def qturn(b, jg):
                j, g = jg
                n = TPB * b + j
                i = GROUPS * n + g
                pe.wait_ge(abs_done, i + 1)
                pe.wait_ge(qrow_done, i + 1)
                if i % (TPB * GROUPS) < 2:
                    pe.wait_ge(fevac_done, 2 * TPB * (b + 1))
                if i - 1 > 0:
                    pe.wait_ge(qt_done, i - 1)
                for k in range(QG):
                    mm = pe.transpose(bank[2 + g % 2][:, k * P:(k + 1) * P], q_row[:, j, QG * g + k, :], ident[:, :])
                mm.then_inc(qturn_done, 1)

            def scores(b, h):
                n = HEADS * b + h
                s = bank[h % 3]
                if h == 0:
                    pe.wait_ge(masks_made, MASKS)
                    pe.wait_ge(qt_done, TPB * GROUPS * (b + 1))
                    pe.wait_ge(fevac_done, 2 * TPB * (b + 1))
                else:
                    if 2 * (n - 2) > 0:
                        pe.wait_ge(exp_done, 2 * (n - 2))
                pe.matmul(s[:, 0:P], q_t[:, h, 0:P], k_t[:, 0:P], start=True, stop=False)
                pe.matmul(s[:, 0:P], ident16[:, :], causal[:, :], start=False, stop=True)
                pe.matmul(s[:, P:3 * P], q_t[:, h, P:2 * P], k_t[:, :], start=True, stop=False)
                pe.matmul(s[:, 2 * P:3 * P], ident16[:, :], causal[:, :], start=False, stop=True)\
                    .then_inc(scores_done, 1)

            def turn(b, h):
                n = HEADS * b + h
                pe.wait_ge(exp_done, 2 * n + 2)
                if h == 0:
                    if TPB * b > 0:
                        pe.wait_ge(place_done, TPB * b)
                if n - 1 > 0:
                    pe.wait_ge(plo_done, n - 1)
                for k in range(3):
                    mm = pe.transpose(bank[3 + h % 2][:, k * P:(k + 1) * P], probs[:, n % 3, k * P:(k + 1) * P],
                                      ident[:, :])
                mm.then_inc(pturn_done, 1)

            def values(b, h):
                n = HEADS * b + h
                pe.wait_ge(phi_done, n + 1)
                pe.wait_ge(plo_done, n + 1)
                pe.wait_ge(vlo_done, TPB * (b + 1))
                if h % 2 == 0:
                    if n // 2 - 1 > 0:
                        pe.wait_ge(onorm_done, n // 2 - 1)
                o = bank[5 + (h // 2) % 2]
                for q, blocks in enumerate(((0,), (1, 2))):
                    at = (2 * (h % 2) + q) * (KR + 1)
                    parts = [(pp, vv, k) for k in blocks for pp, vv in ((p_hi, v_hi), (p_hi, v_lo), (p_lo, v_hi))]
                    for i, (pp, vv, k) in enumerate(parts):
                        mm = pe.matmul(o[:, at:at + KR + 1], pp[:, n % 3, k * P:(k + 1) * P],
                                       vv[:, k // 2, 0:KR + 1], start=(i == 0), stop=(i == len(parts) - 1))
                mm.then_inc(pv_done, 1)

            def oturn(b, jh):
                j, half = jh
                n = TPB * b + j
                pe.wait_ge(onorm_done, HEADS // 2 * b + HEADS // 4 * (half + 1))
                if half == 1:
                    pe.wait_ge(plo_done, HEADS * (b + 1))
                if 2 * n + half - 1 > 0:
                    pe.wait_ge(ot_done, 2 * n + half - 1)
                for k in range(4):
                    at = (4 * half + k) * P
                    mm = pe.transpose(bank[7 - 3 * half][:, k * P:(k + 1) * P], o_row[:, j, at:at + P], ident[:, :])
                mm.then_inc(oturn_done, 1)

            def oproj(b, j):
                n = TPB * b + j
                if n == 0:
                    pe.wait_ge(absorbed_o_kept, 4)
                for half in range(2):
                    pe.wait_ge(ot_done, 2 * n + half + 1)
                    for c in range(4 * half, 4 * half + 4):
                        mm = pe.matmul(bank[5 + j][:, 0:D], o_t[:, c, :], w_out[:, c, :],
                                       start=(c == 0), stop=(c == HEADS // 2 - 1))
                    mm.then_inc(oproj_done, 1)

            def turn2(src, j, done):
                for c in range(DC):
                    mm = pe.transpose(bank[4 + j][:, c * P:(c + 1) * P], src[:, c * P:(c + 1) * P], ident[:, :])
                mm.then_inc(done, 1)

            def ctx_product(src_t, j, done):
                for half in range(2):
                    for c in range(DC):
                        mm = pe.matmul(bank[6 + half][:, :], src_t[:, j, c, :], w_ctx[:, c, half * 512:(half + 1) * 512],
                                       start=(c == 0), stop=(c == DC - 1))
                mm.then_inc(done, 1)

            def x1turn(b, j):
                n = TPB * b + j
                pe.wait_ge(x1_done, n + 1)
                pe.wait_ge(ot_done, 2 * TPB * (b + 1))
                pe.wait_ge(r1_done, TPB * b + 1)
                turn2(res[:, j, :], j, x1turn_done)

            def up(b, j):
                n = TPB * b + j
                pe.wait_ge(x1t_done, n + 1)
                if n == 0:
                    pe.wait_ge(in_wctx, 16)
                pe.wait_ge(r1_done, TPB * (b + 1))
                pe.wait_ge(ot_done, 2 * TPB * (b + 1))
                if CTX * n > 0:
                    pe.wait_ge(pick_step, CTX * n)
                ctx_product(turned, j, up_done)

            def aturn(b, j):
                n = TPB * b + j
                pe.wait_ge(a_done, n + 1)
                turn2(a_row[:, j, :], j, aturn_done)

            def down(b, j):
                n = TPB * b + j
                pe.wait_ge(at_done, n + 1)
                pe.wait_ge(pick_step, CTX * TPB * (b + 1))
                if CTX * n > 0:
                    pe.wait_ge(sel_step, CTX * n)
                ctx_product(turned, j, down_done)

            def x2turn(b, j):
                n = TPB * b + j
                pe.wait_ge(x2_done, n + 1)
                turn2(rows[:, n, :], j, x2turn_done)

            def gate(b, j):
                n = TPB * b + j
                pe.wait_ge(x2t_done, n + 1)
                if n == 0:
                    pe.wait_ge(in_wgate, 16)
                for c in range(DC):
                    mm = pe.matmul(bank[4 + j][:, D:D + EXPERTS], turned[:, j, c, :], w_gate[:, c, :],
                                   start=(c == 0), stop=(c == DC - 1))
                mm.then_inc(gate_done, 1)

            def rank(b, j):
                n = TPB * b + j
                pe.wait_ge(chosen_done, n + 1)
                if n > 0:
                    pe.wait_ge(seen_done, n)
                at = D + EXPERTS
                pe.matmul(bank[4 + j][:, at:at + EXPERTS], earlier[:, :], chosen[:, n, :], start=True, stop=False)
                pe.matmul(bank[4 + j][:, at:at + EXPERTS], ones[:, :], seen[:, n, :], start=False, stop=True)\
                    .then_inc(rank_done, 1)

            def gu_scale_sum(b, part):
                if part == 1:
                    pe.wait_ge(gu_norm_done, 1)
                    pe.wait_ge(place_done, TPB)
                    pe.matmul(bank[7][:, 0:1], ones[:, :], gu_sum[:, :], start=True, stop=True).then_inc(gu_scale_summed, 1)

            PART_PAIRS = ((0, 1), (1, 1), (0, 0))

            def s_turn(b, n):
                if n == 0:
                    pe.wait_ge(exp_done, 2 * HEADS * BATCH)
                    pe.wait_ge(plo_done, HEADS * BATCH)
                if n > 1:
                    pe.wait_ge(s_actt_done, n - 1)
                for c in range(DC):
                    mm = pe.transpose(bank[3][:, c * P:(c + 1) * P], rows[:, n, c * P:(c + 1) * P], ident[:, :])
                mm.then_inc(s_xturn_done, 1)

            def s_gate_up(b, n):
                if n == 0:
                    pe.wait_ge(gu_kept, SHARED)
                pe.wait_ge(s_xt_done, n + 1)
                pe.wait_ge(s_xt_low_done, n + 1)
                if n > 0:
                    pe.wait_ge(s_act_done, 2 * n)
                if n == TILES - 1:
                    pe.wait_ge(e_xt_low_done, SLOT_TILES)
                for s in range(SHARED):
                    for i, (c, (xp, wp)) in enumerate((c, pair) for c in range(DC) for pair in PART_PAIRS):
                        mm = pe.matmul(bank[s][:, 0:GU], s_xt[:, xp, c, :], w_gu_parts[:, c, EXPERTS + s, wp, :],
                                       start=(i == 0), stop=(i == DC * len(PART_PAIRS) - 1))
                    mm.then_inc(s_gu_done, 1)

            def s_act_turn(b, n):
                pe.wait_ge(s_act_done, 2 * n + 2)
                pe.wait_ge(s_xt_done, min(n + 2, TILES))
                pe.wait_ge(s_xt_low_done, min(n + 2, TILES))
                for k in range(2 * SHARED):
                    mm = pe.transpose(bank[3][0:HALF, k * P:(k + 1) * P],
                                      s_act[:, k // 2, (k % 2) * HALF:(k % 2 + 1) * HALF], ident[:, :])
                mm.then_inc(s_turn_done, 1)

            def s_down(b, n):
                if n == 0:
                    pe.wait_ge(in_wdown, 16)
                pe.wait_ge(s_actt_done, n + 1)
                if n > 0:
                    pe.wait_ge(s_sum_done, n)
                if n == TILES - 2:
                    pe.wait_ge(e_act_done, SLOT_TILES)
                for k in range(2 * SHARED):
                    mm = pe.matmul(bank[2][:, 0:D], s_act_t[:, k // 2, k % 2, :], w_down[:, EXPERTS + k // 2, k % 2, :],
                                   start=(k == 0), stop=(k == 2 * SHARED - 1))
                mm.then_inc(s_down_done, 1)

            def count_all(b, i):
                pe.wait_ge(seen_done, TILES)
                pe.wait_ge(place_done, TILES)
                pe.matmul(bank[7][:, 0:EXPERTS], ones[:, :], seen[:, TILES, :], start=True, stop=True)\
                    .then_inc(count_done, 1)

            def e_turn(b, s):
                pe.wait_ge(xs_in[s % XR], 16 * (s // XR + 1))
                if s < 2:
                    pe.wait_ge(s_act_done, SHARED * (TILES - 1))
                if s - 1 > 0:
                    pe.wait_ge(e_xt_low_done, s - 1)
                for c in range(DC):
                    mm = pe.transpose(bank[s % 2][:, c * P:(c + 1) * P], xs[:, s % XR, c * P:(c + 1) * P], ident[:, :])
                mm.then_inc(e_turn_done, 1)

            expert_of = {}

            def e_gate_up(b, s):
                if s == 0:
                    pe.wait_ge(plan_done, 2)
                    pe.wait_ge(gu_kept, EXPERTS + SHARED)
                if s < 2:
                    pe.wait_ge(s_sum_done, TILES - 2)
                    pe.wait_ge(s_actt_done, TILES - 1)
                expert_of[s] = pe.value_load(tile_expert[s:s + 1, 0:1], min_val=0, max_val=EXPERTS - 1)
                pe.wait_ge(e_xt_done, s + 1)
                pe.wait_ge(e_xt_low_done, s + 1)
                if s - 1 > 0:
                    pe.wait_ge(e_act_done, s - 1)
                for i, (c, (xp, wp)) in enumerate((c, pair) for c in range(DC) for pair in PART_PAIRS):
                    mm = pe.matmul(bank[2 + s % 2][:, 0:GU], e_xt[:, s % 2, xp, c, :],
                                   w_gu_parts[:, c, bass.ds(expert_of[s], 1), wp, :],
                                   start=(i == 0), stop=(i == DC * len(PART_PAIRS) - 1))
                mm.then_inc(e_gu_done, 1)

            def e_act_turn(b, s):
                pe.wait_ge(e_act_done, s + 1)
                if s - 1 > 0:
                    pe.wait_ge(e_actt_done, s - 1)
                for c in range(2):
                    mm = pe.transpose(bank[4 + s % 2][0:HALF, c * P:(c + 1) * P], e_act[:, s % 2, c * HALF:(c + 1) * HALF],
                                      ident[:, :])
                mm.then_inc(e_aturn_done, 1)

            def e_down(b, s):
                pe.wait_ge(e_actt_done, s + 1)
                if s - 1 > 0:
                    pe.wait_ge(e_y_done, s - 1)
                for c in range(2):
                    mm = pe.matmul(bank[6 + s % 2][:, 0:D], e_act_t[:, s % 2, c, :], w_down[:, bass.ds(expert_of[s], 1), c, :],
                                   start=(c == 0), stop=(c == 1))
                mm.then_inc(e_down_done, 1)

            def mix(b, n):
                pe.wait_ge(mix_weight_made, TOPK * (n + 1))
                pe.wait_ge(back_in[n], 16)
                if n < 2:
                    pe.wait_ge(e_actt_done, SLOT_TILES)
                else:
                    pe.wait_ge(mix_sum_done, n - 1)
                for k in range(TOPK):
                    mm = pe.matmul(bank[4 + n % 2][:, 0:D], mix_weight[:, n, k, :], back[:, n, k, :],
                                   start=(k == 0), stop=(k == TOPK - 1))
                mm.then_inc(mix_done, 1)

            run({"qkv": qkv, "fturn": latents_turn, "absorb_q": absorb_q, "absorb_o": absorb_o, "qproj": qproj, "qturn": qturn, "scores": scores,
                 "turn": turn, "values": values, "oturn": oturn, "oproj": oproj, "x1turn": x1turn, "up": up,
                 "aturn": aturn, "down": down, "x2turn": x2turn, "gate": gate, "rank": rank,
                 "s_turn": s_turn, "s_gate_up": s_gate_up, "s_act_turn": s_act_turn, "s_down": s_down,
                 "gu_scale": gu_scale_sum, "count": count_all, "e_turn": e_turn, "e_gate_up": e_gate_up, "e_act_turn": e_act_turn,
                 "e_down": e_down, "mix": mix})

        @block.vector
        def _(dve):
            def masks(b, i):
                dve.wait_ge(in_ids, 16)
                dve.tensor_copy(ids_f[:, :], ids_i[:, :]).then_inc(masks_step, 1)
                dve.wait_ge(masks_step, 1)
                for e in range(CTX):
                    if e == 0:
                        dve.tensor_scalar(picks[:, :, 0], ids_f[:, :], float(CTX_STEP), None, ALU.is_lt).then_inc(masks_step, 1)
                    elif e == CTX - 1:
                        dve.tensor_scalar(picks[:, :, e], ids_f[:, :], float(e * CTX_STEP), None, ALU.is_ge).then_inc(masks_step, 1)
                    else:
                        dve.wait_ge(masks_step, 2 * e)
                        dve.tensor_scalar(above[:, :], ids_f[:, :], float(e * CTX_STEP), None, ALU.is_ge).then_inc(masks_step, 1)
                        dve.wait_ge(masks_step, 2 * e + 1)
                        dve.scalar_tensor_tensor(out=picks[:, :, e], in0=ids_f[:, :], scalar=float((e + 1) * CTX_STEP),
                                                     in1=above[:, :], op0=ALU.is_lt, op1=ALU.mult).then_inc(masks_step, 1)

            def absorb_q(b, i):
                for half in range(2):
                    for c in range(2):
                        dve.wait_ge(absorbed_q, 2 * half + c + 1)
                        dve.tensor_tensor(w_q[:, c, 8 * half:8 * half + 8, 0:KR],
                                          bank[4 + 2 * half + c][0:QC, :].rearrange("p (h r) -> p h r", h=8),
                                          w_kn[0:QC, :].unsqueeze(1).broadcast_to([QC, 8, KR]),
                                          ALU.mult).then_inc(absorbed_q_kept, 1)

            def norm(b, j):
                n = TPB * b + j
                if n == 0:
                    dve.wait_ge(in_norms, 32)
                    dve.tensor_scalar(w_qn[:, :], w_qn[:, :], SCALE, None, ALU.mult).then_inc(norms_scaled, 1)
                    dve.wait_ge(norms_scaled, 1)
                    dve.wait_ge(in_rope, 32)
                q = bank[1 + j]
                dve.wait_ge(rms_done, b + 1)
                if n - 1 > 0:
                    dve.wait_ge(fturn_done, n - 1)
                if n - 1 > 0:
                    dve.wait_ge(vlo_done, n - 1)
                dve.scalar_tensor_tensor(out=qn[:, j, :], in0=q[:, 0:QR], scalar=rms[:, 2 * j:2 * j + 1],
                                             in1=w_qn[:, :], op0=ALU.mult, op1=ALU.mult).then_inc(qn_done, 1)
                dve.tensor_scalar(kv_row[:, j, 0:KR], q[:, QR:QR + KR], rms[:, 2 * j + 1:2 * j + 2], None,
                                  ALU.mult).then_inc(kvc_done, 1)
                pe_at, half = QR + KR, ROPE // 2
                if n - 1 > 0:
                    dve.wait_ge(kv_done, n - 1)
                dve.tensor_tensor(k_cos[:, j, :], q[:, pe_at:pe_at + ROPE], cos[:, j, :], ALU.mult).then_inc(krope_done, 1)
                for a, c in ((0, half), (half, 0)):
                    dve.tensor_tensor(k_sin[:, j, a:a + half], q[:, pe_at + c:pe_at + c + half],
                                          sin[:, j, a:a + half], ALU.mult).then_inc(krope_done, 1)
                dve.wait_ge(krope_done, 3 * (n + 1))
                dve.tensor_tensor(kv_row[:, j, KR:HD], k_cos[:, j, :], k_sin[:, j, :], ALU.add).then_inc(kv_done, 1)

            def q_rope(b, jg):
                j, g = jg
                i = GROUPS * (TPB * b + j) + g
                dve.wait_ge(qproj_done, i + 1)
                if i - 1 > 0:
                    dve.wait_ge(qrow_done, i - 1)
                half = ROPE // 2
                q = bank[g % 2][:, :].rearrange("p (h d) -> p h d", h=QG)

                def table(t, a, w):
                    return t[:, j, a:a + w].unsqueeze(1).broadcast_to([P, QG, w])

                dve.tensor_tensor(q_cos[:, i % 2], q[:, :, KR:HD], table(cos, 0, ROPE), ALU.mult)
                dve.tensor_tensor(q_sin[:, i % 2, :, 0:half], q[:, :, KR + half:HD], table(sin, 0, half), ALU.mult)
                dve.tensor_tensor(q_sin[:, i % 2, :, half:ROPE], q[:, :, KR:KR + half], table(sin, half, half),
                                      ALU.mult).then_inc(qrope_done, 1)

            def maxima(b, h):
                n = HEADS * b + h
                dve.wait_ge(scores_done, n + 1)
                if 2 * (n - 2) > 0:
                    dve.wait_ge(exp_done, 2 * (n - 2))
                for q, (at, w) in enumerate(((0, P), (P, 2 * P))):
                    dve.tensor_reduce(neg_max[:, n % 3, q:q + 1], bank[h % 3][:, at:at + w], AX, ALU.max,
                                          negate=True).then_inc(max_done, 1)

            def probs_lo(b, h):
                n = HEADS * b + h
                dve.wait_ge(phi_done, n + 1)
                if n - 2 > 0:
                    dve.wait_ge(pv_done, n - 2)
                dve.tensor_tensor(p_lo[:, n % 3, :], bank[3 + h % 2][:, 0:3 * P], p_hi[:, n % 3, :],
                                      ALU.subtract).then_inc(plo_done, 1)

            def head_out(b, h):
                if h % 2 == 0:
                    return
                n = HEADS * b + h
                pair = n // 2
                o = bank[5 + (h // 2) % 2][:, 0:4 * (KR + 1)].rearrange("p (h q r) -> p h q r", h=2, q=2)
                dve.wait_ge(pv_done, n + 1)
                if 2 * TPB * b > 0:
                    dve.wait_ge(oturn_done, 2 * TPB * b)
                if pair - 1 > 0:
                    dve.wait_ge(onorm_done, pair - 1)
                dve.reciprocal(inv_sum[:, pair % 2, :], o[:, :, :, KR]).then_inc(inv_done, 1)
                dve.wait_ge(inv_done, pair + 1)
                inv = inv_sum[:, pair % 2, :].rearrange("p (h q) -> p h q", h=2).unsqueeze(3).broadcast_to([P, 2, 2, KR])
                dst = o_row[:, :, (h - 1) * KR:(h + 1) * KR].rearrange("p q (h r) -> p h q r", h=2)
                dve.tensor_tensor(dst, o[:, :, :, 0:KR], inv, ALU.mult).then_inc(onorm_done, 1)

            stats_begun = [0]

            def stats_of(mom, j, n, src):
                stats_begun[0] += 1
                dve.bn_stats(stats[:, j, :], src).then_inc(stats_done, 1)
                dve.wait_ge(stats_done, stats_begun[0])
                dve.bn_aggr(moments[:, j, :], stats[:, j, :]).then_inc(mom, 1)

            def normed(inverse, j, n, dst, src, done):
                dve.wait_ge(inverse, n + 1)
                dve.tensor_scalar(dst, src, moments[:, j, 0:1], rstd[:, j, :], ALU.subtract, ALU.mult).then_inc(done, 1)

            def oproj(b, j):
                n = TPB * b + j
                dve.wait_ge(in_x, 16)
                dve.wait_ge(oproj_done, 2 * n + 2)
                dve.tensor_tensor(res[:, j, :], bank[5 + j][:, 0:D], rows[:, n, :], ALU.add).then_inc(r1_done, 1)
                dve.wait_ge(r1_done, n + 1)
                stats_of(r1_mom, j, n, res[:, j, :])

            def x1_norm(b, j):
                n = TPB * b + j
                if n - 1 > 0:
                    dve.wait_ge(x1turn_done, n - 1)
                normed(r1_rstd, j, n, res[:, j, :], res[:, j, :], x1_done)

            def expert_cols(e):
                return bank[6 + e // 2][:, (e % 2) * D:(e % 2 + 1) * D]

            def up(b, j):
                n = TPB * b + j
                if n == 0:
                    dve.wait_ge(masks_step, 7)
                dve.wait_ge(up_done, n + 1)
                if n - 1 > 0:
                    dve.wait_ge(silu_done, n - 1)
                if n - 1 > 0:
                    dve.wait_ge(a_done, n - 1)
                dve.tensor_scalar(picked[:, j, :], expert_cols(0), picks[:, n, 0:1], None, ALU.mult).then_inc(pick_step, 1)
                for e in range(1, CTX):
                    if CTX * n + e > 0:
                        dve.wait_ge(pick_step, CTX * n + e)
                    dve.scalar_tensor_tensor(out=picked[:, j, :], in0=expert_cols(e), scalar=picks[:, n, e:e + 1],
                                                 in1=picked[:, j, :], op0=ALU.mult, op1=ALU.add).then_inc(pick_step, 1)

            def act_product(b, j):
                n = TPB * b + j
                dve.wait_ge(silu_done, n + 1)
                dve.wait_ge(pick_step, CTX * (n + 1))
                if n - 1 > 0:
                    dve.wait_ge(aturn_done, n - 1)
                dve.tensor_tensor(a_row[:, j, :], gated[:, j, :], picked[:, j, :], ALU.mult).then_inc(a_done, 1)

            def down(b, j):
                n = TPB * b + j
                dve.wait_ge(down_done, n + 1)
                dve.wait_ge(x1_done, n + 1)
                for e in range(CTX):
                    if CTX * n + e > 0:
                        dve.wait_ge(sel_step, CTX * n + e)
                    dve.scalar_tensor_tensor(out=res[:, j, :], in0=expert_cols(e), scalar=picks[:, n, e:e + 1],
                                                 in1=res[:, j, :],
                                                 op0=ALU.mult, op1=ALU.add).then_inc(sel_step, 1)
                dve.wait_ge(sel_step, CTX * (n + 1))
                stats_of(r2_mom, j, n, res[:, j, :])

            def x2_norm(b, j):
                n = TPB * b + j
                normed(r2_rstd, j, n, rows[:, n, :], res[:, j, :], x2_done)

            def gate(b, j):
                n = TPB * b + j
                dve.wait_ge(gate_done, n + 1)
                dve.tensor_copy(logits[:, n, :], bank[4 + j][:, D:D + EXPERTS]).then_inc(route_step, 1)
                dve.wait_ge(route_step, 5 * n + 1)
                dve.max(top[:, n, :], logits[:, n, :]).then_inc(route_step, 1)
                dve.wait_ge(route_step, 5 * n + 2)
                dve.max_index(top_i[:, n, :], top[:, n, :], logits[:, n, :]).then_inc(route_step, 1)
                dve.wait_ge(route_step, 5 * n + 3)
                dve.tensor_copy(top_f[:, n, :], top_i[:, n, 0:TOPK]).then_inc(route_step, 1)
                dve.wait_ge(route_step, 5 * n + 4)
                dve.wait_ge(masks_made, MASKS)
                dve.tensor_tensor(onehot[:, j], iota16[:, :].unsqueeze(1).broadcast_to([P, TOPK, EXPERTS]),
                                  top_f[:, n, :].unsqueeze(2).broadcast_to([P, TOPK, EXPERTS]), ALU.is_equal)\
                    .then_inc(route_step, 1)
                dve.wait_ge(route_step, 5 * n + 5)
                with nc.allow_low_precision(reason="sums of at most 8 ones are exact"):
                    dve.tensor_reduce(chosen[:, n, :], onehot[:, j].rearrange("p k e -> p e k"), AX, ALU.add).then_inc(chosen_done, 1)
                    dve.wait_ge(chosen_done, n + 1)
                    dve.tensor_tensor(seen[:, n + 1, :], seen[:, n, :], chosen[:, n, :], ALU.add).then_inc(seen_done, 1)

            def rank(b, j):
                n = TPB * b + j
                dve.wait_ge(rank_done, n + 1)
                at = D + EXPERTS
                dve.tensor_tensor(place[:, n, :], bank[4 + j][:, at:at + EXPERTS], region[:, :], ALU.add).then_inc(place_done, 1)
                dve.wait_ge(place_done, n + 1)
                dve.tensor_tensor(placed[:, j], onehot[:, j],
                                      place[:, n, :].unsqueeze(1).broadcast_to([P, TOPK, EXPERTS]), ALU.mult).then_inc(place_step, 1)
                dve.wait_ge(place_step, 2 * n + 1)
                dve.tensor_reduce(slot_f[:, n, :], placed[:, j], AX, ALU.add).then_inc(place_step, 1)
                dve.wait_ge(place_step, 2 * n + 2)
                dve.tensor_copy(slot[:, n, :], slot_f[:, n, :]).then_inc(slot_done, 1)

            def gu_scale_of(b, part):
                if part == 0:
                    with nc.allow_low_precision(reason="only the scale's power of two is taken from it"):
                        dve.wait_ge(gu_squared, EXPERTS + SHARED)
                        dve.tensor_reduce(gu_sum[:, :], gu_squares[:, :], AX, ALU.add).then_inc(gu_norm_done, 1)
                elif part == 2:
                    dve.wait_ge(gu_scale_summed, 1)
                    dve.tensor_scalar(gu_norm[:, :], bank[7][:, 0:1], 1e-30, None, ALU.max).then_inc(gu_norm_done, 1)
                elif part == 3:
                    dve.wait_ge(gu_inverse_done, 1)
                    dve.tensor_scalar(gu_power[:, 0:1].bitcast(I32), gu_inverse[:, :].bitcast(I32), 0x7F800000, None,
                                      ALU.bitwise_and).then_inc(gu_scale_step, 1)
                    dve.wait_ge(gu_scale_step, 1)
                    dve.tensor_scalar(gu_power[:, 1:2].bitcast(I32), gu_power[:, 0:1].bitcast(I32), -1.0,
                                      float(254 << 23), ALU.mult, ALU.add).then_inc(gu_scale_step, 1)
                    dve.tensor_scalar(gu_scale[:, 0:1], gu_power[:, 0:1], float(2 ** 14), None, ALU.mult).then_inc(gu_scale_step, 1)
                    dve.wait_ge(gu_scale_step, 2)
                    dve.tensor_scalar(gu_scale[:, 1:2], gu_power[:, 1:2], float(2 ** -14), None, ALU.mult).then_inc(gu_scale_step, 1)

            def gu_low(b, i):
                e = (i + EXPERTS) % (EXPERTS + SHARED)
                dve.wait_ge(gu_high_done, i + 1)
                dve.scalar_tensor_tensor(out=w_gu_parts[:, :, e, 0, :], in0=w_gu[:, :, e, :], scalar=gu_scale[:, 0:1],
                                         in1=gu_temp[:, i % 2], op0=ALU.mult, op1=ALU.subtract).then_inc(gu_low_done, 1)
                dve.wait_ge(gu_low_done, i + 1)
                dve.tensor_copy(w_gu_parts[:, :, e, 1, :], gu_temp[:, i % 2]).then_inc(gu_kept, 1)

            def s_turn(b, n):
                dve.wait_ge(s_xt_done, n + 1)
                dve.tensor_tensor(s_xt[:, 1], bank[3][:, 0:D].rearrange("p (c t) -> p c t", c=DC), s_xt[:, 0],
                                  ALU.subtract).then_inc(s_xt_low_done, 1)

            def s_gate_up(b, n):
                for s in range(SHARED):
                    dve.wait_ge(s_silu_done, 2 * n + s + 1)
                    if n > 0:
                        dve.wait_ge(s_turn_done, n)
                    dve.scalar_tensor_tensor(out=s_act[:, s, :], in0=bank[s][:, INNER:GU], scalar=gu_scale[:, 1:2],
                                             in1=s_gate[:, s, :], op0=ALU.mult, op1=ALU.mult).then_inc(s_act_done, 1)

            def s_down(b, n):
                dve.wait_ge(s_down_done, n + 1)
                dve.wait_ge(x2_stored[n % 2], 16 * (n // 2 + 1))
                dve.tensor_tensor(rows[:, n, :], bank[2][:, 0:D], rows[:, n, :], ALU.add).then_inc(s_sum_done, 1)

            def plan(b, part):
                if part == 0:
                    dve.wait_ge(count_done, 1)
                    dve.tensor_copy(count[:, :], bank[7][:, 0:EXPERTS]).then_inc(plan_step, 1)
                    dve.wait_ge(plan_step, 1)
                    dve.tensor_tensor(full[:, :, :], count[:, :].unsqueeze(2).broadcast_to([P, EXPERTS, TILES]),
                                      tile_starts[:, :].unsqueeze(1).broadcast_to([P, EXPERTS, TILES]),
                                      ALU.is_gt).then_inc(plan_step, 1)
                    dve.wait_ge(plan_step, 2)
                    dve.tensor_reduce(tiles_of[:, :], full[:, :, :], AX, ALU.add).then_inc(plan_step, 1)
                    dve.wait_ge(plan_step, 3)
                    dve.tensor_tensor(prior[:, :, :], before[:, :, :],
                                      tiles_of[:, :].unsqueeze(1).broadcast_to([P, EXPERTS, EXPERTS]),
                                      ALU.mult).then_inc(plan_step, 1)
                    dve.tensor_scalar(step_up[:, 1:EXPERTS], tiles_of[:, 0:EXPERTS - 1], -1.0, float(TILES),
                                      ALU.mult, ALU.add).then_inc(plan_step, 1)
                    dve.wait_ge(plan_step, 5)
                    dve.tensor_reduce(base[:, :], prior[:, :, :], AX, ALU.add).then_inc(plan_step, 1)
                else:
                    dve.wait_ge(plan_step, 6)
                    dve.tensor_tensor(begun[:, :], slot_iota[:, :].broadcast_to([P, EXPERTS]), base[:, :],
                                      ALU.is_ge).then_inc(plan_step, 1)
                    dve.wait_ge(plan_step, 7)
                    dve.tensor_reduce(t_expert[:, :], begun[:, :], AX, ALU.add).then_inc(plan_step, 1)
                    dve.tensor_tensor(begun_step[:, :], begun[:, :], step_up[:, :], ALU.mult).then_inc(plan_step, 1)
                    dve.wait_ge(plan_step, 9)
                    dve.tensor_reduce(t_row[:, :], begun_step[:, :], AX, ALU.add).then_inc(plan_step, 1)
                    dve.wait_ge(plan_step, 10)
                    dve.tensor_tensor(tile_block[:, :], t_row[:, :], slot_iota[:, :], ALU.add).then_inc(plan_done, 1)
                    dve.tensor_scalar(tile_expert[:, :], t_expert[:, :], -1.0, None, ALU.add).then_inc(plan_done, 1)

            def weights(b, i):
                best = top[:, :, 0:1]
                dve.tensor_tensor(shifted[:, :, :], logits[:, :, :], best.broadcast_to([P, TILES, EXPERTS]),
                                      ALU.subtract).then_inc(soft_shift, 1)
                dve.tensor_tensor(soft_top[:, :, :], top[:, :, 0:TOPK], best.broadcast_to([P, TILES, TOPK]),
                                      ALU.subtract).then_inc(soft_shift, 1)
                dve.wait_ge(soft_exp, 2)
                dve.tensor_reduce(soft_sum[:, :], shifted[:, :, :], AX, ALU.add).then_inc(soft_step, 1)
                dve.wait_ge(soft_step, 1)
                dve.reciprocal(soft_inv[:, :], soft_sum[:, :]).then_inc(soft_step, 1)
                dve.wait_ge(soft_step, 2)
                dve.tensor_tensor(weight[:, :, :], soft_top[:, :, :],
                                      soft_inv[:, :].unsqueeze(2).broadcast_to([P, TILES, TOPK]), ALU.mult).then_inc(weight_done, 1)

            def e_turn(b, s):
                dve.wait_ge(e_xt_done, s + 1)
                dve.tensor_tensor(e_xt[:, s % 2, 1], bank[s % 2][:, 0:D].rearrange("p (c t) -> p c t", c=DC),
                                  e_xt[:, s % 2, 0], ALU.subtract).then_inc(e_xt_low_done, 1)

            def e_gate_up(b, s):
                dve.wait_ge(e_silu_done, s + 1)
                if s - 1 > 0:
                    dve.wait_ge(e_aturn_done, s - 1)
                dve.scalar_tensor_tensor(out=e_act[:, s % 2, :], in0=bank[2 + s % 2][:, INNER:GU], scalar=gu_scale[:, 1:2],
                                         in1=e_gate[:, s % 2, :], op0=ALU.mult, op1=ALU.mult).then_inc(e_act_done, 1)

            def e_act_turn(b, s):
                dve.wait_ge(e_aturn_done, s + 1)
                if s - 1 > 0:
                    dve.wait_ge(e_down_done, s - 1)
                dve.tensor_copy(e_act_t[:, s % 2],
                                    bank[4 + s % 2][0:HALF, 0:2 * P].rearrange("p (c t) -> p c t", c=2)).then_inc(e_actt_done, 1)

            def mix(b, n):
                dve.wait_ge(mix_done, n + 1)
                dve.wait_ge(s_sum_done, n + 1)
                dve.tensor_tensor(rows[:, n, :], bank[4 + n % 2][:, 0:D], rows[:, n, :], ALU.add).then_inc(mix_sum_done, 1)
                dve.wait_ge(mix_sum_done, n + 1)
                stats_of(r3_mom, n % 2, n, rows[:, n, :])

            def last_norm(b, n):
                if n >= 2:
                    dve.wait_ge(fin_stored[n % 2], 16 * (n // 2))
                normed(r3_rstd, n % 2, n, fin[:, n % 2, :], rows[:, n, :], fin_done)

            run({"keep_o": masks, "absorb_q": absorb_q, "norm": norm, "qproj": q_rope, "scores": maxima, "low": probs_lo, "out": head_out,
                 "oproj": oproj, "x1": x1_norm, "up": up, "act": act_product, "down": down, "x2": x2_norm,
                 "gate": gate, "rank": rank,
                 "gu_scale": gu_scale_of, "gu_low": gu_low, "s_turn": s_turn,
                 "s_gate_up": s_gate_up, "s_down": s_down, "plan": plan, "weights": weights,
                 "e_turn": e_turn, "e_gate_up": e_gate_up,
                 "e_act_turn": e_act_turn, "mix": mix, "fin": last_norm})


def kernel(**inputs):
    import numpy as np
    import concourse.bacc as bacc
    from concourse.bass_utils import run_bass_kernel_spmd

    a = {k: np.asarray(v) for k, v in inputs.items()}
    qb = a["L0_attn_q_b_w"].reshape(HEADS, QHD, QR)
    inv = np.float32(1.0) / np.float32(10000.0) ** (np.arange(0, ROPE, 2, dtype=np.float32) / np.float32(ROPE))
    freqs = np.outer(np.arange(SEQ, dtype=np.float32), inv.astype(np.float32)).astype(np.float32)
    cos = np.concatenate([np.cos(freqs), np.cos(freqs)], 1)
    sin = np.concatenate([-np.sin(freqs), np.sin(freqs)], 1)
    sg, su = a["L0_ffn_sg"], a["L0_ffn_su"]
    gate_up = np.concatenate([a["L0_ffn_wg"], a["L0_ffn_wu"]], 2)
    halves = [np.concatenate([sg[:, h * INNER:(h + 1) * INNER], su[:, h * INNER:(h + 1) * INNER]], 1)
              for h in range(SHARED)]
    laid = {
        "xT": a["x"].reshape(TOKENS, D).T,
        "x": a["x"].reshape(TOKENS, D),
        "ids": a["itok_BxS_13_99985"].reshape(TILES, P).T,
        "wqkvT": np.concatenate([a["L0_attn_q_a_w"], a["L0_attn_kv_a_w"]], 0).T,
        "qlnw": a["L0_attn_q_a_ln_w"],
        "kvlnw": a["L0_attn_kv_a_ln_w"],
        "qnope": qb[:, 0:NOPE, :],
        "qpeT": qb[:, NOPE:QHD, :].transpose(2, 0, 1),
        "kvb": a["L0_attn_kv_b_w"],
        "woT": a["L0_attn_o_w"].T,
        "cosT": cos,
        "sinT": sin,
        "ctxT": a["ctx_2048"].transpose(2, 0, 1).reshape(D, CTX * D),
        "wgateT": a["L0_ffn_w_gate"].T,
        "wgu": np.concatenate([gate_up, np.stack(halves)], 0).transpose(1, 0, 2),
        "wd": np.concatenate([a["L0_ffn_wd"], a["L0_ffn_sd"].reshape(SHARED, INNER, D)], 0),
    }
    nc = bacc.Bacc("TRN2", target_bir_lowering=False, num_devices=1)
    arrays, aps = {}, {}
    for name, v in laid.items():
        v = np.ascontiguousarray(v)
        arrays[f"in_{name}"] = v
        aps[name] = nc.dram_tensor(f"in_{name}", v.shape, mybir.dt.from_np(v.dtype), kind="ExternalInput").ap()
    aps["out"] = nc.dram_tensor("out_0", (TOKENS, D), F32, kind="ExternalOutput").ap()
    decoder_layer(nc, **aps)
    r = run_bass_kernel_spmd(nc, [arrays], core_ids=[0])
    return r.results[0]["out_0"].reshape(BATCH, SEQ, D)
```
